# Optimizing a Trainium2 kernel written in Bass

```python
import numpy as np
import jax
import jax.numpy as jnp

def _softmax(x, axis=-1):
    return jax.nn.softmax(x, axis=axis)

def _gelu(x):
    return jax.nn.gelu(x, approximate=True)

def _silu(x):
    return jax.nn.silu(x)

def _sigmoid(x):
    return jax.nn.sigmoid(x)

def _layernorm(x, axis=-1, eps=1e-05):
    m = jnp.mean(x, axis=axis, keepdims=True)
    v = jnp.var(x, axis=axis, keepdims=True)
    return (x - m) / jnp.sqrt(v + eps)

def _scatter_add(tgt, idx, src, axis=0):
    return tgt.at[idx].add(src)

def _segment_sum(src, seg, n):
    return jax.ops.segment_sum(src, seg, n)
kernel_name = 'mk_gnn_ffn_d4_gnn_r32_f22b5f'

def setup_inputs(seed: int=0):
    np.random.seed(seed)
    _w = jnp.asarray

    def _rec_inputs():
        import jax
        import jax.numpy as jnp
        _gk = jax.random.key(seed)
        x = -0.0002117 + 1 * jax.random.normal(jax.random.fold_in(_gk, 1), (3125, 256), jnp.float32)
        src = jax.random.randint(jax.random.fold_in(_gk, 2), (50000,), 0, 3125, jnp.int32)
        dst = jnp.minimum((3125 * jax.random.uniform(jax.random.fold_in(_gk, 3), (50000,)) ** 2.0).astype(jnp.int32), 99999)
        _o = jnp.argsort(dst, stable=True)
        src = src[_o]
        dst = dst[_o]
        edge_attr_5 = jax.random.uniform(jax.random.fold_in(_gk, 12), (50000, 5), jnp.float32, 0.0, 99.9996)
        edge_weight = jax.random.uniform(jax.random.fold_in(_gk, 14), (50000,), jnp.float32, 0.0, 1)
        node_type_19 = jax.random.randint(jax.random.fold_in(_gk, 15), (3125,), 0, 19, jnp.int32)
        return (x, src, dst, edge_attr_5, edge_weight, node_type_19)
    x, src, dst, edge_attr_5, edge_weight, node_type_19 = _rec_inputs()

    def _L0_gnn_setup():
        import jax, jax.numpy as jnp
        import numpy as np
        N = 3125
        E = 100000
        D = 256
        H = 8
        DH = D // H
        COEF = 1.0 / DH ** 0.5
        key = jax.random.key(seed)
        ks = jax.random.split(key, 7)
        x = jax.random.normal(ks[0], (N, D), dtype=jnp.float32)
        W_qkv = jax.random.normal(ks[1], (D, 3 * D), dtype=jnp.float32) * D ** (-0.5)
        b_qkv = jax.random.normal(ks[2], (3 * D,), dtype=jnp.float32) * 0.01
        W_out = jax.random.normal(ks[3], (2 * D, D), dtype=jnp.float32) * (2 * D) ** (-0.5)
        b_out = jax.random.normal(ks[4], (D,), dtype=jnp.float32) * 0.01
        src = jax.random.randint(ks[5], (E,), 0, N, dtype=jnp.int64)
        dst = jax.random.randint(ks[6], (E,), 0, N, dtype=jnp.int64)
        return {'x': x, 'W_qkv': W_qkv, 'b_qkv': b_qkv, 'W_out': W_out, 'b_out': b_out, 'src': src, 'dst': dst}
    _L0_gnn_all = _L0_gnn_setup()
    _L0_gnn_in = {k: v for k, v in _L0_gnn_all.items() if k in ('W_qkv', 'b_qkv', 'W_out', 'b_out')}
    del _L0_gnn_all

    def _L0_ffn_setup():
        import jax, jax.numpy as jnp
        import numpy as np
        BN_EPS = 0.001

        def _bn(h, g, b, m, v):
            return g * (h - m) * jax.lax.rsqrt(v + BN_EPS) + b
        key = jax.random.key(seed)
        ks = jax.random.split(key, 8)
        B, F, Df = (256, 64, 256)
        E, H, D = (8, 256, 256)
        s1 = 1.0 / np.sqrt(Df)
        s2 = 1.0 / np.sqrt(H)
        return {'x': jax.random.normal(ks[0], (B, F, Df), jnp.float32), 'Wr': jax.random.normal(ks[1], (Df, E), jnp.float32) * s1, 'br': jnp.zeros((E,), jnp.float32), 'W1': jax.random.normal(ks[2], (E, Df, H), jnp.float32) * s1, 'b1': jnp.zeros((E, H), jnp.float32), 'g1': jnp.ones((E, H), jnp.float32), 'be1': jnp.zeros((E, H), jnp.float32), 'm1': jnp.zeros((E, H), jnp.float32), 'v1': jnp.ones((E, H), jnp.float32), 'W2': jax.random.normal(ks[3], (E, H, H), jnp.float32) * s2, 'b2': jnp.zeros((E, H), jnp.float32), 'g2': jnp.ones((E, H), jnp.float32), 'be2': jnp.zeros((E, H), jnp.float32), 'm2': jnp.zeros((E, H), jnp.float32), 'v2': jnp.ones((E, H), jnp.float32), 'Wo': jax.random.normal(ks[4], (E, H, D), jnp.float32) * s2, 'bo': jnp.zeros((E, D), jnp.float32)}
    _L0_ffn_all = _L0_ffn_setup()
    _L0_ffn_in = {k: v for k, v in _L0_ffn_all.items() if k in ('Wr', 'br', 'W1', 'b1', 'g1', 'be1', 'm1', 'v1', 'W2', 'b2', 'g2', 'be2', 'm2', 'v2', 'Wo', 'bo')}
    del _L0_ffn_all

    def _L1_gnn_setup():
        import jax, jax.numpy as jnp
        import numpy as np
        N = 50000
        E = 25000
        IN, HID, OUT = (256, 512, 256)
        key = jax.random.key(seed)
        ks = jax.random.split(key, 8)
        x = jax.random.normal(ks[0], (N, IN), dtype=jnp.float32)
        edge_index = jax.random.randint(ks[1], (2, E), 0, N, dtype=jnp.int64)

        def lin(k, fan_out, fan_in):
            s = 1.0 / np.sqrt(fan_in)
            return jax.random.uniform(k, (fan_out, fan_in), jnp.float32, -s, s)
        return {'x': x, 'edge_index': edge_index, 'W1l': lin(ks[2], HID, IN), 'b1': jnp.zeros((HID,), jnp.float32), 'W1r': lin(ks[3], HID, IN), 'W2l': lin(ks[4], OUT, HID), 'b2': jnp.zeros((OUT,), jnp.float32), 'W2r': lin(ks[5], OUT, HID)}
    _L1_gnn_all = _L1_gnn_setup()
    _L1_gnn_in = {k: v for k, v in _L1_gnn_all.items() if k in ('W1l', 'b1', 'W1r', 'W2l', 'b2', 'W2r')}
    del _L1_gnn_all

    def _L1_ffn_setup():
        import jax, jax.numpy as jnp
        import numpy as np
        B, S, D = (8, 128, 256)
        H = 4 * D
        CAPACITY = 0.5
        key = jax.random.key(seed)
        ks = jax.random.split(key, 6)
        x = jax.random.normal(ks[0], (B, S, D), dtype=jnp.float32)
        attention_mask = jnp.zeros((B, 1, 1, S), dtype=jnp.float32)
        wr = jax.random.normal(ks[1], (D, 1), dtype=jnp.float32) * 0.02
        br = jnp.zeros((1,), dtype=jnp.float32)
        w1 = jax.random.normal(ks[2], (D, H), dtype=jnp.float32) * 0.02
        b1 = jnp.zeros((H,), dtype=jnp.float32)
        w2 = jax.random.normal(ks[3], (H, D), dtype=jnp.float32) * 0.02
        b2 = jnp.zeros((D,), dtype=jnp.float32)
        return {'x': x, 'attention_mask': attention_mask, 'wr': wr, 'br': br, 'w1': w1, 'b1': b1, 'w2': w2, 'b2': b2}
    _L1_ffn_all = _L1_ffn_setup()
    _L1_ffn_in = {k: v for k, v in _L1_ffn_all.items() if k in ('attention_mask', 'wr', 'br', 'w1', 'b1', 'w2', 'b2')}
    del _L1_ffn_all

    def _L2_gnn_setup():
        import jax, jax.numpy as jnp
        import numpy as np
        N = 1024
        E = 4096
        IN = 256
        OUT = 256
        TD = 32
        H = 4
        T = 19
        PROJ = OUT - 2 * TD
        DK = (OUT - TD) // H
        SQRT_DK = float(np.sqrt(DK))
        LN_EPS = 1e-05

        def time_emb(t, w, b):
            return jnp.cos(jnp.log(t + 1.0)[:, None] * w[None, :] + b[None, :])

        def typed_linear(x, W, b, node_type):
            out = jnp.zeros((x.shape[0], W.shape[2]), x.dtype)
            for t in range(W.shape[0]):
                out = jnp.where((node_type == t)[:, None], x @ W[t] + b[t], out)
            return out

        def seg_softmax(att, idx, n):
            m = jax.ops.segment_max(att, idx, num_segments=n)
            e = jnp.exp(att - m[idx])
            s = jax.ops.segment_sum(e, idx, num_segments=n)
            return e / (s[idx] + 1e-16)
        key = jax.random.key(seed)
        ks = jax.random.split(key, 8)
        x = jax.random.normal(ks[0], (N, IN), jnp.float32)
        node_type = jax.random.randint(ks[1], (N,), 0, T, jnp.int32)
        edge_index = jax.random.randint(ks[2], (2, E), 0, N, jnp.int32)
        times = jax.random.uniform(ks[3], (E, 3), jnp.float32, 0.0, 100.0)
        edge_attr = jnp.concatenate([times, node_type[edge_index[0]][:, None].astype(jnp.float32), node_type[edge_index[1]][:, None].astype(jnp.float32)], axis=1)
        s = 0.02
        Wk = jax.random.normal(ks[4], (T, IN, PROJ), jnp.float32) * s
        Wq = jax.random.normal(ks[5], (T, IN, PROJ), jnp.float32) * s
        Wv = jax.random.normal(ks[6], (T, IN, PROJ), jnp.float32) * s
        bk = jnp.zeros((T, PROJ), jnp.float32)
        bq = jnp.zeros((T, PROJ), jnp.float32)
        bv = jnp.zeros((T, PROJ), jnp.float32)
        Wa = jax.random.normal(ks[7], (T, 2 * OUT, IN), jnp.float32) * s
        ba = jnp.zeros((T, IN), jnp.float32)
        gamma = jnp.ones((T, IN), jnp.float32)
        beta = jnp.zeros((T, IN), jnp.float32)
        w_time = jnp.asarray(1.0 / 10 ** np.linspace(0, 1.5, TD), jnp.float32)
        b_time = jnp.zeros((TD,), jnp.float32)
        return dict(x=x, node_type=node_type, edge_index=edge_index, edge_attr=edge_attr, Wk=Wk, bk=bk, Wq=Wq, bq=bq, Wv=Wv, bv=bv, Wa=Wa, ba=ba, gamma=gamma, beta=beta, w_time=w_time, b_time=b_time)
    _L2_gnn_all = _L2_gnn_setup()
    _L2_gnn_in = {k: v for k, v in _L2_gnn_all.items() if k in ('Wk', 'bk', 'Wq', 'bq', 'Wv', 'bv', 'Wa', 'ba', 'gamma', 'beta', 'w_time', 'b_time')}
    del _L2_gnn_all

    def _L2_ffn_setup():
        import jax, jax.numpy as jnp
        import numpy as np
        B, A = (128, 8)
        IN, OUT = (256, 256)
        SH1, SH2 = (256, 128)
        EH1, EH2 = (128, 64)
        E, TOPK = (4, 2)

        def _shared_mlp(x, W1, b1, W2, b2, W3, b3):
            h = jax.nn.relu(x @ W1 + b1)
            h = jax.nn.relu(h @ W2 + b2)
            return h @ W3 + b3

        def _experts_mlp(x, eW1, eb1, eW2, eb2, eW3, eb3):
            h = jax.nn.relu(jnp.einsum('baf,efh->ebah', x, eW1) + eb1[:, None, None, :])
            h = jax.nn.relu(jnp.einsum('ebah,ehg->ebag', h, eW2) + eb2[:, None, None, :])
            o = jnp.einsum('ebag,ego->ebao', h, eW3) + eb3[:, None, None, :]
            return jnp.moveaxis(o, 0, -1)
        key = jax.random.key(seed)
        ks = jax.random.split(key, 16)
        s = 0.05
        return {'x': jax.random.normal(ks[0], (B, A, IN), jnp.float32), 'sW1': jax.random.normal(ks[1], (IN, SH1), jnp.float32) * s, 'sb1': jnp.zeros((SH1,), jnp.float32), 'sW2': jax.random.normal(ks[2], (SH1, SH2), jnp.float32) * s, 'sb2': jnp.zeros((SH2,), jnp.float32), 'sW3': jax.random.normal(ks[3], (SH2, OUT), jnp.float32) * s, 'sb3': jnp.zeros((OUT,), jnp.float32), 'eW1': jax.random.normal(ks[4], (E, IN, EH1), jnp.float32) * s, 'eb1': jnp.zeros((E, EH1), jnp.float32), 'eW2': jax.random.normal(ks[5], (E, EH1, EH2), jnp.float32) * s, 'eb2': jnp.zeros((E, EH2), jnp.float32), 'eW3': jax.random.normal(ks[6], (E, EH2, OUT), jnp.float32) * s, 'eb3': jnp.zeros((E, OUT), jnp.float32), 'gW': jax.random.normal(ks[7], (IN, E), jnp.float32) * s, 'gb': jnp.zeros((E,), jnp.float32)}
    _L2_ffn_all = _L2_ffn_setup()
    _L2_ffn_in = {k: v for k, v in _L2_ffn_all.items() if k in ('sW1', 'sb1', 'sW2', 'sb2', 'sW3', 'sb3', 'eW1', 'eb1', 'eW2', 'eb2', 'eW3', 'eb3', 'gW', 'gb')}
    del _L2_ffn_all

    def _L3_gnn_setup():
        import jax, jax.numpy as jnp
        import numpy as np
        N_NODES = 3125
        N_EDGES = 100000
        D_IN = 256
        D_OUT = 256
        key = jax.random.key(seed)
        k1, k2, k3, k4, k5 = jax.random.split(key, 5)
        x = jax.random.normal(k1, (N_NODES, D_IN), dtype=jnp.float32)
        limit = float(np.sqrt(6.0 / (D_IN + D_OUT)))
        weight = jax.random.uniform(k2, (D_IN, D_OUT), dtype=jnp.float32, minval=-limit, maxval=limit)
        edge_val = jax.random.uniform(k3, (N_EDGES,), dtype=jnp.float32)
        edge_row = jax.random.randint(k4, (N_EDGES,), 0, N_NODES, dtype=jnp.int32)
        edge_col = jax.random.randint(k5, (N_EDGES,), 0, N_NODES, dtype=jnp.int32)
        return {'x': x, 'weight': weight, 'edge_val': edge_val, 'edge_row': edge_row, 'edge_col': edge_col}
    _L3_gnn_all = _L3_gnn_setup()
    _L3_gnn_in = {k: v for k, v in _L3_gnn_all.items() if k in ('weight',)}
    del _L3_gnn_all

    def _L3_ffn_setup():
        import jax, jax.numpy as jnp
        import numpy as np
        IN_CH = 256
        OUT_CH = 256
        key = jax.random.key(seed)
        kx, kw, kb = jax.random.split(key, 3)
        x = jax.random.normal(kx, (8, 128, IN_CH), dtype=jnp.float32)
        bound = 1.0 / np.sqrt(IN_CH)
        weight = jax.random.uniform(kw, (OUT_CH, IN_CH), dtype=jnp.float32, minval=-bound, maxval=bound)
        bias = jax.random.uniform(kb, (OUT_CH,), dtype=jnp.float32, minval=-bound, maxval=bound)
        return {'x': x, 'weight': weight, 'bias': bias}
    _L3_ffn_all = _L3_ffn_setup()
    _L3_ffn_in = {k: v for k, v in _L3_ffn_all.items() if k in ('weight', 'bias')}
    del _L3_ffn_all
    return {'x': x, 'src': src, 'dst': dst, 'edge_attr_5': edge_attr_5, 'edge_weight': edge_weight, 'node_type_19': node_type_19, 'L0_gnn_W_qkv': _L0_gnn_in['W_qkv'], 'L0_gnn_b_qkv': _L0_gnn_in['b_qkv'], 'L0_gnn_W_out': _L0_gnn_in['W_out'], 'L0_gnn_b_out': _L0_gnn_in['b_out'], 'L0_ffn_Wr': _L0_ffn_in['Wr'], 'L0_ffn_br': _L0_ffn_in['br'], 'L0_ffn_W1': _L0_ffn_in['W1'], 'L0_ffn_b1': _L0_ffn_in['b1'], 'L0_ffn_g1': _L0_ffn_in['g1'], 'L0_ffn_be1': _L0_ffn_in['be1'], 'L0_ffn_m1': _L0_ffn_in['m1'], 'L0_ffn_v1': _L0_ffn_in['v1'], 'L0_ffn_W2': _L0_ffn_in['W2'], 'L0_ffn_b2': _L0_ffn_in['b2'], 'L0_ffn_g2': _L0_ffn_in['g2'], 'L0_ffn_be2': _L0_ffn_in['be2'], 'L0_ffn_m2': _L0_ffn_in['m2'], 'L0_ffn_v2': _L0_ffn_in['v2'], 'L0_ffn_Wo': _L0_ffn_in['Wo'], 'L0_ffn_bo': _L0_ffn_in['bo'], 'L1_gnn_W1l': _L1_gnn_in['W1l'], 'L1_gnn_b1': _L1_gnn_in['b1'], 'L1_gnn_W1r': _L1_gnn_in['W1r'], 'L1_gnn_W2l': _L1_gnn_in['W2l'], 'L1_gnn_b2': _L1_gnn_in['b2'], 'L1_gnn_W2r': _L1_gnn_in['W2r'], 'L1_ffn_attention_mask': _L1_ffn_in['attention_mask'], 'L1_ffn_wr': _L1_ffn_in['wr'], 'L1_ffn_br': _L1_ffn_in['br'], 'L1_ffn_w1': _L1_ffn_in['w1'], 'L1_ffn_b1': _L1_ffn_in['b1'], 'L1_ffn_w2': _L1_ffn_in['w2'], 'L1_ffn_b2': _L1_ffn_in['b2'], 'L2_gnn_Wk': _L2_gnn_in['Wk'], 'L2_gnn_bk': _L2_gnn_in['bk'], 'L2_gnn_Wq': _L2_gnn_in['Wq'], 'L2_gnn_bq': _L2_gnn_in['bq'], 'L2_gnn_Wv': _L2_gnn_in['Wv'], 'L2_gnn_bv': _L2_gnn_in['bv'], 'L2_gnn_Wa': _L2_gnn_in['Wa'], 'L2_gnn_ba': _L2_gnn_in['ba'], 'L2_gnn_gamma': _L2_gnn_in['gamma'], 'L2_gnn_beta': _L2_gnn_in['beta'], 'L2_gnn_w_time': _L2_gnn_in['w_time'], 'L2_gnn_b_time': _L2_gnn_in['b_time'], 'L2_ffn_sW1': _L2_ffn_in['sW1'], 'L2_ffn_sb1': _L2_ffn_in['sb1'], 'L2_ffn_sW2': _L2_ffn_in['sW2'], 'L2_ffn_sb2': _L2_ffn_in['sb2'], 'L2_ffn_sW3': _L2_ffn_in['sW3'], 'L2_ffn_sb3': _L2_ffn_in['sb3'], 'L2_ffn_eW1': _L2_ffn_in['eW1'], 'L2_ffn_eb1': _L2_ffn_in['eb1'], 'L2_ffn_eW2': _L2_ffn_in['eW2'], 'L2_ffn_eb2': _L2_ffn_in['eb2'], 'L2_ffn_eW3': _L2_ffn_in['eW3'], 'L2_ffn_eb3': _L2_ffn_in['eb3'], 'L2_ffn_gW': _L2_ffn_in['gW'], 'L2_ffn_gb': _L2_ffn_in['gb'], 'L3_gnn_weight': _L3_gnn_in['weight'], 'L3_ffn_weight': _L3_ffn_in['weight'], 'L3_ffn_bias': _L3_ffn_in['bias']}

def reference(x, src, dst, edge_attr_5, edge_weight, node_type_19, L0_gnn_W_qkv, L0_gnn_b_qkv, L0_gnn_W_out, L0_gnn_b_out, L0_ffn_Wr, L0_ffn_br, L0_ffn_W1, L0_ffn_b1, L0_ffn_g1, L0_ffn_be1, L0_ffn_m1, L0_ffn_v1, L0_ffn_W2, L0_ffn_b2, L0_ffn_g2, L0_ffn_be2, L0_ffn_m2, L0_ffn_v2, L0_ffn_Wo, L0_ffn_bo, L1_gnn_W1l, L1_gnn_b1, L1_gnn_W1r, L1_gnn_W2l, L1_gnn_b2, L1_gnn_W2r, L1_ffn_attention_mask, L1_ffn_wr, L1_ffn_br, L1_ffn_w1, L1_ffn_b1, L1_ffn_w2, L1_ffn_b2, L2_gnn_Wk, L2_gnn_bk, L2_gnn_Wq, L2_gnn_bq, L2_gnn_Wv, L2_gnn_bv, L2_gnn_Wa, L2_gnn_ba, L2_gnn_gamma, L2_gnn_beta, L2_gnn_w_time, L2_gnn_b_time, L2_ffn_sW1, L2_ffn_sb1, L2_ffn_sW2, L2_ffn_sb2, L2_ffn_sW3, L2_ffn_sb3, L2_ffn_eW1, L2_ffn_eb1, L2_ffn_eW2, L2_ffn_eb2, L2_ffn_eW3, L2_ffn_eb3, L2_ffn_gW, L2_ffn_gb, L3_gnn_weight, L3_ffn_weight, L3_ffn_bias):
    import jax
    import jax.numpy as jnp

    def _L0_gnn_ref(x, W_qkv, b_qkv, W_out, b_out, src, dst):
        import jax, jax.numpy as jnp
        import numpy as np
        N = 3125
        E = 100000
        D = 256
        H = 8
        DH = D // H
        COEF = 1.0 / DH ** 0.5
        qkv = (x @ W_qkv + b_qkv).reshape(N, H, 3 * DH)
        q, k, v = (qkv[..., :DH], qkv[..., DH:2 * DH], qkv[..., 2 * DH:])
        scores = jnp.einsum('eh d, eh d -> eh'.replace(' ', ''), k[src], q[dst]) * COEF
        smax = jax.ops.segment_max(scores, dst, num_segments=N)
        smax = jnp.where(jnp.isfinite(smax), smax, 0.0)
        ex = jnp.exp(scores - smax[dst])
        denom = jax.ops.segment_sum(ex, dst, num_segments=N)
        probs = ex / jnp.maximum(denom[dst], 1e-20)
        message = jax.ops.segment_sum(v[src] * probs[:, :, None], dst, num_segments=N)
        message = message.reshape(N, D)
        out = jnp.concatenate([x, message], axis=1) @ W_out + b_out
        return out

    def _L0_ffn_ref(x, Wr, br, W1, b1, g1, be1, m1, v1, W2, b2, g2, be2, m2, v2, Wo, bo):
        import jax, jax.numpy as jnp
        import numpy as np
        BN_EPS = 0.001

        def _bn(h, g, b, m, v):
            return g * (h - m) * jax.lax.rsqrt(v + BN_EPS) + b
        feat = jnp.mean(x, axis=0)
        w = jax.nn.softmax(feat @ Wr + br, axis=-1)
        h = jnp.einsum('bfd,edh->bfeh', x, W1) + b1
        h = jax.nn.relu(_bn(h, g1, be1, m1, v1))
        h = jnp.einsum('bfeh,ehk->bfek', h, W2) + b2
        h = jax.nn.relu(_bn(h, g2, be2, m2, v2))
        y = jnp.einsum('bfeh,ehd->bfed', h, Wo) + bo
        return jnp.einsum('bfed,fe->bfd', y, w)

    def _L1_gnn_ref(x, edge_index, W1l, b1, W1r, W2l, b2, W2r):
        import jax, jax.numpy as jnp
        import numpy as np
        N = 50000
        E = 25000
        IN, HID, OUT = (256, 512, 256)
        src, dst = (edge_index[0], edge_index[1])
        n = x.shape[0]
        deg = jax.ops.segment_sum(jnp.ones((src.shape[0],), x.dtype), dst, num_segments=n)
        inv_deg = 1.0 / jnp.maximum(deg, 1.0)

        def sage(h, Wl, b, Wr):
            agg = jax.ops.segment_sum(h[src], dst, num_segments=n) * inv_deg[:, None]
            return agg @ Wl.T + b + h @ Wr.T
        h = jax.nn.relu(sage(x, W1l, b1, W1r))
        z = sage(h, W2l, b2, W2r)
        return z

    def _L1_ffn_ref(x, attention_mask, wr, br, w1, b1, w2, b2):
        import jax, jax.numpy as jnp
        import numpy as np
        B, S, D = (8, 128, 256)
        H = 4 * D
        CAPACITY = 0.5
        b, s, d = x.shape
        weights = (jnp.einsum('bsd,do->bso', x, wr) + br)[..., 0]
        k = max(1, int(CAPACITY * s))
        kk = k - 1 if k > 1 else 1
        _, idx = jax.lax.top_k(weights, k)
        sel_idx = idx[:, :kk]
        sel = jnp.take_along_axis(x, sel_idx[:, :, None], axis=1)
        h = jax.nn.gelu(jnp.einsum('bkd,dh->bkh', sel, w1) + b1)
        y = jnp.einsum('bkh,hd->bkd', h, w2) + b2
        w_sel = jnp.take_along_axis(weights, sel_idx, axis=1)
        y = y * w_sel[..., None]
        batch_idx = jnp.arange(b)[:, None]
        processed = jnp.zeros_like(x).at[batch_idx, sel_idx].set(y)
        return processed + x

    def _L2_gnn_ref(x, node_type, edge_index, edge_attr, Wk, bk, Wq, bq, Wv, bv, Wa, ba, gamma, beta, w_time, b_time):
        import jax, jax.numpy as jnp
        import numpy as np
        N = 1024
        E = 4096
        IN = 256
        OUT = 256
        TD = 32
        H = 4
        T = 19
        PROJ = OUT - 2 * TD
        DK = (OUT - TD) // H
        SQRT_DK = float(np.sqrt(DK))
        LN_EPS = 1e-05

        def time_emb(t, w, b):
            return jnp.cos(jnp.log(t + 1.0)[:, None] * w[None, :] + b[None, :])

        def typed_linear(x, W, b, node_type):
            out = jnp.zeros((x.shape[0], W.shape[2]), x.dtype)
            for t in range(W.shape[0]):
                out = jnp.where((node_type == t)[:, None], x @ W[t] + b[t], out)
            return out

        def seg_softmax(att, idx, n):
            m = jax.ops.segment_max(att, idx, num_segments=n)
            e = jnp.exp(att - m[idx])
            s = jax.ops.segment_sum(e, idx, num_segments=n)
            return e / (s[idx] + 1e-16)
        row, col = (edge_index[0], edge_index[1])
        n = x.shape[0]
        K = typed_linear(x, Wk, bk, node_type)
        Q = typed_linear(x, Wq, bq, node_type)
        V = typed_linear(x, Wv, bv, node_type)
        e0 = time_emb(edge_attr[:, 0], w_time, b_time)
        e1 = time_emb(edge_attr[:, 1], w_time, b_time)
        e2 = time_emb(edge_attr[:, 2], w_time, b_time)

        def edge_msgs(Kn, Qn, Vn, ek, eq):
            k = jnp.concatenate([Kn, ek], axis=1).reshape(-1, H, DK)
            q = jnp.concatenate([Qn, eq], axis=1).reshape(-1, H, DK)
            att = jnp.einsum('ehd,ed->eh', k, q.sum(axis=1)) / SQRT_DK
            v = jnp.concatenate([Vn, ek], axis=1).reshape(-1, H, DK)
            return (att, v)
        att, v = edge_msgs(K[row], Q[col], V[row], e1, e2)
        att_i, v_i = edge_msgs(K[col], Q[row], V[col], e2, e1)
        att = seg_softmax(att, col, n)
        att_i = seg_softmax(att_i, row, n)
        res = (v * att[:, :, None]).reshape(-1, H * DK)
        res = jnp.concatenate([res, e0], axis=1)
        res_i = (v_i * att_i[:, :, None]).reshape(-1, H * DK)
        res_i = jnp.concatenate([res_i, e0], axis=1)
        agg = jax.ops.segment_sum(res, col, num_segments=n) + jax.ops.segment_sum(res_i, row, num_segments=n)
        h = jnp.concatenate([agg, agg], axis=1)
        o = typed_linear(h, Wa, ba, node_type)
        y = o + x
        mu = y.mean(axis=-1, keepdims=True)
        var = y.var(axis=-1, keepdims=True)
        yn = (y - mu) / jnp.sqrt(var + LN_EPS)
        return yn * gamma[node_type] + beta[node_type]

    def _L2_ffn_ref(x, sW1, sb1, sW2, sb2, sW3, sb3, eW1, eb1, eW2, eb2, eW3, eb3, gW, gb):
        import jax, jax.numpy as jnp
        import numpy as np
        B, A = (128, 8)
        IN, OUT = (256, 256)
        SH1, SH2 = (256, 128)
        EH1, EH2 = (128, 64)
        E, TOPK = (4, 2)

        def _shared_mlp(x, W1, b1, W2, b2, W3, b3):
            h = jax.nn.relu(x @ W1 + b1)
            h = jax.nn.relu(h @ W2 + b2)
            return h @ W3 + b3

        def _experts_mlp(x, eW1, eb1, eW2, eb2, eW3, eb3):
            h = jax.nn.relu(jnp.einsum('baf,efh->ebah', x, eW1) + eb1[:, None, None, :])
            h = jax.nn.relu(jnp.einsum('ebah,ehg->ebag', h, eW2) + eb2[:, None, None, :])
            o = jnp.einsum('ebag,ego->ebao', h, eW3) + eb3[:, None, None, :]
            return jnp.moveaxis(o, 0, -1)
        all_out = _experts_mlp(x, eW1, eb1, eW2, eb2, eW3, eb3)
        shared = _shared_mlp(x, sW1, sb1, sW2, sb2, sW3, sb3)
        gates = jax.nn.softmax(x @ gW + gb, axis=-1)
        topv, topi = jax.lax.top_k(gates, TOPK)
        topw = jax.nn.softmax(topv, axis=-1)
        sel = jnp.take_along_axis(all_out, topi[:, :, None, :], axis=-1)
        gated = jnp.sum(sel * topw[:, :, None, :], axis=-1)
        return shared + gated

    def _L3_gnn_ref(x, weight, edge_val, edge_row, edge_col):
        import jax, jax.numpy as jnp
        import numpy as np
        N_NODES = 3125
        N_EDGES = 100000
        D_IN = 256
        D_OUT = 256
        support = x @ weight
        msgs = support[edge_col] * edge_val[:, None]
        out = jax.ops.segment_sum(msgs, edge_row, num_segments=N_NODES)
        return jax.nn.relu(out)

    def _L3_ffn_ref(x, weight, bias):
        import jax, jax.numpy as jnp
        import numpy as np
        IN_CH = 256
        OUT_CH = 256
        return jnp.einsum('bsi,oi->bso', x, weight) + bias
    edge_index = jnp.stack([src, dst])
    x = x + _L0_gnn_ref(_layernorm(x, axis=-1), L0_gnn_W_qkv, L0_gnn_b_qkv, L0_gnn_W_out, L0_gnn_b_out, src, dst)
    x = x + _L0_ffn_ref(_layernorm(x, axis=-1)[None], L0_ffn_Wr, L0_ffn_br, L0_ffn_W1, L0_ffn_b1, L0_ffn_g1, L0_ffn_be1, L0_ffn_m1, L0_ffn_v1, L0_ffn_W2, L0_ffn_b2, L0_ffn_g2, L0_ffn_be2, L0_ffn_m2, L0_ffn_v2, L0_ffn_Wo, L0_ffn_bo)[0]
    x = x + _L1_gnn_ref(_layernorm(x, axis=-1), edge_index, L1_gnn_W1l, L1_gnn_b1, L1_gnn_W1r, L1_gnn_W2l, L1_gnn_b2, L1_gnn_W2r)
    x = x + _L1_ffn_ref(_layernorm(x, axis=-1)[None], L1_ffn_attention_mask, L1_ffn_wr, L1_ffn_br, L1_ffn_w1, L1_ffn_b1, L1_ffn_w2, L1_ffn_b2)[0]
    x = x + _L2_gnn_ref(_layernorm(x, axis=-1), node_type_19, edge_index, edge_attr_5, L2_gnn_Wk, L2_gnn_bk, L2_gnn_Wq, L2_gnn_bq, L2_gnn_Wv, L2_gnn_bv, L2_gnn_Wa, L2_gnn_ba, L2_gnn_gamma, L2_gnn_beta, L2_gnn_w_time, L2_gnn_b_time)
    x = x + _L2_ffn_ref(_layernorm(x, axis=-1)[None], L2_ffn_sW1, L2_ffn_sb1, L2_ffn_sW2, L2_ffn_sb2, L2_ffn_sW3, L2_ffn_sb3, L2_ffn_eW1, L2_ffn_eb1, L2_ffn_eW2, L2_ffn_eb2, L2_ffn_eW3, L2_ffn_eb3, L2_ffn_gW, L2_ffn_gb)[0]
    x = x + _L3_gnn_ref(_layernorm(x, axis=-1), L3_gnn_weight, edge_weight, src, dst)
    x = x + _L3_ffn_ref(_layernorm(x, axis=-1)[None], L3_ffn_weight, L3_ffn_bias)[0]
    return x

_drawn_inputs = setup_inputs


def setup_inputs(seed=0):
    import zlib

    import numpy as np

    out = dict(_drawn_inputs(seed))
    spreads = {'L0_ffn_br': (0.0, 0.1),
     'L0_ffn_b1': (0.0, 0.373),
     'L0_ffn_g1': (1.0, 0.2),
     'L0_ffn_be1': (0.0, 0.392),
     'L0_ffn_m1': (0.0, 0.368),
     'L0_ffn_v1': (1.0, 0.6),
     'L0_ffn_b2': (0.0, 0.1),
     'L0_ffn_g2': (1.0, 0.2),
     'L0_ffn_be2': (0.0, 0.1),
     'L0_ffn_m2': (0.0, 0.1),
     'L0_ffn_v2': (1.0, 0.574),
     'L0_ffn_bo': (0.0, 0.1),
     'L1_gnn_b1': (0.0, 0.1),
     'L1_gnn_b2': (0.0, 0.1),
     'L1_ffn_b1': (0.0, 0.8),
     'L1_ffn_b2': (0.0, 0.37),
     'L2_gnn_bk': (0.0, 0.8),
     'L2_gnn_bq': (0.0, 0.8),
     'L2_gnn_bv': (0.0, 0.8),
     'L2_gnn_ba': (0.0, 0.8),
     'L2_gnn_gamma': (1.0, 0.2),
     'L2_gnn_beta': (0.0, 0.1),
     'L2_gnn_b_time': (0.0, 0.27),
     'L2_ffn_sb1': (0.0, 0.725),
     'L2_ffn_sb2': (0.0, 0.275),
     'L2_ffn_sb3': (0.0, 0.1),
     'L2_ffn_eb1': (0.0, 0.8),
     'L2_ffn_eb2': (0.0, 0.8),
     'L2_ffn_eb3': (0.0, 0.274),
     'L2_ffn_gb': (0.0, 0.749)}
    factors = {'edge_attr_5': 9.147,
     'L0_gnn_b_qkv': 4.741,
     'L0_gnn_b_out': 4.059,
     'L1_ffn_wr': 3.463,
     'L1_ffn_w1': 3.598,
     'L1_ffn_w2': 3.274,
     'L2_gnn_Wk': 8.0,
     'L2_gnn_Wq': 8.0,
     'L2_gnn_Wv': 8.0,
     'L2_ffn_eW1': 3.811,
     'L2_ffn_eW2': 3.068,
     'L3_ffn_bias': 5.447}
    for name, (base, spread) in spreads.items():
        noise = np.random.default_rng([zlib.crc32(name.encode()), seed]).standard_normal(out[name].shape)
        drawn = base * np.exp(spread * noise) if base else spread * noise
        out[name] = jnp.asarray(drawn.astype(out[name].dtype))
    for name, factor in factors.items():
        out[name] = (out[name] * factor).astype(out[name].dtype)
    return out
```

```python
import numpy as np
from contextlib import ExitStack

import concourse.bass as bass
from concourse import mybir

F32 = mybir.dt.float32
I32 = mybir.dt.int32
U32 = mybir.dt.uint32
BF16 = mybir.dt.bfloat16
ALU = mybir.AluOpType
ACT = mybir.ActivationFunctionType
AXX = mybir.AxisListType.X

P = 128
N = 3125
NT = -(-N // P)
NP = NT * P
D = 256
GT = 5
NG = NT // GT
GR = GT * P
HR = GR // 2
E = 50000
CH = 8
NCH = -(-E // (P * CH))
ET = NCH * CH
EP = ET * P
RUN = 2
ST = 448
assert NCH * CH * P + NT * (RUN * P - 1) <= ST * P
U = 4
NU = ST // U
PW = 8
LO, OTHER, TB, TA, TC, WGT, KEY = range(7)
BIG = 1.0e30
LN_EPS = 1e-5
BN_EPS = 1e-3


def ds(start, size):
    return bass.ds(start, size)


class Phase:

    def __init__(self, nc, name):
        self.nc, self.name, self.stack, self.numbers = nc, name, ExitStack(), []

    def __enter__(self):
        return self

    def __exit__(self, *a):
        self.stack.__exit__(*a)
        runs = []
        for n in sorted(self.numbers):
            if runs and n == runs[-1][1]:
                runs[-1][1] = n + 1
            else:
                runs.append([n, n + 1])
        for first, end in runs:
            self.nc.sync.sem_clear(range(first, end))

    def sem(self, name):
        s = self.stack.enter_context(self.nc.semaphore(f"{self.name}_{name}"))
        self.numbers.append(s.num)
        return s

    def sems(self, name, n):
        return [self.sem(f"{name}{i}") for i in range(n)]

    def gather_sems(self, n):
        return [self.nc.alloc_semaphore(f"{self.name}_gpsimd_dma{i}") for i in range(n)]

    def sb(self, name, shape, dt=F32):
        return self.stack.enter_context(self.nc.sbuf_tensor(f"{self.name}_{name}", shape, dt))

    def ps(self, name, shape, dt=F32):
        return self.stack.enter_context(self.nc.psum_tensor(f"{self.name}_{name}", shape, dt))

    def block(self):
        return self.stack.enter_context(self.nc.Block())


def make_constants(nc, c):
    with Phase(nc, "const") as ph:
        made, cut, i_int = ph.sem("made"), ph.sem("cut"), ph.sem("i_int")
        row_i = ph.sb("row_i", [P, ST], I32)
        col_i = ph.sb("col_i", [P, 1], I32)
        block = ph.block()

        @block.gpsimd
        def _(pool):
            nc.gpsimd.memset(c["ident"][:], 0.0).then_inc(made, 1)
            nc.gpsimd.memset(c["ones"][:], 1.0).then_inc(made, 1)
            nc.gpsimd.iota(row_i[:], [[1, ST]], base=0, channel_multiplier=0).then_inc(i_int, 1)
            nc.gpsimd.iota(col_i[:], [[1, 1]], base=0, channel_multiplier=1).then_inc(i_int, 1)
            pool.wait_ge(made, 2)
            nc.gpsimd.affine_select(out=c["ident"][:], in_=c["ident"][:], compare_op=ALU.not_equal, fill=1.0,
                                    base=0, pattern=[[-1, P]], channel_multiplier=1).then_inc(cut, 1)
            nc.gpsimd.affine_select(out=c["before_col"][:], in_=c["ones"][:], compare_op=ALU.is_gt, fill=0.0,
                                    base=0, pattern=[[-1, P]], channel_multiplier=1).then_inc(cut, 1)
            nc.gpsimd.affine_select(out=c["before_row"][:], in_=c["ones"][:], compare_op=ALU.is_gt, fill=0.0,
                                    base=0, pattern=[[1, P]], channel_multiplier=-1).then_inc(cut, 1)

        @block.vector
        def _(dve):
            dve.wait_ge(i_int, 2)
            nc.vector.tensor_copy(c["iota"][:], row_i[:])
            nc.vector.tensor_copy(c["iota_p"][:], col_i[:])
            nc.vector.memset(c["eps"][:], LN_EPS)
            dve.wait_ge(cut, 1)
            nc.vector.tensor_copy(c["ident_h"][:], c["ident"][:])


def sort_edges(nc, c, io, slots, degree, starts):
    keys = ("dst", "src")
    with Phase(nc, "sort") as ph:
        loaded, filled, blank_made = ph.sem("loaded"), ph.sem("filled"), ph.sem("blank")
        split, floated, zeroed = ph.sem("split"), ph.sem("floated"), ph.sem("zeroed")
        hot = ph.sems("hot", 2)
        counted = ph.sems("counted", 2)
        total, t1, t2, ended = ph.sem("total"), ph.sem("t1"), ph.sem("t2"), ph.sem("ended")
        packed = ph.sem("packed")
        key_i = [ph.sb(f"key_i{k}", [P, ET], I32) for k in range(2)]
        hi_i = [ph.sb(f"hi_i{k}", [P, ET], I32) for k in range(2)]
        lo_i = [ph.sb(f"lo_i{k}", [P, ET], I32) for k in range(2)]
        hi = [ph.sb(f"hi{k}", [P, ET]) for k in range(2)]
        lo = [ph.sb(f"lo{k}", [P, ET]) for k in range(2)]
        key = [ph.sb(f"key{k}", [P, ET]) for k in range(2)]
        pay = [ph.sb(f"pay{k}", [P, ET, PW]) for k in range(2)]
        attr = ph.sb("attr", [P, ET, 5])
        wgt = ph.sb("wgt", [P, ET])
        blank = ph.sb("blank", [P, ST, PW])
        hot_hi = [ph.sb(f"hot_hi{k}", [P, CH, NT], BF16) for k in range(2)]
        hot_lo = [ph.sb(f"hot_lo{k}", [P, CH, P], BF16) for k in range(2)]
        zero = ph.sb("zero", [P, P], BF16)
        count = [ph.sb(f"count{k}", [NT, CH + 1, P]) for k in range(2)]
        small = ph.sb("small", [NT, 2, 8])
        small_i = ph.sb("small_i", [NT, 2, 2], I32)
        incl = ph.sb("incl", [NT, 2, P])
        past = ph.sb("past", [NT, ST])
        i25 = c["iota"][:, 0:NT]
        i128 = c["iota"][:, 0:P]

        with ph.nc.psum_tensor("sort_hist", [NT, 2, 512], F32) as hist, \
                ph.nc.psum_tensor("sort_misc", [P, 2, 512], F32) as misc, ph.nc.Block() as block:

            @block.sync
            def _(sp):
                for k in range(2):
                    sp.dma_start(key_i[k][:], io[keys[k] + "_c"]).then_inc(loaded, 16)
                sp.dma_start(attr[:], io["attr_c"]).then_inc(loaded, 16)
                sp.dma_start(wgt[:], io["w_c"]).then_inc(loaded, 16)
                sp.wait_ge(blank_made, 4)
                for k in range(2):
                    sp.dma_start(slots[k].rearrange("(p t) w -> p t w", t=ST), blank[:]).then_inc(filled, 16)
                sp.wait_ge(filled, 32)

            @block.gpsimd
            def _(pool):
                nc.gpsimd.memset(blank[:], 0.0).then_inc(blank_made, 1)
                pool.wait_ge(blank_made, 1)
                nc.gpsimd.memset(blank[:, :, LO:LO + 1], -1.0).then_inc(blank_made, 1)
                nc.gpsimd.memset(blank[:, :, KEY:KEY + 1], -1.0).then_inc(blank_made, 1)
                nc.gpsimd.memset(zero[:], 0.0).then_inc(blank_made, 1)

            @block.scalar
            def _(act):
                act.wait_ge(loaded, 64)
                act.wait_ge(floated, 2)
                for k in range(2):
                    nc.scalar.copy(pay[k][:, :, LO], lo[k][:])
                    nc.scalar.copy(pay[k][:, :, KEY], key[k][:])
                    nc.scalar.copy(pay[k][:, :, WGT], wgt[:])
                    nc.scalar.copy(pay[k][:, :, TA], attr[:, :, 0])
                    nc.scalar.copy(pay[k][:, :, TB], attr[:, :, 1 + k])
                    nc.scalar.copy(pay[k][:, :, TC], attr[:, :, 2 - k]).then_inc(packed, 1)

            @block.vector
            def _(dve):
                dve.wait_ge(loaded, 64)
                for k in range(2):
                    nc.vector.tensor_scalar(hi_i[k][:], key_i[k][:], 7, None, ALU.logical_shift_right)
                    nc.vector.tensor_scalar(lo_i[k][:], key_i[k][:], P - 1, None, ALU.bitwise_and)
                    nc.vector.tensor_copy(pay[k][:, :, OTHER].bitcast(I32), key_i[1 - k][:])
                    nc.vector.memset(pay[k][:, :, 7], 0.0)
                    nc.vector.tensor_copy(key[k][:], key_i[k][:]).then_inc(split, 1)
                dve.wait_ge(split, 2)
                for k in range(2):
                    nc.vector.tensor_copy(hi[k][:], hi_i[k][:])
                    nc.vector.tensor_copy(lo[k][:], lo_i[k][:]).then_inc(floated, 1)
                dve.wait_ge(floated, 2)
                with nc.vector.Fori(0, NCH) as it:
                    for k in range(2):
                        dve.wait_ge(counted[k], it)
                        nc.vector.tensor_tensor(
                            hot_hi[k][:], i25.unsqueeze(1).to_broadcast([P, CH, NT]),
                            hi[k][:, ds(it * CH, CH)].unsqueeze(2).to_broadcast([P, CH, NT]), ALU.is_equal)
                        nc.vector.tensor_tensor(
                            hot_lo[k][:], i128.unsqueeze(1).to_broadcast([P, CH, P]),
                            lo[k][:, ds(it * CH, CH)].unsqueeze(2).to_broadcast([P, CH, P]),
                            ALU.is_equal).then_inc(hot[k], 1)
                dve.wait_ge(total, 1)
                for k in range(2):
                    nc.vector.tensor_copy(count[k][:, 1, :], hist[:, k, 0:P]).then_inc(t1, 1)
                dve.wait_ge(t1, 2)
                for k in range(2):
                    nc.vector.tensor_reduce(small[:, k, 0:1], count[k][:, 1, :], AXX, ALU.add)
                    nc.vector.tensor_tensor_scan(incl[:, k, :], c["ones"][0:NT, :], count[k][:, 1, :], 0.0,
                                                 ALU.mult, ALU.add).then_inc(t1, 1)
                dve.wait_ge(t1, 4)
                nc.vector.tensor_scalar(small[:, :, 1:2], small[:, :, 0:1], float(RUN * P - 1), None,
                                        ALU.add).then_inc(t1, 1)
                dve.wait_ge(t1, 5)
                nc.vector.tensor_copy(small_i[:, :, 0:1], small[:, :, 1:2]).then_inc(t1, 1)
                dve.wait_ge(t1, 6)
                nc.vector.tensor_scalar(small_i[:, :, 1:2], small_i[:, :, 0:1],
                                        (RUN * P).bit_length() - 1, None, ALU.logical_shift_right).then_inc(t1, 1)
                dve.wait_ge(t1, 7)
                nc.vector.tensor_copy(small[:, :, 2:3], small_i[:, :, 1:2]).then_inc(t2, 1)
                dve.wait_ge(total, 2)
                nc.vector.tensor_copy(small[:, :, 3], misc[0:NT, 0, 0:2]).then_inc(t1, 1)
                dve.wait_ge(t1, 8)
                nc.vector.tensor_tensor(small[:, :, 6:7], small[:, :, 3:4], small[:, :, 2:3], ALU.add)
                nc.vector.tensor_scalar(small[:, :, 5:6], small[:, :, 3:4], float(RUN * P), None,
                                        ALU.mult).then_inc(t1, 1)
                dve.wait_ge(t1, 9)
                nc.vector.tensor_scalar(small[:, :, 4:5], small[:, :, 6:7], float(RUN), None, ALU.mult)
                for k in range(2):
                    nc.vector.tensor_tensor(incl[:, k, :], incl[:, k, :], count[k][:, 1, :],
                                            ALU.subtract).then_inc(t1, 1)
                dve.wait_ge(t1, 11)
                for k in range(2):
                    nc.vector.tensor_scalar(starts[k][:], incl[:, k, :], small[:, k, 5:6], None,
                                            ALU.add)
                for k in range(2):
                    if k:
                        dve.wait_ge(total, 3)
                    nc.vector.tensor_scalar(past[:], c["iota"][0:NT, :], small[:, k, 4:5], None,
                                            ALU.is_ge).then_inc(ended, 1)
                    dve.wait_ge(total, 3 + k)
                    nc.vector.tensor_scalar(c["block_f"][k][:], misc[:, k, 0:ST], float(NT - 1), None,
                                            ALU.min).then_inc(t1, 1)
                    dve.wait_ge(t1, 12 + k)
                    nc.vector.tensor_copy(c["block_i"][k][:], c["block_f"][k][:])
                nc.vector.tensor_copy(degree[:], misc[:, 0, 500 - NT:500])

            @block.tensor
            def _(pe):
                pe.wait_ge(blank_made, 4)
                for k in range(2):
                    nc.tensor.matmul(hist[:, k, 0:P], zero[:, 0:NT], zero[:], start=True, stop=False)
                with nc.tensor.Fori(0, NCH) as it:
                    for k in range(2):
                        pe.wait_ge(hot[k], it + 1)
                        for j in range(CH):
                            last = nc.tensor.matmul(hist[:, k, 0:P], hot_hi[k][:, j, :], hot_lo[k][:, j, :],
                                                    start=False, stop=False)
                        last.then_inc(counted[k], 1)
                for k in range(2):
                    last = nc.tensor.matmul(hist[:, k, 0:P], zero[:, 0:NT], zero[:], start=False, stop=True)
                last.then_inc(total, 1)
                pe.wait_ge(t2, 1)
                nc.tensor.matmul(misc[0:NT, 0, 0:2], c["before_row"][0:NT, 0:NT], small[:, :, 2],
                                 start=True, stop=True).then_inc(total, 1)
                pe.wait_ge(t1, 8)
                nc.tensor.transpose(misc[:, 0, 500 - NT:500], count[0][:, 1, :], c["ident"][0:NT, 0:NT])
                for k in range(2):
                    pe.wait_ge(ended, k + 1)
                    nc.tensor.matmul(misc[:, k, 0:ST], c["ones"][0:NT, :], past[:],
                                     start=True, stop=True).then_inc(total, 1)

        row = [ph.sb(f"row{k}", [P, CH * P], I32) for k in range(2)]
        row_in = ph.sems("row_in", 2)
        hot2 = ph.sems("hot2_", 2)
        turned = ph.sems("turned", 2)
        spread = ph.sems("spread", 2)
        hist_done = ph.sems("hist_done", 2)
        running = ph.sems("running", 2)
        looked = ph.sems("looked", 2)
        ranked = ph.sems("ranked", 2)
        s1, s2 = ph.sems("s1_", 2), ph.sems("s2_", 2)
        placed = ph.sems("placed", 2)
        ringed = ph.sems("ringed", 2)
        scattered = ph.gather_sems(2)
        started, released = ph.sem("started"), ph.sem("released")
        turn_hi = [ph.sb(f"turn_hi{k}", [NT, CH * P]) for k in range(2)]
        junk = ph.sb("junk", [P, CH * P], BF16)
        junk2 = ph.sb("junk2", [P, CH * P], BF16)
        rank = [ph.sb(f"rank{k}", [P, CH]) for k in range(2)]
        seen = [ph.sb(f"seen{k}", [P, CH]) for k in range(2)]
        pos = [ph.sb(f"pos{k}", [P, CH]) for k in range(2)]
        pos_i = [ph.sb(f"pos_i{k}", [P, CH, 3], I32) for k in range(2)]
        rows = [ph.sb(f"rows{k}", [P, CH], I32) for k in range(2)]
        ring = [ph.sb(f"ring{k}", [P, CH, PW]) for k in range(2)]
        hist8 = ph.ps("hist8", [NT, CH * P])
        look = ph.ps("look", [P, CH * P])
        turn = ph.ps("turn", [NT, CH * P], BF16)
        block = ph.block()

        @block.sync
        def _(sp):
            with nc.sync.Fori(0, NCH) as it:
                for k in range(2):
                    sp.wait_ge(ranked[k], it)
                    sp.dma_start(row[k][:], io[keys[k] + "_r"][ds(it * (CH * P), CH * P)]
                                 .partition_broadcast(P)).then_inc(row_in[k], 16)

        @block.vector
        def _(dve):
            for k in range(2):
                nc.vector.tensor_copy(count[k][:, 0, :], starts[k][:]).then_inc(started, 1)
            dve.wait_ge(started, 2)
            with nc.vector.Fori(0, NCH) as it:
                for k in range(2):
                    dve.wait_ge(hist_done[k], it)
                    dve.wait_ge(s1[k], it)
                    nc.vector.tensor_tensor(
                        hot_hi[k][:], i25.unsqueeze(1).to_broadcast([P, CH, NT]),
                        hi[k][:, ds(it * CH, CH)].unsqueeze(2).to_broadcast([P, CH, NT]), ALU.is_equal)
                    nc.vector.tensor_tensor(
                        hot_lo[k][:], i128.unsqueeze(1).to_broadcast([P, CH, P]),
                        lo[k][:, ds(it * CH, CH)].unsqueeze(2).to_broadcast([P, CH, P]),
                        ALU.is_equal).then_inc(hot2[k], 1)
                    dve.wait_ge(row_in[k], it * 16 + 16)
                    for j in range(CH):
                        last = nc.vector.scalar_tensor_tensor(
                            junk[:, j * P:(j + 1) * P], row[k][:, j * P:(j + 1) * P], key[k][:, ds(it * CH + j, 1)],
                            c["before_col"][:], ALU.is_equal, ALU.mult, accum_out=rank[k][:, j:j + 1])
                    last.then_inc(ranked[k], 1)
                    dve.wait_ge(hist_done[k], it + 1)
                    for j in range(CH):
                        nc.vector.tensor_tensor(count[k][:, j + 1, :], count[k][:, j, :],
                                                hist8[:, j * P:(j + 1) * P], ALU.add).then_inc(running[k], 1)
                        dve.wait_ge(running[k], it * CH + j + 1)
                    dve.wait_ge(looked[k], it + 1)
                    nc.vector.tensor_copy(count[k][:, 0, :], count[k][:, CH, :])
                    for j in range(CH):
                        last = nc.vector.scalar_tensor_tensor(
                            junk2[:, j * P:(j + 1) * P], look[:, j * P:(j + 1) * P], 1.0, hot_lo[k][:, j, :],
                            ALU.mult, ALU.mult, accum_out=seen[k][:, j:j + 1])
                    last.then_inc(s1[k], 1)
                    dve.wait_ge(s1[k], it + 1)
                    dve.wait_ge(ranked[k], it + 1)
                    nc.vector.tensor_tensor(pos[k][:], seen[k][:], rank[k][:], ALU.add).then_inc(s2[k], 1)
                    dve.wait_ge(s2[k], it * 5 + 1)
                    nc.vector.tensor_copy(pos_i[k][:, :, 0], pos[k][:]).then_inc(s2[k], 1)
                    dve.wait_ge(s2[k], it * 5 + 2)
                    nc.vector.tensor_scalar(pos_i[k][:, :, 1], pos_i[k][:, :, 0], P - 1, None,
                                            ALU.bitwise_and).then_inc(s2[k], 1)
                    nc.vector.tensor_scalar(pos_i[k][:, :, 2], pos_i[k][:, :, 0], 7, None,
                                            ALU.logical_shift_right).then_inc(s2[k], 1)
                    dve.wait_ge(s2[k], it * 5 + 4)
                    dve.wait_ge(scattered[k], it * (16 * CH))
                    nc.vector.scalar_tensor_tensor(rows[k][:], pos_i[k][:, :, 1], float(ST),
                                                   pos_i[k][:, :, 2], ALU.mult, ALU.add).then_inc(placed[k], 1)
                    nc.vector.sem_inc(s2[k], 1)

        @block.scalar
        def _(act):
            with nc.scalar.Fori(0, NCH) as it:
                for k in range(2):
                    act.wait_ge(turned[k], it + 1)
                    act.wait_ge(looked[k], it)
                    nc.scalar.copy(turn_hi[k][:], turn[:]).then_inc(spread[k], 1)
                    act.wait_ge(scattered[k], it * (16 * CH))
                    nc.scalar.copy(ring[k][:].bitcast(U32).rearrange("p t w -> p (t w)"),
                                   pay[k][:, ds(it * CH, CH), :].bitcast(U32).rearrange("p t w -> p (t w)")
                                   ).then_inc(ringed[k], 1)

        @block.tensor
        def _(pe):
            with nc.tensor.Fori(0, NCH) as it:
                for k in range(2):
                    pe.wait_ge(hot2[k], it + 1)
                    if k:
                        pe.wait_ge(spread[0], it + 1)
                    else:
                        pe.wait_ge(spread[1], it)
                    for j in range(CH):
                        last = nc.tensor.transpose(turn[:, j * P:(j + 1) * P], hot_hi[k][:, j, :],
                                                   c["ident_h"][:])
                    last.then_inc(turned[k], 1)
                    if k:
                        pe.wait_ge(running[0], it * CH + CH)
                    else:
                        pe.wait_ge(running[1], it * CH)
                    for j in range(CH):
                        last = nc.tensor.matmul(hist8[:, j * P:(j + 1) * P], hot_hi[k][:, j, :],
                                                hot_lo[k][:, j, :], start=True, stop=True)
                    last.then_inc(hist_done[k], 1)
                    pe.wait_ge(spread[k], it + 1)
                    pe.wait_ge(running[k], it * CH + CH)
                    if k:
                        pe.wait_ge(s1[0], it + 1)
                    else:
                        pe.wait_ge(s1[1], it)
                    for j in range(CH):
                        last = nc.tensor.matmul(look[:, j * P:(j + 1) * P], turn_hi[k][:, j * P:(j + 1) * P],
                                                count[k][:, j, :], start=True, stop=True)
                    last.then_inc(looked[k], 1)

        @block.gpsimd
        def _(pool):
            with nc.gpsimd.Fori(0, NCH) as it:
                for k in range(2):
                    pool.wait_ge(placed[k], it + 1)
                    pool.wait_ge(ringed[k], it + 1)
                    pool.sem_inc(released, 1)
                    for j in range(CH):
                        pool.indirect_dma_start(
                            out=slots[k], out_offset=bass.IndirectOffsetOnAxis(
                                ap=rows[k][:, j:j + 1].bitcast(U32), axis=0),
                            in_=ring[k][:, j, :], in_offset=None).then_inc(scattered[k], 16)
            for k in range(2):
                pool.wait_ge(scattered[k], NCH * CH * 16)


def turn_slot_rows(nc, c, slots, lo_rows, key_rows):
    TQ = ST // 4
    with Phase(nc, "turn") as ph:
        loaded, turned, copied, stored = ph.sem("loaded"), ph.sem("turned"), ph.sem("copied"), ph.sem("stored")
        slot = [ph.sb(f"slot{k}", [P, ST, PW]) for k in range(2)]
        word = ph.sb("word", [P, 4, ST])
        out = ph.sb("out", [TQ, 4, 4, P])
        picked = ph.sem("picked")
        pt = ph.ps("pt", [TQ, 4, 4, P])
        block = ph.block()

        @block.sync
        def _(sp):
            for k in range(2):
                sp.dma_start(slot[k][:], slots[k].rearrange("(p t) w -> p t w", t=ST)).then_inc(loaded, 16)
            for n in range(4):
                sp.wait_ge(copied, n + 1)
                dst = (lo_rows, key_rows)[n % 2][n // 2]
                sp.dma_start(dst.rearrange("(q t e) -> t q e", q=4, e=P), out[:, n, :, :]).then_inc(stored, 16)
            sp.wait_ge(stored, 64)

        @block.vector
        def _(dve):
            dve.wait_ge(loaded, 32)
            for n in range(4):
                nc.vector.tensor_copy(word[:, n, :], slot[n // 2][:, :, (LO, KEY)[n % 2]]).then_inc(picked, 1)

        @block.tensor
        def _(pe):
            for n in range(4):
                pe.wait_ge(picked, n + 1)
                for q in range(4):
                    last = nc.tensor.transpose(pt[:, n, q, :], word[:, n, q * TQ:(q + 1) * TQ], c["ident"][:])
                last.then_inc(turned, 1)

        @block.scalar
        def _(act):
            for n in range(4):
                act.wait_ge(turned, n + 1)
                nc.scalar.copy(out[:, n, :, :], pt[:, n, :, :]).then_inc(copied, 1)


def layernorm_stats(nc, c, name, src):
    with Phase(nc, name) as ph:
        st = ph.sb("st", [P, NT, 6])
        d = ph.sb("d", [P, NT])
        v = ph.sb("v", [P, NT])
        w = ph.sb("w", [P, NT])
        sd = ph.sb("sd", [P, NT])
        counted, step, rooted = ph.sem("counted"), ph.sem("step"), ph.sem("rooted")
        block = ph.block()

        @block.vector
        def _(dve):
            with nc.vector.Fori(0, NT) as i:
                nc.vector.bn_stats(st[:, ds(i, 1), :].rearrange("p a b -> p (a b)"),
                                   src[:, ds(i, 1), :].rearrange("p a b -> p (a b)")).then_inc(counted, 1)
            dve.wait_ge(counted, NT)
            nc.vector.tensor_tensor(d[:], st[:, :, 1], st[:, :, 4], ALU.subtract)
            nc.vector.tensor_tensor(v[:], st[:, :, 2], st[:, :, 5], ALU.add)
            nc.vector.tensor_tensor(w[:], st[:, :, 1], st[:, :, 4], ALU.add).then_inc(step, 1)
            dve.wait_ge(step, 1)
            nc.vector.tensor_scalar(c["mean"][:], w[:], 0.5, None, ALU.mult)
            nc.vector.scalar_tensor_tensor(d[:], d[:], 0.25, d[:], ALU.mult, ALU.mult).then_inc(step, 1)
            dve.wait_ge(step, 2)
            nc.vector.scalar_tensor_tensor(v[:], v[:], 1.0 / D, d[:], ALU.mult, ALU.add).then_inc(step, 1)
            dve.wait_ge(rooted, 1)
            nc.vector.reciprocal(c["rstd"][:], sd[:])

        @block.scalar
        def _(act):
            act.wait_ge(step, 3)
            nc.scalar.activation(sd[:], v[:], ACT.Sqrt, bias=c["eps"][:]).then_inc(rooted, 1)


class Group:

    def __init__(self, ph, c, src, name="g", pT=None, scale=None, ahead=None):
        self.nc, self.c, self.src, self.scale, self.ahead = ph.nc, c, src, scale, ahead
        self.xn = ph.sb(name + "_xn", [P, GT, D])
        self.xT = ph.sb(name + "_xT", [P, D // P, GR])
        self.pT = ph.ps(name + "_pT", [P, 3, 512]) if pT is None else pT
        self.normed, self.turned = ph.sem(name + "_normed"), ph.sem(name + "_turned")
        self.ready, self.used = ph.sem(name + "_ready"), ph.sem(name + "_used")

    def normalise(self, dve, it):
        dve.wait_ge(self.turned, it)
        for j in range(GT):
            i = it * GT + j
            row = self.src[:, ds(i, 1), 0:D].rearrange("p a b -> p (a b)")
            if self.scale is None:
                last = self.nc.vector.tensor_scalar(self.xn[:, j, :], row, self.c["mean"][:, ds(i, 1)],
                                                    self.c["rstd"][:, ds(i, 1)], ALU.subtract, ALU.mult)
            else:
                last = self.nc.vector.tensor_scalar(self.xn[:, j, :], row, self.scale[:, ds(i, 1)], None,
                                                    ALU.mult)
        last.then_inc(self.normed, 1)

    def turn(self, pe, it):
        pe.wait_ge(self.normed, it + 1)
        pe.wait_ge(self.ready, it)
        if self.ahead:
            pe.wait_ge(self.ahead.ready, it + 1)
        for j in range(GT):
            for h in range(2):
                col = (j % 2) * D + h * P
                last = self.nc.tensor.transpose(self.pT[:, j // 2, col:col + P], self.xn[:, j, h * P:(h + 1) * P],
                                                self.c["ident"][:])
        last.then_inc(self.turned, 1)

    def copy(self, act, it):
        act.wait_ge(self.turned, it + 1)
        act.wait_ge(self.used, it)
        for b in range(3):
            n = 2 if b < 2 else 1
            last = self.nc.scalar.copy(
                self.xT[:, :, 2 * b * P:(2 * b + n) * P].rearrange("p h (j r) -> p j h r", r=P),
                self.pT[:, b, 0:n * D].rearrange("p (j h r) -> p j h r", h=2, r=P))
        last.then_inc(self.ready, 1)


def rowof(t, i):
    return t[:, ds(i, 1), :].rearrange("p a b -> p (a b)")


def attention_inputs(nc, c, io, X, q_rows, kv_table):
    with Phase(nc, "qkv") as ph:
        g = Group(ph, c, X)
        w = ph.sb("w", [P, 2, 4 * D])
        bias = ph.sb("bias", [P, 4 * D])
        kv = ph.sb("kv", [P, GT, 2 * D])
        prod = ph.ps("prod", [P, 2, 4 * D])
        loaded, done, moved = ph.sem("loaded"), ph.sem("done"), ph.sem("moved")
        evac, kept = ph.sem("evac"), ph.sem("kept")
        stored = ph.sems("stored", GT)
        block = ph.block()

        @block.sync
        def _(sp):
            sp.dma_start(w[:], io["W0"].rearrange("(h p) n -> p h n", p=P)).then_inc(loaded, 16)
            sp.dma_start(bias[:], io["b0"].partition_broadcast(P)).then_inc(loaded, 16)
            with nc.sync.Fori(0, NG) as it:
                for j in range(GT):
                    sp.wait_ge(evac, it * GT + j + 1)
                    sp.dma_start(kv_table[ds((it * GT + j) * P, P), :], kv[:, j, :]).then_inc(stored[j], 16)
            for j in range(GT):
                sp.wait_ge(stored[j], 16 * NG)

        @block.vector
        def _(dve):
            dve.wait_ge(loaded, 32)
            with nc.vector.Fori(0, NG) as it:
                g.normalise(dve, it)
                for j in range(GT):
                    i = it * GT + j
                    dve.wait_ge(done, i + 1)
                    nc.vector.tensor_tensor(rowof(q_rows, i), prod[:, j % 2, D:2 * D], bias[:, D:2 * D], ALU.add)
                    dve.wait_ge(stored[j], it * 16)
                    nc.vector.tensor_tensor(kv[:, j, :], prod[:, j % 2, 2 * D:], bias[:, 2 * D:],
                                            ALU.add)
                    nc.vector.tensor_tensor(rowof(X, i), rowof(X, i), bias[:, 0:D], ALU.add).then_inc(moved, 1)
                    dve.wait_ge(moved, i + 1)
                    nc.vector.tensor_tensor(rowof(X, i), rowof(X, i), prod[:, j % 2, 0:D],
                                            ALU.add).then_inc(evac, 1)

        @block.scalar
        def _(act):
            with nc.scalar.Fori(0, NG) as it:
                g.copy(act, it)

        @block.tensor
        def _(pe):
            pe.wait_ge(loaded, 32)
            with nc.tensor.Fori(0, NG) as it:
                g.turn(pe, it)
                pe.wait_ge(g.ready, it + 1)
                for j in range(GT):
                    pe.wait_ge(evac, it * GT + max(j - 1, 0))
                    for half in range(2):
                        for h in range(2):
                            last = nc.tensor.matmul(prod[:, j % 2, half * 512:(half + 1) * 512],
                                                    g.xT[:, h, j * P:(j + 1) * P],
                                                    w[:, h, half * 512:(half + 1) * 512],
                                                    start=(h == 0), stop=(h == 1))
                    last.then_inc(done, 1)
                pe.wait_ge(done, it * GT + GT)
                pe.sem_inc(g.used, 1)


def attention_scores(nc, c, slots, lo_rows, q_rows, kv_table, v_stream, scores, blocks):
    H, DH, R = 8, D // 8, 4
    last_round = NU // R - 1
    with Phase(nc, "score") as ph:
        slot = ph.sb("slot", [P, ST + R * U, PW])
        lo_row = ph.sb("lo_row", [P, R, U * P])
        hotT = ph.sb("hotT", [P, R, U, P])
        idx = ph.sb("idx", [P, R, U], I32)
        kv = ph.sb("kv", [P, R, U, 2 * D])
        prod = ph.sb("prod", [P, 2, U, D])
        q = [ph.ps(f"q{u}", [P, U, D]) for u in range(R)]
        loaded, blanked, released = ph.sem("loaded"), ph.sem("blanked"), ph.sem("released")
        row_in, picked, hot = ph.sems("row_in", R), ph.sems("picked", R), ph.sems("hot", R)
        gathered, asked, mult = ph.gather_sems(R), ph.sems("asked", R), ph.sems("mult", R)
        streamed, summed = ph.sems("streamed", R), ph.sems("summed", 2)
        block = ph.block()

        @block.sync
        def _(sp):
            def fetch_row(start, u):
                sp.dma_start(lo_row[:, u, :], lo_rows[ds(start, U * P)]
                             .partition_broadcast(P)).then_inc(row_in[u], 16)

            def stream(n, u):
                sp.wait_ge(gathered[u], (n + 1) * (16 * U))
                sp.dma_start(v_stream[:, ds((n * R + u) * U, U), :], kv[:, u, :, D:]).then_inc(streamed[u], 16)

            sp.dma_start(slot[:, 0:ST, :], slots.rearrange("(p t) w -> p t w", t=ST)).then_inc(loaded, 16)
            for u in range(R):
                fetch_row(u * (U * P), u)
            with nc.sync.Fori(0, last_round) as it:
                for u in range(R):
                    sp.wait_ge(hot[u], it + 1)
                    fetch_row(it * (R * U * P) + (R + u) * (U * P), u)
                    stream(it, u)
            for u in range(R):
                stream(last_round, u)
            for u in range(R):
                sp.wait_ge(streamed[u], 16 * (NU // R))

        @block.scalar
        def _(act):
            def pick(n, u):
                nc.scalar.copy(idx[:, u, :].bitcast(U32), slot[:, ds((n * R + u) * U, U), OTHER].bitcast(U32)
                               ).then_inc(picked[u], 1)

            act.wait_ge(loaded, 16)
            act.wait_ge(blanked, 1)
            for u in range(R):
                pick(0, u)
            with nc.scalar.Fori(0, NU // R) as it:
                for u in range(R):
                    act.wait_ge(gathered[u], (it + 1) * (16 * U))
                    pick(it + 1, u)

        @block.gpsimd
        def _(pool):
            with nc.gpsimd.Fori(0, NU // R) as it:
                for u in range(R):
                    pool.wait_ge(picked[u], it + 1)
                    pool.wait_ge(mult[u], it)
                    pool.wait_ge(streamed[u], it * 16)
                    pool.sem_inc(released, 1)
                    for j in range(U):
                        pool.indirect_dma_start(
                            out=kv[:, u, j, :], out_offset=None, in_=kv_table,
                            in_offset=bass.IndirectOffsetOnAxis(ap=idx[:, u, j:j + 1].bitcast(U32), axis=0)
                        ).then_inc(gathered[u], 16)

        @block.vector
        def _(dve):
            def make_hot(n, u):
                dve.wait_ge(row_in[u], n * 16 + 16)
                dve.wait_ge(asked[u], n)
                nc.vector.tensor_scalar(hotT[:, u, :, :].rearrange("p a b -> p (a b)"), lo_row[:, u, :],
                                        c["iota_p"][:], None, ALU.is_equal).then_inc(hot[u], 1)

            def score(n, u, hot_next=None):
                dve.wait_ge(gathered[u], (n + 1) * (16 * U))
                dve.wait_ge(asked[u], n + 1)
                dve.wait_ge(summed[u % 2], n * (R // 2) + u // 2)
                nc.vector.tensor_tensor(prod[:, u % 2, :, :], kv[:, u, :, 0:D], q[u][:], ALU.mult
                                        ).then_inc(mult[u], 1)
                if hot_next:
                    make_hot(*hot_next)
                dve.wait_ge(mult[u], n + 1)
                nc.vector.tensor_reduce(
                    scores[:, ds((n * R + u) * (U * H), U * H)],
                    prod[:, u % 2, :, :].rearrange("p j (h d) -> p (j h) d", d=DH), AXX, ALU.add
                ).then_inc(summed[u % 2], 1)

            dve.wait_ge(loaded, 16)
            nc.vector.memset(slot[:, ST:, :], 0.0).then_inc(blanked, 1)
            make_hot(0, 0)
            make_hot(0, 1)
            with nc.vector.Fori(0, last_round) as it:
                for u in range(R):
                    score(it, u, (it + (u + 2) // R, (u + 2) % R))
            for u in range(R):
                score(last_round, u, (last_round, u + 2) if u + 2 < R else None)

        @block.tensor
        def _(pe):
            with nc.tensor.Fori(0, NU // R) as it:
                for u in range(R):
                    nb = load_blocks(nc.tensor, blocks, it * R + u)
                    pe.wait_ge(hot[u], it + 1)
                    pe.wait_ge(mult[u], it)
                    for j in range(U):
                        last = nc.tensor.matmul(q[u][:, j, :], hotT[:, u, j, :], rowof(q_rows, nb[j // RUN]),
                                                start=True, stop=True)
                    last.then_inc(asked[u], 1)


def load_blocks(eng, blocks, unit):
    return [eng.value_load(blocks[0:1, ds(unit * U + j, 1)], min_val=0, max_val=NT - 1)
            for j in range(0, U, RUN)]


def segment_softmax(nc, c, name, H, scale, key_rows, scores):
    J = P // H
    G = ST // J
    L = G * P
    R = ST // (P // 4)
    S = G // R
    with Phase(nc, name) as ph:
        sc = ph.sb("sc", [P, L])
        key = ph.sb("key", [P, L])
        neg = ph.sb("neg", [P, L + 1])
        top = ph.sb("top", [P, L])
        tin = ph.sb("tin", [P, S, P])
        j_sel, h_sel = ph.sb("j_sel", [P, J]), ph.sb("h_sel", [P, P])
        ints = ph.sb("ints", [P, 2, P + 2], I32)
        flt = ph.sb("flt", [P, P + 2])
        ends = ph.sb("ends", [P, 4])
        each = ph.sb("each", [P, 4, J])
        every = ph.sb("every", [P, 4, J])
        cand = ph.sb("cand", [P, 2, 2 * J])
        best = ph.sb("best", [P, 2])
        pt = [ph.ps(f"pt{s}", [P, P]) for s in range(S)]
        pall = ph.ps("pall", [P, 4 * J])
        loaded = ph.sem("loaded")
        picked, turned, copied = ph.sem("picked"), ph.sem("turned"), ph.sem("copied")
        step, spread = ph.sem("step"), ph.sem("spread")
        raised, back, written = ph.sem("raised"), ph.sem("back"), ph.sem("written")
        by_stretch = scores[:].rearrange("p (j g h) -> p g j h", g=G, h=H)
        block = ph.block()

        @block.sync
        def _(sp):
            sp.dma_start(key[:],
                         key_rows.rearrange("(j l) -> j l", l=L).unsqueeze(1).to_broadcast([J, H, L])
                         ).then_inc(loaded, 16)

        @block.vector
        def _(dve):
            with nc.vector.Fori(0, R) as it:
                for s in range(S):
                    dve.wait_ge(turned, it * S + max(s + 1 - S, 0))
                    nc.vector.tensor_copy(
                        tin[:, s, :].rearrange("p (j h) -> p j h", h=H),
                        by_stretch[:, ds(it * S + s, 1), :, :].rearrange("p g j h -> p (g j) h")
                    ).then_inc(picked, 1)
            nc.vector.tensor_copy(ints[:, 0, 0:P], c["iota"][:, 0:P])
            nc.vector.tensor_copy(ints[:, 0, P:P + 1], c["iota_p"][:]).then_inc(step, 1)
            dve.wait_ge(step, 1)
            nc.vector.tensor_scalar(ints[:, 1, 0:P + 1], ints[:, 0, 0:P + 1], H - 1, None, ALU.bitwise_and).then_inc(step, 1)
            nc.vector.tensor_scalar(ints[:, 1, P + 1:P + 2], ints[:, 0, P:P + 1], H.bit_length() - 1, None,
                                    ALU.logical_shift_right).then_inc(step, 1)
            dve.wait_ge(step, 3)
            nc.vector.tensor_copy(flt[:], ints[:, 1, :]).then_inc(step, 1)
            dve.wait_ge(step, 4)
            nc.vector.tensor_scalar(h_sel[:], flt[:, 0:P], flt[:, P:P + 1], None, ALU.is_equal)
            nc.vector.tensor_scalar(j_sel[:], c["iota"][:, 0:J], flt[:, P + 1:P + 2], None, ALU.is_equal)
            dve.wait_ge(loaded, 16)
            nc.vector.memset(neg[:, 0:1], -BIG)
            nc.vector.memset(neg[:, L:L + 1], -BIG)
            nc.vector.tensor_tensor(neg[:, 1:L], key[:, 1:L], key[:, 0:L - 1], ALU.not_equal).then_inc(step, 1)
            dve.wait_ge(step, 5)
            nc.vector.tensor_scalar(neg[:, 1:L], neg[:, 1:L], -BIG, None, ALU.mult).then_inc(step, 1)
            dve.wait_ge(step, 6)
            dve.wait_ge(copied, G)
            nc.vector.tensor_tensor_scan(top[:], neg[:, 0:L], sc[:], -BIG, ALU.add, ALU.max).then_inc(step, 1)
            dve.wait_ge(step, 7)
            nc.vector.tensor_tensor_scan(top[:, ::-1], neg[:, L:0:-1], top[:, ::-1], -BIG, ALU.add, ALU.max
                                         ).then_inc(step, 1)
            dve.wait_ge(step, 8)
            nc.vector.tensor_copy(ends[:, 0:1], key[:, 0:1])
            nc.vector.tensor_copy(ends[:, 1:2], key[:, L - 1:L])
            nc.vector.tensor_copy(ends[:, 2:3], top[:, 0:1])
            nc.vector.tensor_copy(ends[:, 3:4], top[:, L - 1:L]).then_inc(step, 1)
            dve.wait_ge(step, 9)
            for n in range(4):
                nc.vector.tensor_scalar(each[:, n, :], j_sel[:], ends[:, n:n + 1], None, ALU.mult
                                        ).then_inc(step, 1)
            dve.wait_ge(spread, 1)
            nc.vector.tensor_copy(every[:].rearrange("p a j -> p (a j)"), pall[:]).then_inc(step, 1)
            dve.wait_ge(step, 14)
            for n in range(2):
                nc.vector.tensor_scalar(cand[:, n, :], every[:, 0:2, :].rearrange("p a j -> p (a j)"),
                                        ends[:, n:n + 1], -BIG, ALU.not_equal, ALU.mult).then_inc(step, 1)
            for n in range(2):
                dve.wait_ge(step, 15 + n)
                nc.vector.tensor_tensor(cand[:, n, :], cand[:, n, :],
                                        every[:, 2:4, :].rearrange("p a j -> p (a j)"), ALU.add
                                        ).then_inc(step, 1)
            dve.wait_ge(step, 18)
            nc.vector.tensor_reduce(best[:], cand[:], AXX, ALU.max).then_inc(step, 1)
            dve.wait_ge(step, 19)
            for n in range(2):
                nc.vector.tensor_scalar(neg[:, 0:L], key[:], ends[:, n:n + 1], -BIG, ALU.not_equal, ALU.mult
                                        ).then_inc(step, 1)
                dve.wait_ge(step, 20 + 2 * n)
                nc.vector.scalar_tensor_tensor(top[:], neg[:, 0:L], best[:, n:n + 1], top[:], ALU.add, ALU.max
                                               ).then_inc(step, 1)
                dve.wait_ge(step, 21 + 2 * n)
            nc.vector.tensor_tensor(sc[:], sc[:], top[:], ALU.subtract).then_inc(step, 1)
            with nc.vector.Fori(0, R) as it:
                for s in range(S):
                    dve.wait_ge(back, it * S + s + 1)
                    nc.vector.tensor_copy(
                        by_stretch[:, ds(it * S + s, 1), :, :].rearrange("p g j h -> p (g j) h"),
                        pt[s][:].rearrange("p (j h) -> p j h", h=H)).then_inc(written, 1)

        @block.tensor
        def _(pe):
            with nc.tensor.Fori(0, R) as it:
                for s in range(S):
                    pe.wait_ge(picked, it * S + s + 1)
                    pe.wait_ge(copied, it * S + max(s + 1 - S, 0))
                    nc.tensor.transpose(pt[s][:], tin[:, s, :], c["ident"][:]).then_inc(turned, 1)
            pe.wait_ge(step, 13)
            nc.tensor.matmul(pall[:], h_sel[:], each[:].rearrange("p a j -> p (a j)"), start=True, stop=True
                             ).then_inc(spread, 1)
            with nc.tensor.Fori(0, R) as it:
                for s in range(S):
                    pe.wait_ge(raised, it * S + s + 1)
                    pe.wait_ge(written, it * S + max(s + 1 - S, 0))
                    nc.tensor.transpose(pt[s][:], tin[:, s, :], c["ident"][:]).then_inc(back, 1)

        @block.scalar
        def _(act):
            with nc.scalar.Fori(0, R) as it:
                for s in range(S):
                    act.wait_ge(turned, it * S + s + 1)
                    nc.scalar.copy(sc[:, ds((it * S + s) * P, P)], pt[s][:]).then_inc(copied, 1)
            act.wait_ge(step, 24)
            with nc.scalar.Fori(0, R) as it:
                for s in range(S):
                    act.wait_ge(back, it * S + max(s + 1 - S, 0))
                    nc.scalar.activation(tin[:, s, :], sc[:, ds((it * S + s) * P, P)], ACT.Exp, scale=scale
                                         ).then_inc(raised, 1)


def attention_values(nc, c, name, slots, v_stream, ex, blocks, agg, H, VW):
    W = D + H
    with Phase(nc, name) as ph:
        slot = ph.sb("slot", [P, ST, PW])
        hot = ph.sb("hot", [P, 2, U, P])
        v = ph.sb("v", [P, 2, U, D])
        msg = ph.sb("msg", [P, 2, U, W])
        out = [ph.ps(f"out{u}", [P, U // RUN, 512]) for u in range(2)]
        loaded = ph.sem("loaded")
        v_in, made, scaled, tailed = ph.sems("v_in", 2), ph.sems("made", 2), ph.sems("scaled", 2), ph.sems("tailed", 2)
        summed, added, cleared = ph.sems("summed", 2), ph.sems("added", 2), ph.sem("cleared")
        block = ph.block()

        @block.sync
        def _(sp):
            sp.dma_start(slot[:], slots.rearrange("(p t) w -> p t w", t=ST)).then_inc(loaded, 16)
            with nc.sync.Fori(0, NU // 2) as it:
                for u in range(2):
                    sp.wait_ge(scaled[u], it)
                    sp.wait_ge(tailed[u], it)
                    sp.dma_start(v[:, u, :, :], v_stream[:, ds((it * 2 + u) * U, U), :]).then_inc(v_in[u], 16)

        @block.scalar
        def _(act):
            with nc.scalar.Fori(0, NU // 2) as it:
                for u in range(2):
                    act.wait_ge(summed[u], it)
                    last = nc.scalar.copy(
                        msg[:, u, :, VW:VW + H],
                        ex[:, ds((it * 2 + u) * (U * H), U * H)].rearrange("p (j h) -> p j h", h=H))
                    if VW < D:
                        act.wait_ge(v_in[u], it * 16 + 16)
                        last = nc.scalar.copy(msg[:, u, :, VW + H:W], v[:, u, :, VW:D])
                    last.then_inc(tailed[u], 1)

        @block.vector
        def _(dve):
            def make(it, u):
                dve.wait_ge(summed[u], it)
                nc.vector.tensor_tensor(
                    hot[:, u, :, :], c["iota"][:, 0:P].unsqueeze(1).to_broadcast([P, U, P]),
                    slot[:, ds((it * 2 + u) * U, U), LO].unsqueeze(2).to_broadcast([P, U, P]),
                    ALU.is_equal).then_inc(made[u], 1)
                dve.wait_ge(v_in[u], it * 16 + 16)
                nc.vector.tensor_tensor(
                    msg[:, u, :, 0:VW].rearrange("p j (h d) -> p j h d", h=H),
                    v[:, u, :, 0:VW].rearrange("p j (h d) -> p j h d", h=H),
                    ex[:, ds((it * 2 + u) * (U * H), U * H)].rearrange("p (j h) -> p j h", h=H)
                    .unsqueeze(3).to_broadcast([P, U, H, VW // H]), ALU.mult).then_inc(scaled[u], 1)

            def add(it, u):
                nb = load_blocks(nc.vector, blocks, it * 2 + u)
                dve.wait_ge(summed[u], it + 1)
                for r in range(U // RUN):
                    if r:
                        dve.wait_ge(added[u], it * (U // RUN) + r)
                    else:
                        dve.wait_ge(added[1 - u], (it + u) * (U // RUN))
                    nc.vector.tensor_tensor(agg[:, ds(nb[r], 1), 0:W].rearrange("p a b -> p (a b)"),
                                            agg[:, ds(nb[r], 1), 0:W].rearrange("p a b -> p (a b)"),
                                            out[u][:, r, 0:W], ALU.add).then_inc(added[u], 1)

            nc.vector.memset(agg[:], 0.0).then_inc(cleared, 1)
            dve.wait_ge(loaded, 16)
            dve.wait_ge(cleared, 1)
            for u in range(2):
                make(0, u)
            with nc.vector.Fori(0, NU // 2 - 1) as it:
                for u in range(2):
                    make(it + 1, u)
                    add(it, u)
            for u in range(2):
                add(NU // 2 - 1, u)

        @block.tensor
        def _(pe):
            with nc.tensor.Fori(0, NU // 2) as it:
                for u in range(2):
                    pe.wait_ge(made[u], it + 1)
                    pe.wait_ge(scaled[u], it + 1)
                    pe.wait_ge(tailed[u], it + 1)
                    pe.wait_ge(added[u], it * (U // RUN))
                    for j in range(U):
                        last = nc.tensor.matmul(out[u][:, j // RUN, 0:W], hot[:, u, j, :], msg[:, u, j, :],
                                                start=(j % RUN == 0), stop=(j % RUN == RUN - 1))
                    last.then_inc(summed[u], 1)


def attention_output(nc, c, io, X, agg):
    H = 8
    with Phase(nc, "attn_out") as ph:
        w = ph.sb("w", [P, 2, D])
        msg = ph.sb("msg", [P, GT, D])
        den = ph.sb("den", [P, NT, H])
        rec = ph.sb("rec", [P, NT, H])
        mT = ph.sb("mT", [P, GT, 2, P])
        pT = ph.ps("pT", [P, GT, 512])
        prod = ph.ps("prod", [P, 3, 512])
        loaded, clipped, recd, made = ph.sem("loaded"), ph.sem("clipped"), ph.sem("recd"), ph.sem("made")
        turned, copied, done, added = ph.sem("turned"), ph.sem("copied"), ph.sem("done"), ph.sem("added")
        block = ph.block()

        @block.sync
        def _(sp):
            sp.dma_start(w[:], io["W0m"].rearrange("(h p) n -> p h n", p=P)).then_inc(loaded, 16)

        @block.vector
        def _(dve):
            nc.vector.tensor_scalar(den[:], agg[:, :, D:D + H], 1e-20, None, ALU.max).then_inc(clipped, 1)
            dve.wait_ge(clipped, 1)
            nc.vector.reciprocal(rec[:], den[:]).then_inc(recd, 1)
            dve.wait_ge(recd, 1)
            with nc.vector.Fori(0, NG) as it:
                dve.wait_ge(turned, it * GT)
                for j in range(GT):
                    i = it * GT + j
                    nc.vector.tensor_tensor(
                        msg[:, j, :].rearrange("p (h d) -> p h d", h=H),
                        agg[:, ds(i, 1), 0:D].rearrange("p a (h d) -> p (a h) d", h=H),
                        rec[:, ds(i, 1), :].rearrange("p a h -> p (a h)").unsqueeze(2)
                        .to_broadcast([P, H, D // H]), ALU.mult).then_inc(made, 1)
                for j in range(GT):
                    i = it * GT + j
                    dve.wait_ge(done, i + 1)
                    nc.vector.tensor_tensor(rowof(X, i), rowof(X, i), prod[:, j % 3, 0:D],
                                            ALU.add).then_inc(added, 1)

        @block.tensor
        def _(pe):
            pe.wait_ge(loaded, 16)
            with nc.tensor.Fori(0, NG) as it:
                for j in range(GT):
                    pe.wait_ge(made, it * GT + j + 1)
                    pe.wait_ge(copied, it * GT + j)
                    for h in range(2):
                        last = nc.tensor.transpose(pT[:, j, h * P:(h + 1) * P], msg[:, j, h * P:(h + 1) * P],
                                                   c["ident"][:])
                    last.then_inc(turned, 1)
                for j in range(GT):
                    pe.wait_ge(copied, it * GT + j + 1)
                    pe.wait_ge(added, it * GT + max(j - 2, 0))
                    for h in range(2):
                        last = nc.tensor.matmul(prod[:, j % 3, 0:D], mT[:, j, h, :], w[:, h, :],
                                                start=(h == 0), stop=(h == 1))
                    last.then_inc(done, 1)

        @block.scalar
        def _(act):
            with nc.scalar.Fori(0, NG) as it:
                for j in range(GT):
                    act.wait_ge(turned, it * GT + j + 1)
                    act.wait_ge(done, it * GT)
                    nc.scalar.copy(mT[:, j, :, :].rearrange("p h r -> p (h r)"), pT[:, j, 0:D]).then_inc(copied, 1)


class Products:

    def __init__(self, ph, jobs, g):
        self.nc, self.jobs = ph.nc, jobs
        self.hp = ph.ps("hp", [P, 4, 512])
        self.yp = [ph.ps("yp", [P, 512])[:, 0:D], g.pT[:, 2, 0:D]]
        self.filled, self.kept = ph.sem("filled"), ph.sem("kept")
        self.done, self.taken = ph.sem("done"), ph.sem("taken")
        self.nt = sum(j["kind"] == "T" for j in jobs)
        self.nr = len(jobs) - self.nt

    def multiply(self, pe, it, before=None):
        t = r = 0
        for job in self.jobs:
            if before:
                before(pe, it, job)
            if job["kind"] == "T":
                pe.wait_ge(self.kept, it * self.nt + max(t - 1, job.get("needs", 0), 0))
                m = job["rows"]
                for half in range(2):
                    out = self.hp[0:m, 2 * (t % 2) + half, 0:HR]
                    terms = job["terms"]
                    for k, (w, x) in enumerate(terms):
                        last = self.nc.tensor.matmul(out, w, x[:, half * HR:(half + 1) * HR],
                                                     start=(k == 0), stop=(k == len(terms) - 1))
                last.then_inc(self.filled, 1)
                t += 1
            else:
                pe.wait_ge(self.taken, it * self.nr + max(r - 1, 0))
                if job.get("needs", 0):
                    pe.wait_ge(self.kept, it * self.nt + job["needs"])
                terms = job["terms"]
                for k, (x, w) in enumerate(terms):
                    last = self.nc.tensor.matmul(self.yp[r % 2], x, w,
                                                 start=(k == 0), stop=(k == len(terms) - 1))
                last.then_inc(self.done, 1)
                r += 1

    def keep(self, act, it):
        t = 0
        for job in self.jobs:
            if job["kind"] == "T":
                act.wait_ge(self.filled, it * self.nt + t + 1)
                m = job["rows"]
                self.nc.scalar.activation(
                    job["out"].rearrange("p (a b) -> p a b", a=2),
                    self.hp[0:m, 2 * (t % 2):2 * (t % 2) + 2, 0:HR], job["func"],
                    bias=job["bias"], scale=job.get("scale", 1.0)).then_inc(self.kept, 1)
                t += 1

    def take(self, dve, it):
        r = 0
        for job in self.jobs:
            if job["kind"] == "R":
                dve.wait_ge(self.done, it * self.nr + r + 1)
                job["take"](it, self.yp[r % 2]).then_inc(self.taken, 1)
                r += 1


class Gate:

    def __init__(self, ph, c, g, experts, w, bias_row, extra=0):
        self.nc, self.c, self.g, self.n, self.w, self.bias_row = ph.nc, c, g, experts, w, bias_row
        self.lg = ph.sb("gate_lg", [P, GT, experts])
        self.mx = ph.sb("gate_mx", [P, GT])
        self.ex = ph.sb("gate_ex", [P, GT, experts])
        self.sm = ph.sb("gate_sm", [P, GT])
        self.rs = ph.sb("gate_rs", [P, GT])
        self.wt = ph.sb("gate_wt", [P, GT, experts + extra])
        self.wT = ph.sb("gate_wT", [experts + extra, GT, P])
        self.m = experts + extra
        self.logits, self.step = ph.sem("gate_logits"), ph.sem("gate_step")
        self.exped, self.gated = ph.sem("gate_exped"), ph.sem("gate_gated")
        self.turned, self.copied = ph.sem("gate_turned"), ph.sem("gate_copied")

    def bcast(self, t, n=None):
        return t[:].unsqueeze(2).to_broadcast([P, GT, n or self.n])

    def ask(self, pe, it, pr):
        pe.wait_ge(pr.taken, it * pr.nr)
        for j in range(GT):
            for h in range(2):
                last = self.nc.tensor.matmul(pr.yp[0][:, j * self.n:(j + 1) * self.n],
                                             self.g.xT[:, h, j * P:(j + 1) * P], self.w[:, h, :],
                                             start=(h == 0), stop=(h == 1))
        last.then_inc(self.logits, 1)
        pe.wait_ge(self.gated, it + 1)
        for j in range(GT):
            last = self.nc.tensor.transpose(self.g.pT[0:self.m, j // 4, (j % 4) * P:(j % 4 + 1) * P],
                                            self.wt[:, j, :], self.c["ident"][:])
        last.then_inc(self.turned, 1)
        pe.wait_ge(self.copied, it + 1)

    def copy(self, act, it):
        act.wait_ge(self.turned, it + 1)
        self.nc.scalar.copy(self.wT[:, 0:4, :].rearrange("e j r -> e (j r)"), self.g.pT[0:self.m, 0, :])
        self.nc.scalar.copy(self.wT[:, 4, :], self.g.pT[0:self.m, 1, 0:P]).then_inc(self.copied, 1)

    STEPS = 5

    def start(self, dve, it, pr, steps):
        nc, s = self.nc, self.step
        base = it * steps
        dve.wait_ge(self.logits, it + 1)
        nc.vector.tensor_tensor(self.lg[:], pr.yp[0][:, 0:GT * self.n].rearrange("p (j e) -> p j e", e=self.n),
                                self.bias_row[:].unsqueeze(1).to_broadcast([P, GT, self.n]), ALU.add).then_inc(s, 1)
        dve.wait_ge(s, base + 1)
        nc.vector.tensor_reduce(self.mx[:], self.lg[:], AXX, ALU.max).then_inc(s, 1)
        dve.wait_ge(s, base + 2)
        nc.vector.tensor_tensor(self.lg[:], self.lg[:], self.bcast(self.mx), ALU.subtract).then_inc(s, 1)
        dve.wait_ge(self.exped, it * (steps > 5) + it + 1)
        nc.vector.tensor_reduce(self.sm[:], self.ex[:], AXX, ALU.add).then_inc(s, 1)
        dve.wait_ge(s, base + 4)
        nc.vector.reciprocal(self.rs[:], self.sm[:]).then_inc(s, 1)
        dve.wait_ge(s, base + 5)

    def exp(self, act, it, steps):
        act.wait_ge(self.step, it * steps + 3)
        self.nc.scalar.activation(self.ex[:], self.lg[:], ACT.Exp).then_inc(self.exped, 1)


def batch_norm_terms(nc, c, name, io, keys, scale, shift):
    with Phase(nc, name) as ph:
        b, g, be, m, v = (ph.sb(k, list(scale.shape)) for k in ("b", "g", "be", "m", "v"))
        eps = ph.sb("eps", [P, 1])
        loaded, rooted, step, set_ = ph.sem("loaded"), ph.sem("rooted"), ph.sem("step"), ph.sem("set")
        block = ph.block()

        @block.sync
        def _(sp):
            for t, k in zip((b, g, be, m, v), keys):
                sp.dma_start(t[:], io[k]).then_inc(loaded, 16)

        @block.scalar
        def _(act):
            act.wait_ge(set_, 1)
            act.wait_ge(loaded, 80)
            nc.scalar.activation(v[:], v[:], ACT.Sqrt, bias=eps[:]).then_inc(rooted, 1)

        @block.vector
        def _(dve):
            nc.vector.memset(eps[:], BN_EPS).then_inc(set_, 1)
            dve.wait_ge(rooted, 1)
            nc.vector.reciprocal(scale[:], v[:])
            nc.vector.tensor_tensor(b[:], b[:], m[:], ALU.subtract).then_inc(step, 1)
            dve.wait_ge(step, 1)
            nc.vector.tensor_tensor(scale[:], scale[:], g[:], ALU.mult).then_inc(step, 1)
            dve.wait_ge(step, 2)
            nc.vector.tensor_tensor(b[:], b[:], scale[:], ALU.mult).then_inc(step, 1)
            dve.wait_ge(step, 3)
            nc.vector.tensor_tensor(shift[:], b[:], be[:], ALU.add)


def expert_layers(nc, c, io, X):
    NE, M = 8, 2
    with Phase(nc, "moe0") as outer:
        s1, t1, s2, t2 = (outer.sb(k, [P, NE * M]) for k in ("s1", "t1", "s2", "t2"))
        batch_norm_terms(nc, c, "bn1", io, ["F0b1", "F0g1", "F0be1", "F0m1", "F0v1"], s1, t1)
        batch_norm_terms(nc, c, "bn2", io, ["F0b2", "F0g2", "F0be2", "F0m2", "F0v2"], s2, t2)
        with Phase(nc, "moe0_") as ph:
            g = Group(ph, c, X)
            w1, w2, w3 = (ph.sb(k, [P, NE, 2, D]) for k in ("w1", "w2", "w3"))
            wr, br, bo = ph.sb("wr", [P, 2, NE]), ph.sb("br", [P, NE]), ph.sb("bo", [NE, D])
            h1, h2 = ph.sb("h1", [P, 2, M, GR]), ph.sb("h2", [P, 2, M, GR])
            gate = Gate(ph, c, g, NE, wr, br)
            loaded, chain = ph.sem("loaded"), ph.sem("chain")
            jobs = []
            order = [("first", 0)]
            for e in range(NE):
                order += [("first", e + 1)] * (e + 1 < NE) + [("second", e)] + [("out", e - 1)] * (e > 0)
            order += [("out", NE - 1)]

            def take_bias(j):
                return lambda it, y: nc.vector.tensor_tensor(rowof(X, it * GT + j), rowof(X, it * GT + j), y, ALU.add)

            def take_expert(j, e):
                def take(it, y):
                    nc.vector.wait_ge(pr.taken, it * (GT * (NE + 1)) + GT * e + j + 1)
                    return nc.vector.scalar_tensor_tensor(
                        rowof(X, it * GT + j), y, gate.wt[:, j, e:e + 1], rowof(X, it * GT + j), ALU.mult, ALU.add)
                return take

            for j in range(GT):
                jobs.append(dict(kind="R", terms=[(gate.wT[:, j, :], bo[:])], take=take_bias(j)))
            kept, t = {}, 0
            for what, e in order:
                if what == "out":
                    for j in range(GT):
                        jobs.append(dict(kind="R", needs=kept["second", e], take=take_expert(j, e), terms=[
                            (h2[:, e % 2, k, j * P:(j + 1) * P], w3[:, e, k, :]) for k in range(M)]))
                    continue
                w, x, h, s, b = (w1, g.xT, h1, s1, t1) if what == "first" else (w2, h1, h2, s2, t2)
                for m in range(M):
                    jobs.append(dict(
                        kind="T", rows=P, func=ACT.Relu, out=h[:, e % 2, m, :],
                        needs=kept["first", e] if what == "second" else 0,
                        scale=s[:, e * M + m:e * M + m + 1], bias=b[:, e * M + m:e * M + m + 1],
                        terms=[(w[:, e, k, m * P:(m + 1) * P],
                                g.xT[:, k, :] if what == "first" else h1[:, e % 2, k, :]) for k in range(2)]))
                    t += 1
                kept[what, e] = t
            pr = Products(ph, jobs, g)
            block = ph.block()

            @block.sync
            def _(sp):
                for t, k in ((w1, "F0W1"), (w2, "F0W2"), (w3, "F0W3")):
                    sp.dma_start(t[:].rearrange("p e k n -> p (e k) n"),
                                 io[k].rearrange("e (k p) n -> p (e k) n", p=P)).then_inc(loaded, 16)
                sp.dma_start(wr[:], io["F0Wr"].rearrange("(k p) n -> p k n", p=P)).then_inc(loaded, 16)
                sp.dma_start(br[:], io["F0br"].partition_broadcast(P)).then_inc(loaded, 16)
                sp.dma_start(bo[:], io["F0bo"]).then_inc(loaded, 16)

            @block.vector
            def _(dve):
                dve.wait_ge(loaded, 96)
                with nc.vector.Fori(0, NG) as it:
                    g.normalise(dve, it)
                    gate.start(dve, it, pr, Gate.STEPS)
                    nc.vector.tensor_tensor(gate.wt[:], gate.ex[:], gate.bcast(gate.rs), ALU.mult
                                            ).then_inc(gate.gated, 1)
                    dve.wait_ge(gate.gated, it + 1)
                    pr.take(dve, it)

            @block.scalar
            def _(act):
                with nc.scalar.Fori(0, NG) as it:
                    g.copy(act, it)
                    gate.exp(act, it, Gate.STEPS)
                    gate.copy(act, it)
                    pr.keep(act, it)

            @block.tensor
            def _(pe):
                pe.wait_ge(loaded, 96)
                with nc.tensor.Fori(0, NG) as it:
                    pe.wait_ge(pr.taken, it * pr.nr)
                    g.turn(pe, it)
                    pe.wait_ge(g.ready, it + 1)
                    gate.ask(pe, it, pr)
                    pr.multiply(pe, it)
                    pe.wait_ge(pr.done, (it + 1) * pr.nr)
                    pe.sem_inc(g.used, 1)


def aggregate(nc, c, name, slots, table, blocks, agg, weighted):
    R = 4
    with Phase(nc, name) as ph:
        slot = ph.sb("slot", [P, ST + R * U, PW])
        hot = ph.sb("hot", [P, R, U, P])
        idx = ph.sb("idx", [P, R, U], I32)
        row = ph.sb("row", [P, R, U, D])
        out = [ph.ps(f"out{u}", [P, U // RUN, 512]) for u in range(2)]
        loaded, cleared, released = ph.sem("loaded"), ph.sem("cleared"), ph.sem("released")
        picked, gathered = ph.sems("picked", R), ph.gather_sems(R)
        made, summed, added = ph.sems("made", R), ph.sems("summed", R), ph.sem("added")
        block = ph.block()

        @block.sync
        def _(sp):
            sp.dma_start(slot[:, 0:ST, :], slots.rearrange("(p t) w -> p t w", t=ST)).then_inc(loaded, 16)

        @block.scalar
        def _(act):
            def pick(n, u):
                nc.scalar.copy(idx[:, u, :].bitcast(U32), slot[:, ds((n * R + u) * U, U), OTHER].bitcast(U32)
                               ).then_inc(picked[u], 1)

            act.wait_ge(loaded, 16)
            act.wait_ge(cleared, 2)
            for u in range(R):
                pick(0, u)
            with nc.scalar.Fori(0, NU // R) as it:
                for u in range(R):
                    act.wait_ge(gathered[u], (it + 1) * (16 * U))
                    pick(it + 1, u)

        @block.gpsimd
        def _(pool):
            with nc.gpsimd.Fori(0, NU // R) as it:
                for u in range(R):
                    pool.wait_ge(picked[u], it + 1)
                    pool.wait_ge(summed[u], it)
                    pool.sem_inc(released, 1)
                    for j in range(U):
                        pool.indirect_dma_start(
                            out=row[:, u, j, :], out_offset=None, in_=table,
                            in_offset=bass.IndirectOffsetOnAxis(ap=idx[:, u, j:j + 1].bitcast(U32), axis=0)
                        ).then_inc(gathered[u], 16)

        @block.vector
        def _(dve):
            def make(n, u):
                dve.wait_ge(summed[u], n)
                for j in range(U):
                    t = (n * R + u) * U + j
                    last = nc.vector.tensor_scalar(
                        hot[:, u, j, :], c["iota"][:, 0:P], slot[:, ds(t, 1), LO],
                        slot[:, ds(t, 1), WGT] if weighted else None, ALU.is_equal,
                        ALU.mult if weighted else ALU.bypass)
                last.then_inc(made[u], 1)

            def add(n, u):
                nb = load_blocks(nc.vector, blocks, n * R + u)
                dve.wait_ge(summed[u], n + 1)
                for r in range(U // RUN):
                    dve.wait_ge(added, (n * R + u) * (U // RUN) + r)
                    nc.vector.tensor_tensor(agg[:, ds(nb[r], 1), 0:D].rearrange("p a b -> p (a b)"),
                                            agg[:, ds(nb[r], 1), 0:D].rearrange("p a b -> p (a b)"),
                                            out[u % 2][:, r, 0:D], ALU.add).then_inc(added, 1)

            nc.vector.memset(agg[:], 0.0).then_inc(cleared, 1)
            nc.vector.memset(slot[:, ST:, :], 0.0).then_inc(cleared, 1)
            dve.wait_ge(loaded, 16)
            dve.wait_ge(cleared, 2)
            make(0, 0)
            with nc.vector.Fori(0, NU // R - 1) as it:
                for u in range(R):
                    make(it + (u + 1) // R, (u + 1) % R)
                    add(it, u)
            for u in range(R):
                if u + 1 < R:
                    make(NU // R - 1, u + 1)
                add(NU // R - 1, u)

        @block.tensor
        def _(pe):
            with nc.tensor.Fori(0, NU // R) as it:
                for u in range(R):
                    pe.wait_ge(made[u], it + 1)
                    pe.wait_ge(gathered[u], (it + 1) * (16 * U))
                    pe.wait_ge(added, (it * R + max(u - 1, 0)) * (U // RUN))
                    for j in range(U):
                        last = nc.tensor.matmul(out[u % 2][:, j // RUN, 0:D], hot[:, u, j, :], row[:, u, j, :],
                                                start=(j % RUN == 0), stop=(j % RUN == RUN - 1))
                    last.then_inc(summed[u], 1)


def store_normalised(nc, c, name, X, table):
    with Phase(nc, name) as ph:
        xn = ph.sb("xn", [P, GT, D])
        normed, stored = ph.sem("normed"), ph.sems("stored", GT)
        block = ph.block()

        @block.vector
        def _(dve):
            with nc.vector.Fori(0, NG) as it:
                for j in range(GT):
                    i = it * GT + j
                    dve.wait_ge(stored[j], it * 16)
                    nc.vector.tensor_scalar(xn[:, j, :], rowof(X, i), c["mean"][:, ds(i, 1)],
                                            c["rstd"][:, ds(i, 1)], ALU.subtract, ALU.mult).then_inc(normed, 1)

        @block.sync
        def _(sp):
            with nc.sync.Fori(0, NG) as it:
                for j in range(GT):
                    i = it * GT + j
                    sp.wait_ge(normed, i + 1)
                    sp.dma_start(table[ds(i * P, P), :], xn[:, j, :]).then_inc(stored[j], 16)
            for j in range(GT):
                sp.wait_ge(stored[j], 16 * NG)


def sage_layers(nc, c, io, X, agg, degree, inv_deg, z_table):
    M = 4
    with Phase(nc, "sage") as ph:
        g = Group(ph, c, X)
        m = Group(ph, c, agg, "m", pT=g.pT, scale=inv_deg, ahead=g)
        w1, w2 = ph.sb("w1", [P, 4, M * P]), ph.sb("w2", [P, M, 2 * D])
        b1, b2 = ph.sb("b1", [P, M]), ph.sb("b2", [P, D])
        h = ph.sb("h", [P, M, GR])
        z = ph.sb("z", [P, GT, D])
        loaded, stored, clipped = ph.sem("loaded"), ph.sems("stored", GT), ph.sem("clipped")
        biased = ph.sem("biased")
        jobs = []
        for n in range(M):
            jobs.append(dict(kind="T", rows=P, func=ACT.Relu, out=h[:, n, :], bias=b1[:, n:n + 1], terms=[
                (w1[:, k, n * P:(n + 1) * P], (m, g)[k // 2].xT[:, k % 2, :]) for k in range(4)]))

        def take_z(j):
            def take(it, y):
                nc.vector.wait_ge(stored[j], it * 16)
                return nc.vector.tensor_copy(z[:, j, :], y)
            return take

        def take_x(j):
            def take(it, y):
                nc.vector.wait_ge(biased, it * GT + j + 1)
                return nc.vector.tensor_tensor(rowof(X, it * GT + j), rowof(X, it * GT + j), y, ALU.add)
            return take

        for j in range(GT):
            for n, take in enumerate((take_z(j), take_x(j))):
                jobs.append(dict(kind="R", needs=M, take=take, terms=[
                    (h[:, k, j * P:(j + 1) * P], w2[:, k, n * D:(n + 1) * D]) for k in range(M)]))
        pr = Products(ph, jobs, g)
        block = ph.block()

        @block.sync
        def _(sp):
            sp.dma_start(w1[:], io["S1W1"].rearrange("(k p) n -> p k n", p=P)).then_inc(loaded, 16)
            sp.dma_start(w2[:], io["S1W2"].rearrange("(k p) n -> p k n", p=P)).then_inc(loaded, 16)
            sp.dma_start(b1[:], io["S1b1"]).then_inc(loaded, 16)
            sp.dma_start(b2[:], io["S1b2"].partition_broadcast(P)).then_inc(loaded, 16)
            with nc.sync.Fori(0, NG) as it:
                for j in range(GT):
                    sp.wait_ge(pr.taken, it * pr.nr + 2 * j + 1)
                    sp.dma_start(z_table[ds((it * GT + j) * P, P), :], z[:, j, :]).then_inc(stored[j], 16)
            for j in range(GT):
                sp.wait_ge(stored[j], 16 * NG)

        @block.vector
        def _(dve):
            dve.wait_ge(loaded, 64)
            nc.vector.tensor_scalar(inv_deg[:], degree[:], 1.0, None, ALU.max).then_inc(clipped, 1)
            dve.wait_ge(clipped, 1)
            nc.vector.reciprocal(inv_deg[:], inv_deg[:]).then_inc(clipped, 1)
            dve.wait_ge(clipped, 2)
            with nc.vector.Fori(0, NG) as it:
                g.normalise(dve, it)
                m.normalise(dve, it)
                dve.wait_ge(g.normed, it + 1)
                for j in range(GT):
                    nc.vector.tensor_tensor(rowof(X, it * GT + j), rowof(X, it * GT + j), b2[:], ALU.add
                                            ).then_inc(biased, 1)
                pr.take(dve, it)

        @block.scalar
        def _(act):
            with nc.scalar.Fori(0, NG) as it:
                g.copy(act, it)
                m.copy(act, it)
                pr.keep(act, it)

        @block.tensor
        def _(pe):
            pe.wait_ge(loaded, 64)
            with nc.tensor.Fori(0, NG) as it:
                pe.wait_ge(pr.taken, it * pr.nr)
                g.turn(pe, it)
                m.turn(pe, it)
                pe.wait_ge(m.ready, it + 1)
                pr.multiply(pe, it)
                pe.wait_ge(pr.done, (it + 1) * pr.nr)
                pe.sem_inc(g.used, 1)
                pe.sem_inc(m.used, 1)


def add_scaled(nc, name, X, agg, scale):
    with Phase(nc, name) as ph:
        block = ph.block()

        @block.vector
        def _(dve):
            with nc.vector.Fori(0, NT) as i:
                nc.vector.scalar_tensor_tensor(rowof(X, i), agg[:, ds(i, 1), 0:D].rearrange("p a b -> p (a b)"),
                                               scale[:, ds(i, 1)], rowof(X, i), ALU.mult, ALU.add)


def choose_tokens(nc, c, io, X, row_dram, chosen):
    TOP = int(0.5 * N) - 1
    LAST = N - (NT - 1) * P
    with Phase(nc, "choose") as ph:
        wr, br = ph.sb("wr", [P, D]), ph.sb("br", [P, 1])
        xn, prod = ph.sb("xn", [P, NT, D]), ph.sb("prod", [P, NT, D])
        rw = ph.sb("rw", [P, NT])
        pad = ph.sb("pad", [P, 1])
        rows = ph.sb("rows", [NT, P])
        every = ph.sb("every", [P, NP])
        junk = ph.sb("junk", [P, 4, NP], BF16)
        part = ph.sb("part", [P, NT, 4])
        rank = ph.sb("rank", [P, NT])
        pt = ph.ps("pt", [NT, P])
        loaded, normed, dotted, step = ph.sem("loaded"), ph.sem("normed"), ph.sem("dotted"), ph.sem("step")
        turned, copied, stored, back = ph.sem("turned"), ph.sem("copied"), ph.sem("stored"), ph.sem("back")
        counted = ph.sem("counted")
        block = ph.block()

        @block.sync
        def _(sp):
            sp.dma_start(wr[:], io["C1wr"].partition_broadcast(P)).then_inc(loaded, 16)
            sp.dma_start(br[:], io["C1br"].partition_broadcast(P)).then_inc(loaded, 16)
            sp.wait_ge(copied, 1)
            sp.dma_start(row_dram.rearrange("(t r) -> t r", r=P), rows[:]).then_inc(stored, 16)
            sp.wait_ge(stored, 16)
            sp.dma_start(every[:], row_dram.partition_broadcast(P)).then_inc(back, 16)

        @block.vector
        def _(dve):
            nc.vector.memset(part[:], 0.0)
            dve.wait_ge(loaded, 32)
            with nc.vector.Fori(0, NT) as i:
                nc.vector.tensor_scalar(rowof(xn, i), rowof(X, i), c["mean"][:, ds(i, 1)],
                                        c["rstd"][:, ds(i, 1)], ALU.subtract, ALU.mult).then_inc(normed, 1)
            dve.wait_ge(normed, NT)
            with nc.vector.Fori(0, NG) as it:
                nc.vector.tensor_tensor(prod[:, ds(it * GT, GT), :], xn[:, ds(it * GT, GT), :],
                                        wr[:].unsqueeze(1).to_broadcast([P, GT, D]), ALU.mult).then_inc(dotted, 1)
            dve.wait_ge(dotted, NG)
            nc.vector.tensor_reduce(rw[:], prod[:], AXX, ALU.add).then_inc(step, 1)
            nc.vector.tensor_scalar(pad[:], c["iota_p"][:], float(LAST), -BIG, ALU.is_ge, ALU.mult
                                    ).then_inc(step, 1)
            dve.wait_ge(step, 2)
            nc.vector.tensor_scalar(rw[:], rw[:], br[:], None, ALU.add).then_inc(step, 1)
            dve.wait_ge(step, 3)
            nc.vector.tensor_tensor(rw[:, NT - 1:NT], rw[:, NT - 1:NT], pad[:], ALU.add).then_inc(step, 1)
            dve.wait_ge(back, 16)
            for t in range(NT):
                w = rw[:, t:t + 1]
                own = slice(t * P, (t + 1) * P)
                if t:
                    dve.wait_ge(counted, t)
                if t:
                    nc.vector.tensor_scalar(junk[:, 0, 0:t * P], every[:, 0:t * P], w, 0.0, ALU.is_ge, ALU.add,
                                            accum_out=part[:, t, 0:1])
                nc.vector.tensor_scalar(junk[:, 1, 0:NP - t * P], every[:, t * P:], w, 0.0, ALU.is_gt, ALU.add,
                                        accum_out=part[:, t, 1:2])
                nc.vector.scalar_tensor_tensor(junk[:, 2, 0:P], every[:, own], w, c["before_col"][:],
                                               ALU.is_equal, ALU.mult, accum_out=part[:, t, 2:3]
                                               ).then_inc(counted, 1)
            dve.wait_ge(counted, NT)
            nc.vector.tensor_reduce(rank[:], part[:], AXX, ALU.add).then_inc(step, 1)
            dve.wait_ge(step, 5)
            nc.vector.scalar_tensor_tensor(chosen[:], rank[:], TOP - 0.5, rw[:], ALU.is_lt, ALU.mult)

        @block.tensor
        def _(pe):
            pe.wait_ge(step, 4)
            nc.tensor.transpose(pt[:], rw[:], c["ident"][:]).then_inc(turned, 1)

        @block.scalar
        def _(act):
            act.wait_ge(turned, 1)
            nc.scalar.copy(rows[:], pt[:]).then_inc(copied, 1)


def chosen_ffn(nc, c, io, X, chosen):
    M = 8
    with Phase(nc, "ffn1") as ph:
        g = Group(ph, c, X)
        w1, w2 = ph.sb("w1", [P, 2, M * P]), ph.sb("w2", [P, M, D])
        b1, b2 = ph.sb("b1", [P, M]), ph.sb("b2", [P, D])
        h = ph.sb("h", [P, M, GR])
        y1, y2 = ph.sb("y1", [P, GT, D]), ph.sb("y2", [P, GT, D])
        loaded, chain = ph.sem("loaded"), ph.sem("chain")
        jobs = []
        for n in range(M):
            jobs.append(dict(kind="T", rows=P, func=ACT.Gelu_apprx_tanh, out=h[:, n, :], bias=b1[:, n:n + 1],
                             terms=[(w1[:, k, n * P:(n + 1) * P], g.xT[:, k, :]) for k in range(2)]))

        def take_x(j):
            return lambda it, y: nc.vector.tensor_tensor(y1[:, j, :], y, b2[:], ALU.add)

        for j in range(GT):
            jobs.append(dict(kind="R", needs=M, take=take_x(j), terms=[
                (h[:, k, j * P:(j + 1) * P], w2[:, k, :]) for k in range(M)]))
        pr = Products(ph, jobs, g)
        block = ph.block()

        @block.sync
        def _(sp):
            sp.dma_start(w1[:], io["C1W1"].rearrange("(k p) n -> p k n", p=P)).then_inc(loaded, 16)
            sp.dma_start(w2[:], io["C1W2"].rearrange("(k p) n -> p k n", p=P)).then_inc(loaded, 16)
            sp.dma_start(b1[:], io["C1b1"]).then_inc(loaded, 16)
            sp.dma_start(b2[:], io["C1b2"].partition_broadcast(P)).then_inc(loaded, 16)

        @block.vector
        def _(dve):
            dve.wait_ge(loaded, 64)
            with nc.vector.Fori(0, NG) as it:
                g.normalise(dve, it)
                pr.take(dve, it)
                dve.wait_ge(pr.taken, (it + 1) * pr.nr)
                for j in range(GT):
                    nc.vector.scalar_tensor_tensor(y2[:, j, :], y1[:, j, :], chosen[:, ds(it * GT + j, 1)],
                                                   g.xn[:, j, :], ALU.mult, ALU.add).then_inc(chain, 1)
                dve.wait_ge(chain, (it + 1) * GT)
                nc.vector.tensor_tensor(X[:, ds(it * GT, GT), :], X[:, ds(it * GT, GT), :], y2[:], ALU.add)

        @block.scalar
        def _(act):
            with nc.scalar.Fori(0, NG) as it:
                g.copy(act, it)
                pr.keep(act, it)

        @block.tensor
        def _(pe):
            pe.wait_ge(loaded, 64)
            with nc.tensor.Fori(0, NG) as it:
                pe.wait_ge(pr.taken, it * pr.nr)
                g.turn(pe, it)
                pe.wait_ge(g.ready, it + 1)
                pr.multiply(pe, it)
                pe.wait_ge(pr.done, (it + 1) * pr.nr)
                pe.sem_inc(g.used, 1)


def mixture_ffn(nc, c, io, X):
    NE, K = 4, 2
    EH = 64
    STEPS = 14
    with Phase(nc, "moe2") as ph:
        g = Group(ph, c, X)
        sw1, sw2, sw3 = ph.sb("sw1", [P, 2, 2 * P]), ph.sb("sw2", [P, 2, P]), ph.sb("sw3", [P, D])
        ew1, ew2, ew3 = ph.sb("ew1", [P, NE, 2, P]), ph.sb("ew2", [P, NE, EH]), ph.sb("ew3", [EH, NE, D])
        bias = ph.sb("bias", [P, 3 + NE])
        eb2 = ph.sb("eb2", [EH, NE])
        b3 = ph.sb("b3", [NE + 1, D])
        gw, gb = ph.sb("gw", [P, 2, NE]), ph.sb("gb", [P, NE])
        sh1, sh2 = ph.sb("sh1", [P, 2, GR]), ph.sb("sh2", [P, GR])
        eh1, eh2 = ph.sb("eh1", [P, NE, GR]), ph.sb("eh2", [EH, NE, GR])
        gate = Gate(ph, c, g, NE, gw, gb, extra=1)
        lower, upper = ph.sb("lower", [P, NE, NE]), ph.sb("upper", [P, NE, NE])
        ge, gt = ph.sb("ge", [P, GT, NE, NE]), ph.sb("gt", [P, GT, NE, NE])
        prob = ph.sb("prob", [P, GT, NE])
        sel = ph.sb("sel", [P, GT, NE])
        loaded, masked = ph.sem("loaded"), ph.sem("masked")
        jobs = []

        def T(w, x, out, func, b, needs, rows=P):
            jobs.append(dict(kind="T", rows=rows, func=func, out=out, bias=b, needs=needs,
                             terms=list(zip(w, x))))

        for n in range(2):
            T([sw1[:, k, n * P:(n + 1) * P] for k in range(2)], [g.xT[:, k, :] for k in range(2)],
              sh1[:, n, :], ACT.Relu, bias[:, n:n + 1], 0)
        for e in range(NE):
            T([ew1[:, e, k, :] for k in range(2)], [g.xT[:, k, :] for k in range(2)],
              eh1[:, e, :], ACT.Relu, bias[:, 3 + e:4 + e], 0)
        T([sw2[:, k, :] for k in range(2)], [sh1[:, k, :] for k in range(2)], sh2[:], ACT.Relu, bias[:, 2:3], 2)
        for e in range(NE):
            T([ew2[:, e, :]], [eh1[:, e, :]], eh2[:, e, :], ACT.Relu, eb2[:, e:e + 1], 3 + e, rows=EH)

        def take(j, e):
            def f(it, y):
                i = it * GT + j
                if e < 0:
                    return nc.vector.tensor_tensor(rowof(X, i), rowof(X, i), y, ALU.add)
                nc.vector.wait_ge(pr.taken, it * pr.nr + GT * (e + 1) + j + 1 - GT)
                return nc.vector.scalar_tensor_tensor(rowof(X, i), y, gate.wt[:, j, e:e + 1], rowof(X, i),
                                                      ALU.mult, ALU.add)
            return f

        for j in range(GT):
            jobs.append(dict(kind="R", needs=7, take=take(j, -1), terms=[
                (gate.wT[:, j, :], b3[:]), (sh2[:, j * P:(j + 1) * P], sw3[:])]))
        for e in range(NE):
            for j in range(GT):
                jobs.append(dict(kind="R", needs=8 + e, take=take(j, e), terms=[
                    (eh2[:, e, j * P:(j + 1) * P], ew3[:, e, :])]))
        pr = Products(ph, jobs, g)
        block = ph.block()

        @block.sync
        def _(sp):
            sp.dma_start(sw1[:], io["M2sW1"].rearrange("(k p) n -> p k n", p=P)).then_inc(loaded, 16)
            sp.dma_start(sw2[:], io["M2sW2"].rearrange("(k p) n -> p k n", p=P)).then_inc(loaded, 16)
            sp.dma_start(sw3[:], io["M2sW3"]).then_inc(loaded, 16)
            sp.dma_start(ew1[:].rearrange("p e k n -> p (e k) n"),
                         io["M2eW1"].rearrange("e (k p) n -> p (e k) n", p=P)).then_inc(loaded, 16)
            sp.dma_start(ew2[:], io["M2eW2"].rearrange("e p n -> p e n")).then_inc(loaded, 16)
            sp.dma_start(ew3[:], io["M2eW3"].rearrange("e p n -> p e n")).then_inc(loaded, 16)
            sp.dma_start(bias[:], io["M2b"]).then_inc(loaded, 16)
            sp.dma_start(eb2[:], io["M2eb2"]).then_inc(loaded, 16)
            sp.dma_start(b3[:], io["M2b3"]).then_inc(loaded, 16)
            sp.dma_start(gw[:], io["M2gW"].rearrange("(k p) n -> p k n", p=P)).then_inc(loaded, 16)
            sp.dma_start(gb[:], io["M2gb"].partition_broadcast(P)).then_inc(loaded, 16)

        @block.gpsimd
        def _(pool):
            pat = c["ones"][:, 0:NE * NE].rearrange("p (a b) -> p a b", b=NE)
            nc.gpsimd.affine_select(out=lower[:], in_=pat, compare_op=ALU.is_gt, fill=0.0, base=0,
                                    pattern=[[1, NE], [-1, NE]], channel_multiplier=0).then_inc(masked, 1)
            nc.gpsimd.affine_select(out=upper[:], in_=pat, compare_op=ALU.is_gt, fill=0.0, base=0,
                                    pattern=[[-1, NE], [1, NE]], channel_multiplier=0).then_inc(masked, 1)

        @block.vector
        def _(dve):
            dve.wait_ge(loaded, 16 * 11)
            dve.wait_ge(masked, 2)
            nc.vector.memset(gate.wt[:], 1.0)
            s, V = gate.step, nc.vector
            shape = [P, GT, NE, NE]
            with nc.vector.Fori(0, NG) as it:
                g.normalise(dve, it)
                gate.start(dve, it, pr, STEPS)
                base = it * STEPS
                V.tensor_tensor(prob[:], gate.ex[:], gate.bcast(gate.rs), ALU.mult).then_inc(s, 1)
                dve.wait_ge(s, base + 6)
                mine = prob[:].unsqueeze(3).to_broadcast(shape)
                theirs = prob[:].unsqueeze(2).to_broadcast(shape)
                V.tensor_tensor(ge[:], theirs, mine, ALU.is_ge)
                V.tensor_tensor(gt[:], theirs, mine, ALU.is_gt)
                V.tensor_reduce(gate.mx[:], prob[:], AXX, ALU.max).then_inc(s, 1)
                dve.wait_ge(s, base + 7)
                V.tensor_tensor(ge[:], ge[:], lower[:].unsqueeze(1).to_broadcast(shape), ALU.mult)
                V.tensor_tensor(gt[:], gt[:], upper[:].unsqueeze(1).to_broadcast(shape), ALU.mult)
                V.tensor_tensor(gate.lg[:], prob[:], gate.bcast(gate.mx), ALU.subtract).then_inc(s, 1)
                dve.wait_ge(s, base + 8)
                V.tensor_tensor(ge[:], ge[:], gt[:], ALU.add).then_inc(s, 1)
                dve.wait_ge(s, base + 9)
                V.tensor_reduce(sel[:], ge[:], AXX, ALU.add).then_inc(s, 1)
                dve.wait_ge(s, base + 10)
                dve.wait_ge(gate.exped, it * 2 + 2)
                V.scalar_tensor_tensor(sel[:], sel[:], K - 0.5, gate.ex[:], ALU.is_lt, ALU.mult).then_inc(s, 1)
                dve.wait_ge(s, base + 11)
                V.tensor_reduce(gate.sm[:], sel[:], AXX, ALU.add).then_inc(s, 1)
                dve.wait_ge(s, base + 12)
                V.reciprocal(gate.rs[:], gate.sm[:]).then_inc(s, 1)
                dve.wait_ge(s, base + 13)
                V.tensor_tensor(gate.wt[:, :, 0:NE], sel[:], gate.bcast(gate.rs), ALU.mult
                                ).then_inc(gate.gated, 1)
                V.sem_inc(s, 1)
                dve.wait_ge(gate.gated, it + 1)
                pr.take(dve, it)

        @block.scalar
        def _(act):
            with nc.scalar.Fori(0, NG) as it:
                g.copy(act, it)
                gate.exp(act, it, STEPS)
                act.wait_ge(gate.step, it * STEPS + 8)
                nc.scalar.activation(gate.ex[:], gate.lg[:], ACT.Exp).then_inc(gate.exped, 1)
                gate.copy(act, it)
                pr.keep(act, it)

        @block.tensor
        def _(pe):
            pe.wait_ge(loaded, 16 * 11)
            with nc.tensor.Fori(0, NG) as it:
                pe.wait_ge(pr.taken, it * pr.nr)
                g.turn(pe, it)
                pe.wait_ge(g.ready, it + 1)
                gate.ask(pe, it, pr)
                pr.multiply(pe, it)
                pe.wait_ge(pr.done, (it + 1) * pr.nr)
                pe.sem_inc(g.used, 1)


def row_product(nc, c, io, name, X, weight, take_to_dram=None, bias=None):
    with Phase(nc, name) as ph:
        g = Group(ph, c, X)
        w, b = ph.sb("w", [P, 2, D]), ph.sb("b", [P, D])
        z = ph.sb("z", [P, GT, D])
        loaded, stored, biased = ph.sem("loaded"), ph.sems("stored", GT), ph.sem("biased")

        def take(j):
            def f(it, y):
                if take_to_dram is None:
                    nc.vector.wait_ge(biased, it * GT + j + 1)
                    return nc.vector.tensor_tensor(rowof(X, it * GT + j), rowof(X, it * GT + j), y, ALU.add)
                nc.vector.wait_ge(stored[j], it * 16)
                return nc.vector.tensor_copy(z[:, j, :], y)
            return f

        pr = Products(ph, [dict(kind="R", take=take(j), terms=[
            (g.xT[:, k, j * P:(j + 1) * P], w[:, k, :]) for k in range(2)]) for j in range(GT)], g)
        block = ph.block()

        @block.sync
        def _(sp):
            sp.dma_start(w[:], io[weight].rearrange("(k p) n -> p k n", p=P)).then_inc(loaded, 16)
            sp.dma_start(b[:], io[bias or weight].rearrange("n -> n").partition_broadcast(P) if bias else
                         io[weight][0:P, :]).then_inc(loaded, 16)
            if take_to_dram is not None:
                with nc.sync.Fori(0, NG) as it:
                    for j in range(GT):
                        sp.wait_ge(pr.taken, it * GT + j + 1)
                        sp.dma_start(take_to_dram[ds((it * GT + j) * P, P), :], z[:, j, :]).then_inc(stored[j], 16)
                for j in range(GT):
                    sp.wait_ge(stored[j], 16 * NG)

        @block.vector
        def _(dve):
            dve.wait_ge(loaded, 32)
            with nc.vector.Fori(0, NG) as it:
                g.normalise(dve, it)
                if take_to_dram is None:
                    dve.wait_ge(g.normed, it + 1)
                    for j in range(GT):
                        nc.vector.tensor_tensor(rowof(X, it * GT + j), rowof(X, it * GT + j), b[:], ALU.add
                                                ).then_inc(biased, 1)
                pr.take(dve, it)

        @block.scalar
        def _(act):
            with nc.scalar.Fori(0, NG) as it:
                g.copy(act, it)

        @block.tensor
        def _(pe):
            pe.wait_ge(loaded, 32)
            with nc.tensor.Fori(0, NG) as it:
                pe.wait_ge(pr.taken, it * pr.nr)
                g.turn(pe, it)
                pe.wait_ge(g.ready, it + 1)
                pr.multiply(pe, it)
                pe.wait_ge(pr.done, (it + 1) * pr.nr)
                pe.sem_inc(g.used, 1)


def add_relu(nc, name, X, agg):
    with Phase(nc, name) as ph:
        block = ph.block()

        @block.vector
        def _(dve):
            with nc.vector.Fori(0, NT) as i:
                nc.vector.scalar_tensor_tensor(rowof(X, i), agg[:, ds(i, 1), 0:D].rearrange("p a b -> p (a b)"),
                                               0.0, rowof(X, i), ALU.max, ALU.add)


TY = 19
TT = 45
TG = TT // GT
PROJ, TD, H2 = 192, 32, 4
DK = (PROJ + TD) // H2
KVQ = 2 * PROJ + DK
assert NP + TY * (P - 1) < (TT + 1) * P
TWO_PI = 6.283185307179586
ROUND = 12582912.0


def sort_nodes(nc, c, io, X, pos_i, type_i, xs):
    with Phase(nc, "nodes") as ph:
        ty_i, ty = ph.sb("ty_i", [P, NT], I32), ph.sb("ty", [P, NT])
        hot, incl, tmp = ph.sb("hot", [P, TY, NT]), ph.sb("incl", [P, TY, NT]), ph.sb("tmp", [P, TY, NT])
        tot, run = ph.sb("tot", [P, TY, NT]), ph.sb("run", [P, TY, NT])
        keep = ph.sb("keep", [P, TY, NT])
        num, num_i = ph.sb("num", [P, 6, TY]), ph.sb("num_i", [P, 2, TY], I32)
        pos, tt = ph.sb("pos", [P, NT]), ph.sb("tt", [P, TT])
        past = ph.sb("past", [P, TT, TY])
        zero = ph.sb("zero", [P, D])
        xn = ph.sb("xn", [P, GT, D])
        zrow = ph.sem("zrow")
        loaded, step, pe_done, filled = ph.sem("loaded"), ph.sem("step"), ph.sem("pe_done"), ph.sem("filled")
        placed, normed, released = ph.sem("placed"), ph.sem("normed"), ph.sem("released")
        sent = ph.gather_sems(GT)
        ranks, totals = ph.ps("ranks", [P, TY * NT]), ph.ps("totals", [P, TY * NT])
        block = ph.block()

        @block.sync
        def _(sp):
            sp.dma_start(ty_i[:], io["T2type"]).then_inc(loaded, 16)
            sp.wait_ge(zrow, 1)
            sp.dma_start(xs.rearrange("(t p) d -> p t d", p=P), zero[:].unsqueeze(1).to_broadcast([P, TT, D])
                         ).then_inc(filled, 16)

        @block.vector
        def _(dve):
            V = nc.vector
            V.memset(zero[:], 0.0).then_inc(zrow, 1)
            V.memset(keep[:], 1.0).then_inc(zrow, 1)
            dve.wait_ge(zrow, 2)
            V.memset(keep[:, :, 0:1], 0.0)
            dve.wait_ge(loaded, 16)
            V.tensor_copy(ty[:], ty_i[:]).then_inc(step, 1)
            dve.wait_ge(step, 1)
            V.tensor_tensor(hot[:], c["iota"][:, 0:TY].unsqueeze(2).to_broadcast([P, TY, NT]),
                            ty[:].unsqueeze(1).to_broadcast([P, TY, NT]), ALU.is_equal).then_inc(step, 1)
            dve.wait_ge(pe_done, 2)
            V.tensor_copy(tot[:].rearrange("p a b -> p (a b)"), totals[:]).then_inc(step, 1)
            dve.wait_ge(step, 3)
            V.tensor_tensor_scan(run[:].rearrange("p a b -> p (a b)"), keep[:].rearrange("p a b -> p (a b)"),
                                 tot[:].rearrange("p a b -> p (a b)"), 0.0, ALU.mult, ALU.add).then_inc(step, 1)
            dve.wait_ge(step, 4)
            V.tensor_scalar(num[:, 0, :], run[:, :, NT - 1], float(P - 1), None, ALU.add)
            V.tensor_tensor(tmp[:], run[:], tot[:], ALU.subtract).then_inc(step, 1)
            dve.wait_ge(step, 5)
            V.tensor_copy(num_i[:, 0, :], num[:, 0, :])
            V.tensor_tensor(incl[:].rearrange("p a b -> p (a b)"), tmp[:].rearrange("p a b -> p (a b)"),
                            ranks[:], ALU.add).then_inc(step, 1)
            dve.wait_ge(step, 6)
            V.tensor_scalar(num_i[:, 1, :], num_i[:, 0, :], 7, None, ALU.logical_shift_right).then_inc(step, 1)
            dve.wait_ge(step, 7)
            V.tensor_copy(num[:, 1, :], num_i[:, 1, :]).then_inc(step, 1)
            dve.wait_ge(step, 8)
            V.tensor_tensor_scan(num[:, 2, :], c["ones"][:, 0:TY], num[:, 1, :], 0.0, ALU.mult, ALU.add
                                 ).then_inc(step, 1)
            dve.wait_ge(step, 9)
            V.tensor_tensor(num[:, 3, :], num[:, 2, :], num[:, 1, :], ALU.subtract)
            V.tensor_tensor(past[:], c["iota"][:, 0:TT].unsqueeze(2).to_broadcast([P, TT, TY]),
                            num[:, 2, :].unsqueeze(1).to_broadcast([P, TT, TY]), ALU.is_ge).then_inc(step, 1)
            dve.wait_ge(step, 10)
            V.tensor_scalar(num[:, 4, :], num[:, 3, :], float(P), None, ALU.mult)
            V.tensor_reduce(tt[:], past[:], AXX, ALU.add).then_inc(step, 1)
            dve.wait_ge(step, 11)
            V.tensor_tensor(tmp[:], incl[:], num[:, 4, :].unsqueeze(2).to_broadcast([P, TY, NT]), ALU.add)
            V.tensor_scalar(tt[:], tt[:], float(TY - 1), None, ALU.min).then_inc(step, 1)
            dve.wait_ge(step, 12)
            V.tensor_copy(type_i[:], tt[:])
            V.tensor_tensor(tmp[:], tmp[:], hot[:], ALU.mult).then_inc(step, 1)
            dve.wait_ge(step, 13)
            V.tensor_reduce(pos[:], tmp[:].rearrange("p t i -> p i t"), AXX, ALU.add).then_inc(step, 1)
            dve.wait_ge(step, 14)
            V.tensor_copy(pos_i[:], pos[:]).then_inc(placed, 1)
            for i in range(NT):
                if i >= GT:
                    dve.wait_ge(sent[i % GT], 16 * (i // GT))
                V.tensor_scalar(xn[:, i % GT, :], X[:, i, :], c["mean"][:, i:i + 1], c["rstd"][:, i:i + 1],
                                ALU.subtract, ALU.mult).then_inc(normed, 1)

        @block.tensor
        def _(pe):
            pe.wait_ge(step, 2)
            for out, m in ((ranks, "before_row"), (totals, "ones")):
                nc.tensor.matmul(out[:], c[m][:], hot[:].rearrange("p a b -> p (a b)"), start=True, stop=True
                                 ).then_inc(pe_done, 1)

        @block.gpsimd
        def _(pool):
            pool.wait_ge(filled, 16)
            pool.wait_ge(placed, 1)
            for i in range(NT):
                pool.wait_ge(normed, i + 1)
                pool.indirect_dma_start(
                    out=xs, out_offset=bass.IndirectOffsetOnAxis(ap=pos_i[:, i:i + 1].bitcast(U32), axis=0),
                    in_=xn[:, i % GT, :], in_offset=None).then_inc(sent[i % GT], 16)
            for j in range(GT):
                pool.wait_ge(sent[j], 16 * NG)


def type_projections(nc, c, io, type_i, xs, kvq_s):
    with Phase(nc, "typed") as ph:
        w = ph.sb("w", [P, TY * 2, KVQ])
        wb = ph.sb("wb", [1, TY, KVQ])
        pT = ph.ps("pT", [P, 3, 512])
        prod = ph.ps("prod", [P, GT, 512])
        loaded, qloaded, summed = ph.sem("loaded"), ph.sem("qloaded"), ph.sem("summed")
        x_in, turned, ready = ph.sem("x_in"), ph.sem("turned"), ph.sem("ready")
        done, taken, stored = ph.sem("done"), ph.sem("taken"), ph.sems("stored", GT)

        with Phase(nc, "typed_q") as pq:
            wq, bq = pq.sb("wq", [P, TY * 2, PROJ]), pq.sb("bq", [1, TY, PROJ])
            block = pq.block()

            @block.sync
            def _(sp):
                for n, k in enumerate(("Wv", "Wk")):
                    sp.dma_start(w[:, :, n * PROJ:(n + 1) * PROJ],
                                 io["T2" + k].rearrange("t (k p) n -> p (t k) n", p=P)).then_inc(qloaded, 16)
                sp.dma_start(wq[:], io["T2Wq"].rearrange("t (k p) n -> p (t k) n", p=P)).then_inc(qloaded, 16)
                for n, k in enumerate(("bv", "bk")):
                    sp.dma_start(wb[:, :, n * PROJ:(n + 1) * PROJ], io["T2" + k].unsqueeze(0)).then_inc(qloaded, 16)
                sp.dma_start(bq[:], io["T2bq"].unsqueeze(0)).then_inc(qloaded, 16)

            @block.vector
            def _(dve):
                dve.wait_ge(qloaded, 96)
                for n, (dst, q) in enumerate(((w[:, :, 2 * PROJ:], wq[:]), (wb[:, :, 2 * PROJ:], bq[:]))):
                    nc.vector.tensor_tensor(dst, q[:, :, 0:DK], q[:, :, DK:2 * DK], ALU.add).then_inc(summed, 1)
                    dve.wait_ge(summed, 3 * n + 1)
                    nc.vector.tensor_tensor(dst, dst, q[:, :, 2 * DK:3 * DK], ALU.add).then_inc(summed, 1)
                    dve.wait_ge(summed, 3 * n + 2)
                    nc.vector.tensor_tensor(dst[:, :, 0:PROJ - 3 * DK], dst[:, :, 0:PROJ - 3 * DK],
                                            q[:, :, 3 * DK:], ALU.add).then_inc(summed, 1)

        x = ph.sb("x", [P, GT, D])
        xT = ph.sb("xT", [P, GT, D])
        y = ph.sb("y", [P, GT, KVQ])
        block = ph.block()

        @block.sync
        def _(sp):
            with nc.sync.Fori(0, TG) as it:
                sp.wait_ge(turned, it)
                sp.dma_start(x[:], xs.rearrange("(t p) d -> p t d", p=P)[:, ds(it * GT, GT), :]).then_inc(x_in, 16)
                for j in range(GT):
                    sp.wait_ge(taken, it * GT + j + 1)
                    sp.dma_start(kvq_s[ds((it * GT + j) * P, P), :], y[:, j, :]).then_inc(stored[j], 16)
            for j in range(GT):
                sp.wait_ge(stored[j], 16 * TG)

        @block.tensor
        def _(pe):
            with nc.tensor.Fori(0, TG) as it:
                pe.wait_ge(x_in, it * 16 + 16)
                pe.wait_ge(ready, it)
                for j in range(GT):
                    for h in range(2):
                        col = (j % 2) * D + h * P
                        last = nc.tensor.transpose(pT[:, j // 2, col:col + P], x[:, j, h * P:(h + 1) * P],
                                                   c["ident"][:])
                last.then_inc(turned, 1)
                pe.wait_ge(ready, it + 1)
                pe.wait_ge(taken, it * GT)
                for j in range(GT):
                    t = nc.tensor.value_load(type_i[0:1, ds(it * GT + j, 1)], min_val=0, max_val=TY - 1)
                    for h in range(2):
                        nc.tensor.matmul(prod[:, j, 0:KVQ], xT[:, j, h * P:(h + 1) * P],
                                         w[:, ds(t * 2 + h, 1), :].rearrange("p a n -> p (a n)"),
                                         start=(h == 0), stop=False)
                    nc.tensor.matmul(prod[:, j, 0:KVQ], c["ones"][0:1, :],
                                     wb[:, ds(t, 1), :].rearrange("p a n -> p (a n)"),
                                     start=False, stop=True).then_inc(done, 1)

        @block.scalar
        def _(act):
            with nc.scalar.Fori(0, TG) as it:
                act.wait_ge(turned, it + 1)
                act.wait_ge(done, it * GT)
                for b in range(3):
                    n = 2 if b < 2 else 1
                    last = nc.scalar.copy(xT[:, 2 * b:2 * b + n, :].rearrange("p j d -> p (j d)"),
                                          pT[:, b, 0:n * D])
                last.then_inc(ready, 1)

        @block.vector
        def _(dve):
            with nc.vector.Fori(0, TG) as it:
                for j in range(GT):
                    dve.wait_ge(done, it * GT + j + 1)
                    dve.wait_ge(stored[j], it * 16)
                    nc.vector.tensor_copy(y[:, j, :], prod[:, j, 0:KVQ]).then_inc(taken, 1)


def nodes_back(nc, c, pos_i, kvq_s, vk_table, q_rows):
    with Phase(nc, "back") as ph:
        y = ph.sb("y", [P, GT, KVQ])
        got, kept = ph.gather_sems(GT), ph.sem("kept")
        stored = ph.sems("stored", GT)
        block = ph.block()

        @block.gpsimd
        def _(pool):
            for i in range(NT):
                j = i % GT
                if i >= GT:
                    pool.wait_ge(kept, i - GT + 1)
                    pool.wait_ge(stored[j], 16 * (i // GT))
                pool.indirect_dma_start(
                    out=y[:, j, :], out_offset=None, in_=kvq_s,
                    in_offset=bass.IndirectOffsetOnAxis(ap=pos_i[:, i:i + 1].bitcast(U32), axis=0)
                ).then_inc(got[j], 16)

        @block.vector
        def _(dve):
            for i in range(NT):
                dve.wait_ge(got[i % GT], 16 * (i // GT) + 16)
                nc.vector.tensor_copy(q_rows[:, i, :], y[:, i % GT, 2 * PROJ:]).then_inc(kept, 1)

        @block.sync
        def _(sp):
            for i in range(NT):
                sp.wait_ge(got[i % GT], 16 * (i // GT) + 16)
                sp.dma_start(vk_table[i * P:(i + 1) * P, :], y[:, i % GT, 0:2 * PROJ]).then_inc(stored[i % GT], 16)
            for j in range(GT):
                sp.wait_ge(stored[j], 16 * NG)


def timed_scores(nc, c, io, name, slots, lo_rows, q_rows, vk_table, v_stream, scores, blocks):
    W = PROJ + TD
    R = 4
    last_round = NU // R - 1
    with Phase(nc, name) as ph:
        slot = ph.sb("slot", [P, ST + R * U, PW])
        logt = ph.sb("logt", [P, ST, 3])
        wt, bt = ph.sb("wt", [P, TD]), ph.sb("bt", [P, TD])
        lo_row = ph.sb("lo_row", [P, R, U * P])
        hotT = ph.sb("hotT", [P, R, U, P])
        idx = ph.sb("idx", [P, R, U], I32)
        vk = ph.sb("vk", [P, R, U, 2 * PROJ + TD])
        turns, whole = ph.sb("turns", [P, 2, 3 * U, TD]), ph.sb("whole", [P, 2, 3 * U, TD])
        emb = ph.sb("emb", [P, R, U, 2, TD])
        q_time = ph.sb("q_time", [P, R, U, DK])
        prod = ph.sb("prod", [P, 2, U, W])
        q = [ph.ps(f"q{u}", [P, U, P]) for u in range(R)]
        loaded, prepared, logged, released = ph.sem("loaded"), ph.sem("prepared"), ph.sem("logged"), ph.sem("rel")
        row_in, picked, hot = ph.sems("row_in", R), ph.sems("picked", R), ph.sems("hot", R)
        gathered, asked, mult = ph.gather_sems(R), ph.sems("asked", R), ph.sems("mult", R)
        phase, rounded, left = ph.sems("phase", 2), ph.sems("rounded", 2), ph.sems("left", 2)
        waved, joined = ph.sems("waved", R), ph.sems("joined", R)
        streamed, summed = ph.sems("streamed", R), ph.sems("summed", 2)
        block = ph.block()

        @block.sync
        def _(sp):
            def fetch_row(start, u):
                sp.dma_start(lo_row[:, u, :], lo_rows[ds(start, U * P)]
                             .partition_broadcast(P)).then_inc(row_in[u], 16)

            def stream(n, u):
                sp.wait_ge(gathered[u], (n + 1) * (16 * U))
                sp.wait_ge(waved[u], n + 1)
                sp.dma_start(v_stream[:, ds((n * R + u) * U, U), PROJ:D],
                             emb[:, u, :, :, :].rearrange("p j e d -> p j (e d)")).then_inc(streamed[u], 16)
                sp.dma_start(v_stream[:, ds((n * R + u) * U, U), 0:PROJ], vk[:, u, :, 0:PROJ]
                             ).then_inc(streamed[u], 16)

            sp.dma_start(slot[:, 0:ST, :], slots.rearrange("(p t) w -> p t w", t=ST)).then_inc(loaded, 16)
            sp.dma_start(wt[:], io["T2w"].partition_broadcast(P)).then_inc(loaded, 16)
            sp.dma_start(bt[:], io["T2b"].partition_broadcast(P)).then_inc(loaded, 16)
            for u in range(R):
                fetch_row(u * (U * P), u)
            with nc.sync.Fori(0, last_round) as it:
                for u in range(R):
                    sp.wait_ge(hot[u], it + 1)
                    fetch_row(it * (R * U * P) + (R + u) * (U * P), u)
                    stream(it, u)
            for u in range(R):
                stream(last_round, u)
            for u in range(R):
                sp.wait_ge(streamed[u], 32 * (NU // R))

        @block.gpsimd
        def _(pool):
            with nc.gpsimd.Fori(0, NU // R) as it:
                for u in range(R):
                    pool.wait_ge(picked[u], it + 1)
                    pool.wait_ge(mult[u], it)
                    pool.wait_ge(streamed[u], it * 32)
                    pool.sem_inc(released, 1)
                    for j in range(U):
                        pool.indirect_dma_start(
                            out=vk[:, u, j, 0:2 * PROJ], out_offset=None, in_=vk_table,
                            in_offset=bass.IndirectOffsetOnAxis(ap=idx[:, u, j:j + 1].bitcast(U32), axis=0)
                        ).then_inc(gathered[u], 16)

        @block.scalar
        def _(act):
            def pick(n, u):
                nc.scalar.copy(idx[:, u, :].bitcast(U32), slot[:, ds((n * R + u) * U, U), OTHER].bitcast(U32)
                               ).then_inc(picked[u], 1)

            act.wait_ge(loaded, 48)
            act.wait_ge(prepared, 4)
            for u in range(2):
                pick(0, u)
            nc.scalar.activation(logt[:], slot[:, 0:ST, TB:TB + 3], ACT.Ln, bias=c["ones"][:, 0:1]
                                 ).then_inc(logged, 1)
            with nc.scalar.Fori(0, NU // R) as it:
                for u in range(R):
                    done_before = it * (R // 2) + u // 2
                    act.wait_ge(phase[u % 2], (done_before + 1) * 2)
                    act.wait_ge(left[u % 2], done_before)
                    nc.scalar.activation(whole[:, u % 2, :, :].rearrange("p a d -> p (a d)"),
                                         turns[:, u % 2, :, :].rearrange("p a d -> p (a d)"), ACT.Copy,
                                         bias=ROUND).then_inc(rounded[u % 2], 1)
                    act.wait_ge(left[u % 2], done_before + 1)
                    act.wait_ge(streamed[u], it * 32)
                    act.wait_ge(asked[u], it)
                    parts = turns[:, u % 2, :, :].rearrange("p (j e) d -> p j e d", e=3)
                    nc.scalar.activation(q_time[:, u, :, DK - TD:], parts[:, :, 2, :], ACT.Sin,
                                         scale=-6.283185)
                    nc.scalar.activation(emb[:, u, :, :, :], parts[:, :, 0:2, :], ACT.Sin,
                                         scale=-6.283185).then_inc(waved[u], 1)
                    act.wait_ge(waved[u], it + 1)
                    act.wait_ge(mult[u], it)
                    nc.scalar.copy(vk[:, u, :, 2 * PROJ:], emb[:, u, :, 0, :]).then_inc(joined[u], 1)
                    if u < 2:
                        act.wait_ge(gathered[u + 2], it * (16 * U))
                        pick(it, u + 2)
                    else:
                        act.wait_ge(gathered[u - 2], (it + 1) * (16 * U))
                        pick(it + 1, u - 2)

        @block.vector
        def _(dve):
            V = nc.vector

            def make_hot(n, u):
                dve.wait_ge(row_in[u], n * 16 + 16)
                dve.wait_ge(asked[u], n)
                V.tensor_scalar(hotT[:, u, :, :].rearrange("p a b -> p (a b)"), lo_row[:, u, :],
                                c["iota_p"][:], None, ALU.is_equal).then_inc(hot[u], 1)

            def turns_scaled(n, u):
                if u < 2:
                    dve.wait_ge(waved[u + 2], n)
                else:
                    dve.wait_ge(waved[u - 2], n + 1)
                V.tensor_tensor(turns[:, u % 2, :, :],
                                logt[:, ds((n * R + u) * U, U), :].rearrange("p t e -> p (t e)")
                                .unsqueeze(2).to_broadcast([P, 3 * U, TD]),
                                wt[:].unsqueeze(1).to_broadcast([P, 3 * U, TD]), ALU.mult
                                ).then_inc(phase[u % 2], 1)

            def turns_shifted(n, u):
                dve.wait_ge(phase[u % 2], (n * (R // 2) + u // 2) * 2 + 1)
                V.tensor_tensor(turns[:, u % 2, :, :], turns[:, u % 2, :, :],
                                bt[:].unsqueeze(1).to_broadcast([P, 3 * U, TD]), ALU.add
                                ).then_inc(phase[u % 2], 1)

            def turns_left(n, u):
                dve.wait_ge(rounded[u % 2], n * (R // 2) + u // 2 + 1)
                V.scalar_tensor_tensor(turns[:, u % 2, :, :], whole[:, u % 2, :, :], ROUND, turns[:, u % 2, :, :],
                                       ALU.subtract, ALU.subtract).then_inc(left[u % 2], 1)

            def multiply(n, u):
                dve.wait_ge(asked[u], n + 1)
                dve.wait_ge(gathered[u], (n + 1) * (16 * U))
                dve.wait_ge(joined[u], n + 1)
                dve.wait_ge(summed[u % 2], n * (R // 2) + u // 2)
                V.tensor_tensor(
                    prod[:, u % 2, :, :].rearrange("p j (h d) -> p j h d", d=DK),
                    vk[:, u, :, PROJ:].rearrange("p j (h d) -> p j h d", d=DK),
                    q[u][:, :, 0:DK].unsqueeze(2).to_broadcast([P, U, H2, DK]), ALU.mult).then_inc(mult[u], 1)

            def total(n, u):
                dve.wait_ge(mult[u], n + 1)
                V.tensor_reduce(scores[:, ds((n * R + u) * (U * H2), U * H2)],
                                prod[:, u % 2, :, :].rearrange("p j (h d) -> p (j h) d", d=DK), AXX, ALU.add
                                ).then_inc(summed[u % 2], 1)

            V.memset(slot[:, ST:, :], 0.0).then_inc(prepared, 1)
            V.memset(q_time[:], 0.0).then_inc(prepared, 1)
            dve.wait_ge(loaded, 48)
            V.tensor_scalar(wt[:], wt[:], 1.0 / TWO_PI, None, ALU.mult).then_inc(prepared, 1)
            V.tensor_scalar(bt[:], bt[:], 1.0 / TWO_PI, 0.25, ALU.mult, ALU.add).then_inc(prepared, 1)
            dve.wait_ge(prepared, 4)
            dve.wait_ge(logged, 1)
            for u in range(2):
                make_hot(0, u)
                turns_scaled(0, u)
                turns_shifted(0, u)
                turns_left(0, u)

            def unit(n, u, following):
                if following:
                    make_hot(*following)
                    turns_scaled(*following)
                multiply(n, u)
                if following:
                    turns_shifted(*following)
                total(n, u)
                if following:
                    turns_left(*following)

            with nc.vector.Fori(0, last_round) as it:
                for u in range(R):
                    unit(it, u, (it + (u + 2) // R, (u + 2) % R))
            for u in range(R):
                unit(last_round, u, (last_round, u + 2) if u + 2 < R else None)

        @block.tensor
        def _(pe):
            with nc.tensor.Fori(0, NU // R) as it:
                for u in range(R):
                    nb = load_blocks(nc.tensor, blocks, it * R + u)
                    pe.wait_ge(hot[u], it + 1)
                    pe.wait_ge(mult[u], it)
                    pe.wait_ge(waved[u], it + 1)
                    nc.tensor.matmul(q[u][:, :, 0:DK], c["ident"][:], q_time[:, u, :, :], start=True, stop=False)
                    for j in range(U):
                        last = nc.tensor.matmul(q[u][:, j, 0:DK], hotT[:, u, j, :], rowof(q_rows, nb[j // RUN]),
                                                start=False, stop=(j == U - 1))
                    last.then_inc(asked[u], 1)


def fold_direction(nc, name, agg, both, first):
    VW = PROJ + TD
    with Phase(nc, name) as ph:
        den, rec = ph.sb("den", [P, NT, H2]), ph.sb("rec", [P, NT, H2])
        t = ph.sb("t", [P, NT, VW])
        s = ph.sem("s")
        block = ph.block()

        @block.vector
        def _(dve):
            V = nc.vector
            V.tensor_scalar(den[:], agg[:, :, VW:VW + H2], 1e-16, None, ALU.add).then_inc(s, 1)
            dve.wait_ge(s, 1)
            V.reciprocal(rec[:], den[:]).then_inc(s, 1)
            dve.wait_ge(s, 2)
            dst = both[:, :, 0:VW] if first else t[:]
            for h in range(H2):
                cols = slice(h * DK, (h + 1) * DK)
                last = V.tensor_tensor(dst[:, :, cols], agg[:, :, cols],
                                       rec[:, :, h:h + 1].to_broadcast([P, NT, DK]), ALU.mult)
            if first:
                V.tensor_copy(both[:, :, VW:D], agg[:, :, VW + H2:D + H2])
            else:
                last.then_inc(s, 1)
                dve.wait_ge(s, 3)
                V.tensor_tensor(both[:, :, 0:VW], both[:, :, 0:VW], t[:], ALU.add)
                V.tensor_tensor(both[:, :, VW:D], both[:, :, VW:D], agg[:, :, VW + H2:D + H2], ALU.add)


def type_output(nc, c, io, pos_i, type_i, both, xs, as_, X):
    with Phase(nc, "tout") as ph:
        w = ph.sb("w", [P, TY * 2, D])
        rows = ph.sb("rows", [P, 2, TY, D])
        ba = ph.sb("ba", [1, TY, D])
        pT, prod = ph.ps("pT", [P, 3, 512]), ph.ps("prod", [P, GT, 512])
        loaded, summed = ph.sem("loaded"), ph.sem("summed")
        filled, zeroed = ph.sem("filled"), ph.sem("zeroed")
        a_in, x_in, turned, ready, done = (ph.sem(k) for k in ("a_in", "x_in", "turned", "ready", "done"))
        added, counted, aggred, rooted, recd = (ph.sem(k) for k in ("added", "counted", "aggred", "rooted", "recd"))
        spread = ph.sem("spread")
        normed, scaled, final, stored = ph.sem("normed"), ph.sem("scaled"), ph.sem("final"), ph.sem("stored")
        order = "(t p) d -> p t d"

        with Phase(nc, "tout_w") as pw:
            low = pw.sb("low", [P, TY, D])
            low_in, wrote = pw.sem("low_in"), pw.gather_sems(1)[0]
            w_k = w[:].rearrange("p (t k) n -> p t k n", k=2)
            zero = pw.sb("zero", [P, D])
            block = pw.block()

            @block.sync
            def _(sp):
                wa = io["T2Wa"].rearrange("t (s k p) n -> s p t k n", s=2, p=P)
                for k in range(2):
                    sp.dma_start(w_k[:, :, k, :], wa[0, :, :, k, :]).then_inc(loaded, 16)
                for n, k in enumerate(("gamma", "beta")):
                    sp.dma_start(rows[:, n, :, :].rearrange("p t n -> p (t n)"),
                                 io["T2" + k].rearrange("t n -> (t n)").partition_broadcast(P)).then_inc(loaded, 16)
                sp.dma_start(ba[:], io["T2ba"].unsqueeze(0)).then_inc(loaded, 16)
                sp.wait_ge(zeroed, 1)
                sp.dma_start(as_.rearrange(order, p=P), zero[:].unsqueeze(1).to_broadcast([P, TT, D])
                             ).then_inc(filled, 16)
                for k in range(2):
                    if k:
                        sp.wait_ge(summed, 1)
                    sp.dma_start(low[:], wa[1, :, :, k, :]).then_inc(low_in, 16)
                sp.wait_ge(loaded, 16 * 5)

            @block.vector
            def _(dve):
                nc.vector.memset(zero[:], 0.0).then_inc(zeroed, 1)
                dve.wait_ge(loaded, 16 * 5)
                for k in range(2):
                    dve.wait_ge(low_in, 16 * (k + 1))
                    nc.vector.tensor_tensor(w_k[:, :, k, :], w_k[:, :, k, :], low[:], ALU.add).then_inc(summed, 1)

            @block.gpsimd
            def _(pool):
                pool.wait_ge(filled, 16)
                for i in range(NT):
                    pool.indirect_dma_start(
                        out=as_, out_offset=bass.IndirectOffsetOnAxis(ap=pos_i[:, i:i + 1].bitcast(U32), axis=0),
                        in_=both[:, i, :], in_offset=None).then_inc(wrote, 16)
                pool.wait_ge(wrote, 16 * NT)

        a, x = ph.sb("a", [P, GT, D]), ph.sb("x", [P, GT, D])
        aT = ph.sb("aT", [P, GT, D])
        y = ph.sb("y", [P, GT, D])
        st, mv = ph.sb("st", [P, GT, 6]), ph.sb("mv", [P, GT, 2])
        sd, rs = ph.sb("sd", [P, GT]), ph.sb("rs", [P, GT])

        with ph.nc.Block() as block:
            @block.sync
            def _(sp):
                with nc.sync.Fori(0, TG) as it:
                    sp.wait_ge(turned, it)
                    sp.dma_start(a[:], as_.rearrange(order, p=P)[:, ds(it * GT, GT), :]).then_inc(a_in, 16)
                    sp.wait_ge(added, it * GT)
                    sp.dma_start(x[:], xs.rearrange(order, p=P)[:, ds(it * GT, GT), :]).then_inc(x_in, 16)
                    sp.wait_ge(final, (it + 1) * GT)
                    sp.dma_start(as_.rearrange(order, p=P)[:, ds(it * GT, GT), :], y[:]).then_inc(stored, 16)
                sp.wait_ge(stored, 16 * TG)

            @block.tensor
            def _(pe):
                with nc.tensor.Fori(0, TG) as it:
                    pe.wait_ge(a_in, it * 16 + 16)
                    pe.wait_ge(ready, it)
                    for j in range(GT):
                        for h in range(2):
                            col = (j % 2) * D + h * P
                            last = nc.tensor.transpose(pT[:, j // 2, col:col + P], a[:, j, h * P:(h + 1) * P],
                                                       c["ident"][:])
                    last.then_inc(turned, 1)
                    pe.wait_ge(ready, it + 1)
                    pe.wait_ge(added, it * GT)
                    for j in range(GT):
                        t = nc.tensor.value_load(type_i[0:1, ds(it * GT + j, 1)], min_val=0, max_val=TY - 1)
                        for h in range(2):
                            nc.tensor.matmul(prod[:, j, 0:D], aT[:, j, h * P:(h + 1) * P],
                                             w[:, ds(t * 2 + h, 1), :].rearrange("p a n -> p (a n)"),
                                             start=(h == 0), stop=False)
                        nc.tensor.matmul(prod[:, j, 0:D], c["ones"][0:1, :],
                                         ba[:, ds(t, 1), :].rearrange("p a n -> p (a n)"),
                                         start=False, stop=True).then_inc(done, 1)

            @block.scalar
            def _(act):
                with nc.scalar.Fori(0, TG) as it:
                    act.wait_ge(turned, it + 1)
                    act.wait_ge(done, it * GT)
                    for b in range(3):
                        n = 2 if b < 2 else 1
                        last = nc.scalar.copy(aT[:, 2 * b:2 * b + n, :].rearrange("p j d -> p (j d)"),
                                              pT[:, b, 0:n * D])
                    last.then_inc(ready, 1)
                    act.wait_ge(aggred, (it + 1) * GT)
                    nc.scalar.activation(sd[:], mv[:, :, 1], ACT.Sqrt, bias=c["eps"][:]).then_inc(rooted, 1)

            @block.vector
            def _(dve):
                V = nc.vector
                with nc.vector.Fori(0, TG) as it:
                    dve.wait_ge(x_in, it * 16 + 16)
                    dve.wait_ge(stored, it * 16)
                    for j in range(GT):
                        dve.wait_ge(done, it * GT + j + 1)
                        V.tensor_tensor(y[:, j, :], prod[:, j, 0:D], x[:, j, :], ALU.add).then_inc(added, 1)
                    for j in range(GT):
                        dve.wait_ge(added, it * GT + j + 1)
                        V.bn_stats(st[:, j, :], y[:, j, :]).then_inc(counted, 1)
                    for j in range(GT):
                        if j == 0:
                            dve.wait_ge(counted, it * GT + GT)
                            dve.sem_inc(spread, 1)
                        V.bn_aggr(mv[:, j, :], st[:, j, :]).then_inc(aggred, 1)
                    dve.wait_ge(rooted, it + 1)
                    V.reciprocal(rs[:], sd[:]).then_inc(recd, 1)
                    dve.wait_ge(recd, it + 1)
                    for j in range(GT):
                        V.tensor_scalar(y[:, j, :], y[:, j, :], mv[:, j, 0:1], rs[:, j:j + 1],
                                        ALU.subtract, ALU.mult).then_inc(normed, 1)
                    for j in range(GT):
                        t = nc.vector.value_load(type_i[0:1, ds(it * GT + j, 1)], min_val=0, max_val=TY - 1)
                        for n, (before, after) in enumerate(((normed, scaled), (scaled, final))):
                            dve.wait_ge(before, it * GT + j + 1)
                            V.tensor_tensor(y[:, j, :], y[:, j, :],
                                            rows[:, n, ds(t, 1), :].rearrange("p a n -> p (a n)"),
                                            (ALU.mult, ALU.add)[n]).then_inc(after, 1)

        with Phase(nc, "tout_x") as px:
            got = px.gather_sems(GT)
            moved = px.sem("moved")
            back = px.sb("back", [P, GT, D])
            block = px.block()

            @block.gpsimd
            def _(pool):
                for i in range(NT):
                    if i >= GT:
                        pool.wait_ge(moved, i - GT + 1)
                    pool.indirect_dma_start(
                        out=back[:, i % GT, :], out_offset=None, in_=as_,
                        in_offset=bass.IndirectOffsetOnAxis(ap=pos_i[:, i:i + 1].bitcast(U32), axis=0)
                    ).then_inc(got[i % GT], 16)

            @block.vector
            def _(dve):
                for i in range(NT):
                    dve.wait_ge(got[i % GT], 16 * (i // GT) + 16)
                    nc.vector.tensor_tensor(X[:, i, :], X[:, i, :], back[:, i % GT, :], ALU.add).then_inc(moved, 1)


def load_nodes(nc, x, X):
    with Phase(nc, "load") as ph:
        loaded = ph.sem("loaded")
        block = ph.block()

        @block.sync
        def _(sp):
            sp.dma_start(X[:], x.rearrange("(t p) d -> p t d", p=P)).then_inc(loaded, 16)
            sp.wait_ge(loaded, 16)


def store_nodes(nc, X, out):
    with Phase(nc, "store") as ph:
        stored = ph.sem("stored")
        block = ph.block()
        whole = N // P
        rest = N - whole * P

        @block.sync
        def _(sp):
            sp.dma_start(out[0:whole * P].rearrange("(t p) d -> p t d", p=P), X[:, 0:whole, :]).then_inc(stored, 16)
            sp.dma_start(out[whole * P:N], X[0:rest, whole, :]).then_inc(stored, 16)
            sp.wait_ge(stored, 32)


def gnn_ffn_kernel(nc, io, out):
    def table(name, *shape):
        return nc.dram_tensor(name, shape, F32, kind="Internal").ap()

    with ExitStack() as whole:
        def sb(name, shape, dt=F32, stack=whole):
            return stack.enter_context(nc.sbuf_tensor(name, shape, dt))

        c = dict(ident=sb("ident", [P, P]), ones=sb("ones", [P, P]), before_col=sb("before_col", [P, P]),
                 before_row=sb("before_row", [P, P]), iota=sb("iota", [P, ST]), iota_p=sb("iota_p", [P, 1]),
                 eps=sb("eps", [P, 1]), ident_h=sb("ident_h", [P, P], BF16),
                 mean=sb("mean", [P, NT]), rstd=sb("rstd", [P, NT]),
                 block_f=[sb(f"block_f{k}", [P, ST]) for k in range(2)],
                 block_i=[sb(f"block_i{k}", [P, ST], I32) for k in range(2)])
        X = sb("X", [P, NT, D])
        degree, inv_degree, chosen = sb("degree", [P, NT]), sb("inv_degree", [P, NT]), sb("chosen", [P, NT])
        slots = [table(f"slots{k}", P * ST, PW) for k in range(2)]
        lo_rows = [table(f"lo_rows{k}", P * ST) for k in range(2)]
        key_rows = [table(f"key_rows{k}", P * ST) for k in range(2)]
        v_stream = table("v_stream", P, ST, D)
        node_table = table("node_table", NP, D)

        make_constants(nc, c)
        load_nodes(nc, io["x"], X)
        with ExitStack() as part:
            starts = [sb(f"starts{k}", [NT, P], stack=part) for k in range(2)]
            sort_edges(nc, c, io, slots, degree, starts)
        turn_slot_rows(nc, c, slots, lo_rows, key_rows)

        layernorm_stats(nc, c, "norm0", X)
        with ExitStack() as part:
            agg = sb("agg0", [P, NT, D + 8], stack=part)
            Q, scores = sb("Q", [P, NT, D], stack=part), sb("scores0", [P, ST * 8], stack=part)
            kv_table = table("kv_table", NP, 2 * D)
            attention_inputs(nc, c, io, X, Q, kv_table)
            attention_scores(nc, c, slots[0], lo_rows[0], Q, kv_table, v_stream, scores, c["block_i"][0])
            segment_softmax(nc, c, "soft0", 8, 32 ** -0.5, key_rows[0], scores)
            attention_values(nc, c, "values0", slots[0], v_stream, scores, c["block_i"][0], agg, 8, D)
            attention_output(nc, c, io, X, agg)
        layernorm_stats(nc, c, "norm1", X)
        expert_layers(nc, c, io, X)

        layernorm_stats(nc, c, "norm2", X)
        store_normalised(nc, c, "xn", X, node_table)
        sage_table = table("sage_table", NP, D)
        with ExitStack() as part:
            agg = sb("agg1", [P, NT, D], stack=part)
            aggregate(nc, c, "mean1", slots[0], node_table, c["block_i"][0], agg, False)
            sage_layers(nc, c, io, X, agg, degree, inv_degree, sage_table)
            aggregate(nc, c, "mean2", slots[0], sage_table, c["block_i"][0], agg, False)
            add_scaled(nc, "add_mean2", X, agg, inv_degree)
        layernorm_stats(nc, c, "norm3", X)
        choose_tokens(nc, c, io, X, table("router_row", NP), chosen)
        chosen_ffn(nc, c, io, X, chosen)

        layernorm_stats(nc, c, "norm4", X)
        with ExitStack() as part:
            pos_i, type_i = sb("pos_i", [P, NT], I32, part), sb("type_i", [P, TT], I32, part)
            sorted_x, sorted_agg = table("sorted_x", TT * P, D), table("sorted_agg", TT * P, D)
            sorted_kvq, vk_table = table("sorted_kvq", TT * P, KVQ), table("vk_table", NP, 2 * PROJ)
            sort_nodes(nc, c, io, X, pos_i, type_i, sorted_x)
            type_projections(nc, c, io, type_i, sorted_x, sorted_kvq)
            both = sb("both", [P, NT, D], stack=part)
            with ExitStack() as inner:
                agg, q_rows = sb("agg2", [P, NT, D + H2], stack=inner), sb("q_rows", [P, NT, DK], stack=inner)
                scores = sb("scores2", [P, ST * H2], stack=inner)
                nodes_back(nc, c, pos_i, sorted_kvq, vk_table, q_rows)
                for k in range(2):
                    timed_scores(nc, c, io, f"timed{k}", slots[k], lo_rows[k], q_rows, vk_table, v_stream,
                                 scores, c["block_i"][k])
                    segment_softmax(nc, c, f"soft2{k}", H2, DK ** -0.5, key_rows[k], scores)
                    attention_values(nc, c, f"values2{k}", slots[k], v_stream, scores, c["block_i"][k], agg,
                                     H2, PROJ + TD)
                    fold_direction(nc, f"fold{k}", agg, both, k == 0)
            type_output(nc, c, io, pos_i, type_i, both, sorted_x, sorted_agg, X)
        layernorm_stats(nc, c, "norm5", X)
        mixture_ffn(nc, c, io, X)

        layernorm_stats(nc, c, "norm6", X)
        row_product(nc, c, io, "support", X, "G3w", take_to_dram=node_table)
        with ExitStack() as part:
            agg = sb("agg3", [P, NT, D], stack=part)
            aggregate(nc, c, "weighted", slots[1], node_table, c["block_i"][1], agg, True)
            add_relu(nc, "relu3", X, agg)
        layernorm_stats(nc, c, "norm7", X)
        row_product(nc, c, io, "last", X, "F3w", bias="F3b")
        store_nodes(nc, X, out)


def laid_out(i):
    def cols(a):
        return a.reshape(-1, P).T

    def pad(a, rows, value):
        return np.concatenate([a, np.full((rows - len(a),) + a.shape[1:], value, a.dtype)])

    def edge_cols(a):
        return np.swapaxes(a.reshape((ET, P) + a.shape[1:]), 0, 1)

    heads = 8
    qkv_w = i["L0_gnn_W_qkv"].reshape(D, heads, 3, D // heads)
    qkv_b = i["L0_gnn_b_qkv"].reshape(heads, 3, D // heads)
    src, dst = pad(i["src"], EP, NP - 1), pad(i["dst"], EP, NP - 1)
    r = dict(x=pad(i["x"], NP, 0), src_c=edge_cols(src), dst_c=edge_cols(dst), src_r=src, dst_r=dst,
             attr_c=edge_cols(pad(i["edge_attr_5"], EP, 0)), w_c=edge_cols(pad(i["edge_weight"], EP, 0)),
             W0=np.concatenate([i["L0_gnn_W_out"][:D]] + [qkv_w[:, :, k].reshape(D, D) for k in range(3)], 1),
             b0=np.concatenate([i["L0_gnn_b_out"]] + [qkv_b[:, k].reshape(D) for k in range(3)]),
             W0m=i["L0_gnn_W_out"][D:])
    r.update(F0W1=i["L0_ffn_W1"], F0W2=i["L0_ffn_W2"], F0W3=i["L0_ffn_Wo"], F0Wr=i["L0_ffn_Wr"],
             F0br=i["L0_ffn_br"], F0bo=i["L0_ffn_bo"])
    for layer in (1, 2):
        for k in ("b", "g", "be", "m", "v"):
            r[f"F0{k}{layer}"] = cols(i[f"L0_ffn_{k}{layer}"])
    r.update(S1W1=np.concatenate([i["L1_gnn_W1l"].T, i["L1_gnn_W1r"].T]),
             S1W2=np.concatenate([i["L1_gnn_W2l"].T, i["L1_gnn_W2r"].T], 1),
             S1b1=cols(i["L1_gnn_b1"]), S1b2=i["L1_gnn_b2"],
             C1wr=i["L1_ffn_wr"].reshape(-1), C1br=i["L1_ffn_br"], C1W1=i["L1_ffn_w1"], C1W2=i["L1_ffn_w2"],
             C1b1=cols(i["L1_ffn_b1"]), C1b2=i["L1_ffn_b2"])
    m = {k[7:]: v for k, v in i.items() if k.startswith("L2_ffn_")}
    r.update(M2sW1=m["sW1"], M2sW2=m["sW2"], M2sW3=m["sW3"], M2eW1=m["eW1"], M2eW2=m["eW2"], M2eW3=m["eW3"],
             M2b=cols(np.concatenate([m["sb1"], m["sb2"], m["eb1"].reshape(-1)])), M2eb2=m["eb2"].T,
             M2b3=np.concatenate([m["eb3"], m["sb3"][None]]), M2gW=m["gW"], M2gb=m["gb"])
    r.update(T2type=cols(pad(i["node_type_19"], NP, 0)), T2w=i["L2_gnn_w_time"], T2b=i["L2_gnn_b_time"])
    for k in ("Wk", "Wq", "Wv", "bk", "bq", "bv", "Wa", "ba", "gamma", "beta"):
        r["T2" + k] = i["L2_gnn_" + k]
    r.update(G3w=i["L3_gnn_weight"], F3w=i["L3_ffn_weight"].T, F3b=i["L3_ffn_bias"])
    return r


def kernel(**inputs):
    import numpy as _np
    import concourse.bacc as _bacc
    from concourse import mybir as _mybir
    from concourse.bass_utils import run_bass_kernel_spmd as _run

    nc = _bacc.Bacc("TRN2", target_bir_lowering=False, num_devices=1)
    arrays, io = {}, {}
    for name, a in laid_out({k: _np.asarray(v) for k, v in inputs.items()}).items():
        a = _np.ascontiguousarray(a)
        arrays[f"in_{name}_dram"] = a
        io[name] = nc.dram_tensor(f"in_{name}_dram", a.shape, _mybir.dt.from_np(a.dtype), kind="ExternalInput").ap()
    out = nc.dram_tensor("out_0_dram", (N, D), F32, kind="ExternalOutput").ap()
    gnn_ffn_kernel(nc, io, out)
    r = _run(nc, [arrays], core_ids=[0])
    return r.results[0]["out_0_dram"]
```

```python
import numpy as np
from contextlib import ExitStack

import concourse.bass as bass
from concourse import mybir

F32 = mybir.dt.float32
I32 = mybir.dt.int32
U32 = mybir.dt.uint32
BF16 = mybir.dt.bfloat16
ALU = mybir.AluOpType
ACT = mybir.ActivationFunctionType
AXX = mybir.AxisListType.X

P = 128
N = 3125
NT = -(-N // P)
NP = NT * P
D = 256
GT = 5
NG = NT // GT
GR = GT * P
HR = GR // 2
E = 50000
CH = 8
NCH = -(-E // (P * CH))
ET = NCH * CH
EP = ET * P
RUN = 2
ST = 448
assert NCH * CH * P + NT * (RUN * P - 1) <= ST * P
U = 4
NU = ST // U
PW = 8
LO, OTHER, TB, TA, TC, WGT, KEY = range(7)
BIG = 1.0e30
LN_EPS = 1e-5
BN_EPS = 1e-3


def ds(start, size):
    return bass.ds(start, size)


class Phase:

    def __init__(self, nc, name):
        self.nc, self.name, self.stack, self.numbers = nc, name, ExitStack(), []

    def __enter__(self):
        return self

    def __exit__(self, *a):
        self.stack.__exit__(*a)
        runs = []
        for n in sorted(self.numbers):
            if runs and n == runs[-1][1]:
                runs[-1][1] = n + 1
            else:
                runs.append([n, n + 1])
        for first, end in runs:
            self.nc.sync.sem_clear(range(first, end))

    def sem(self, name):
        s = self.stack.enter_context(self.nc.semaphore(f"{self.name}_{name}"))
        self.numbers.append(s.num)
        return s

    def sems(self, name, n):
        return [self.sem(f"{name}{i}") for i in range(n)]

    def gather_sems(self, n):
        return [self.nc.alloc_semaphore(f"{self.name}_gpsimd_dma{i}") for i in range(n)]

    def sb(self, name, shape, dt=F32):
        return self.stack.enter_context(self.nc.sbuf_tensor(f"{self.name}_{name}", shape, dt))

    def ps(self, name, shape, dt=F32):
        return self.stack.enter_context(self.nc.psum_tensor(f"{self.name}_{name}", shape, dt))

    def block(self):
        return self.stack.enter_context(self.nc.Block())


def make_constants(nc, c):
    with Phase(nc, "const") as ph:
        made, cut, i_int = ph.sem("made"), ph.sem("cut"), ph.sem("i_int")
        row_i = ph.sb("row_i", [P, ST], I32)
        col_i = ph.sb("col_i", [P, 1], I32)
        block = ph.block()

        @block.gpsimd
        def _(pool):
            nc.gpsimd.memset(c["ident"][:], 0.0).then_inc(made, 1)
            nc.gpsimd.memset(c["ones"][:], 1.0).then_inc(made, 1)
            nc.gpsimd.iota(row_i[:], [[1, ST]], base=0, channel_multiplier=0).then_inc(i_int, 1)
            nc.gpsimd.iota(col_i[:], [[1, 1]], base=0, channel_multiplier=1).then_inc(i_int, 1)
            pool.wait_ge(made, 2)
            nc.gpsimd.affine_select(out=c["ident"][:], in_=c["ident"][:], compare_op=ALU.not_equal, fill=1.0,
                                    base=0, pattern=[[-1, P]], channel_multiplier=1).then_inc(cut, 1)
            nc.gpsimd.affine_select(out=c["before_col"][:], in_=c["ones"][:], compare_op=ALU.is_gt, fill=0.0,
                                    base=0, pattern=[[-1, P]], channel_multiplier=1).then_inc(cut, 1)
            nc.gpsimd.affine_select(out=c["before_row"][:], in_=c["ones"][:], compare_op=ALU.is_gt, fill=0.0,
                                    base=0, pattern=[[1, P]], channel_multiplier=-1).then_inc(cut, 1)

        @block.vector
        def _(dve):
            dve.wait_ge(i_int, 2)
            nc.vector.tensor_copy(c["iota"][:], row_i[:])
            nc.vector.tensor_copy(c["iota_p"][:], col_i[:])
            nc.vector.memset(c["eps"][:], LN_EPS)
            dve.wait_ge(cut, 1)
            nc.vector.tensor_copy(c["ident_h"][:], c["ident"][:])


def sort_edges(nc, c, io, X, slots, degree, starts):
    keys = ("dst", "src")
    with Phase(nc, "sort") as ph:
        loaded, filled, blank_made = ph.sem("loaded"), ph.sem("filled"), ph.sem("blank")
        split, floated = ph.sem("split"), ph.sem("floated")
        hot = ph.sems("hot", 2)
        counted = ph.sems("counted", 2)
        total, t1, t2, ended = ph.sem("total"), ph.sem("t1"), ph.sem("t2"), ph.sem("ended")
        packed, nodes_in = ph.sem("packed"), ph.sem("nodes_in")
        key_i = [ph.sb(f"key_i{k}", [P, ET], I32) for k in range(2)]
        hi_i = [ph.sb(f"hi_i{k}", [P, ET], I32) for k in range(2)]
        lo_i = [ph.sb(f"lo_i{k}", [P, ET], I32) for k in range(2)]
        hi = [ph.sb(f"hi{k}", [P, ET]) for k in range(2)]
        lo = [ph.sb(f"lo{k}", [P, ET]) for k in range(2)]
        key = [ph.sb(f"key{k}", [P, ET]) for k in range(2)]
        pay = [ph.sb(f"pay{k}", [P, ET, PW]) for k in range(2)]
        attr = ph.sb("attr", [P, ET, 5])
        wgt = ph.sb("wgt", [P, ET])
        blank = ph.sb("blank", [P, ST, PW])
        hot_hi = [ph.sb(f"hot_hi{k}", [P, CH, NT], BF16) for k in range(2)]
        hot_lo = [ph.sb(f"hot_lo{k}", [P, CH, P], BF16) for k in range(2)]
        zero = ph.sb("zero", [P, P], BF16)
        count = [ph.sb(f"count{k}", [NT, CH + 1, P]) for k in range(2)]
        small = ph.sb("small", [NT, 2, 8])
        small_i = ph.sb("small_i", [NT, 2, 2], I32)
        incl = ph.sb("incl", [NT, 2, P])
        past = ph.sb("past", [NT, ST])
        i25 = c["iota"][:, 0:NT]
        i128 = c["iota"][:, 0:P]

        with ph.nc.psum_tensor("sort_hist", [NT, 2, 512], F32) as hist, \
                ph.nc.psum_tensor("sort_misc", [P, 2, 512], F32) as misc, ph.nc.Block() as block:

            @block.sync
            def _(sp):
                for k in range(2):
                    sp.dma_start(key_i[k][:], io[keys[k] + "_c"]).then_inc(loaded, 16)
                sp.dma_start(attr[:], io["attr_c"]).then_inc(loaded, 16)
                sp.dma_start(wgt[:], io["w_c"]).then_inc(loaded, 16)
                sp.wait_ge(blank_made, 4)
                for k in range(2):
                    sp.dma_start(slots[k].rearrange("(p t) w -> p t w", t=ST), blank[:]).then_inc(filled, 16)
                sp.dma_start(X[:], io["x"].rearrange("(t p) d -> p t d", p=P)).then_inc(nodes_in, 16)
                sp.wait_ge(filled, 32)
                sp.wait_ge(nodes_in, 16)

            @block.gpsimd
            def _(pool):
                nc.gpsimd.memset(blank[:], 0.0).then_inc(blank_made, 1)
                pool.wait_ge(blank_made, 1)
                nc.gpsimd.memset(blank[:, :, LO:LO + 1], -1.0).then_inc(blank_made, 1)
                nc.gpsimd.memset(blank[:, :, KEY:KEY + 1], -1.0).then_inc(blank_made, 1)
                nc.gpsimd.memset(zero[:], 0.0).then_inc(blank_made, 1)

            @block.scalar
            def _(act):
                act.wait_ge(loaded, 64)
                act.wait_ge(floated, 2)
                for k in range(2):
                    nc.scalar.copy(pay[k][:, :, LO], lo[k][:])
                    nc.scalar.copy(pay[k][:, :, KEY], key[k][:])
                    nc.scalar.copy(pay[k][:, :, WGT], wgt[:])
                    nc.scalar.copy(pay[k][:, :, TA], attr[:, :, 0])
                    nc.scalar.copy(pay[k][:, :, TB], attr[:, :, 1 + k])
                    nc.scalar.copy(pay[k][:, :, TC], attr[:, :, 2 - k]).then_inc(packed, 1)

            @block.vector
            def _(dve):
                dve.wait_ge(loaded, 64)
                for k in range(2):
                    nc.vector.tensor_scalar(hi_i[k][:], key_i[k][:], 7, None, ALU.logical_shift_right)
                    nc.vector.tensor_scalar(lo_i[k][:], key_i[k][:], P - 1, None, ALU.bitwise_and)
                    nc.vector.tensor_copy(pay[k][:, :, OTHER].bitcast(I32), key_i[1 - k][:])
                    nc.vector.memset(pay[k][:, :, 7], 0.0)
                    nc.vector.tensor_copy(key[k][:], key_i[k][:]).then_inc(split, 1)
                dve.wait_ge(split, 2)
                for k in range(2):
                    nc.vector.tensor_copy(hi[k][:], hi_i[k][:])
                    nc.vector.tensor_copy(lo[k][:], lo_i[k][:]).then_inc(floated, 1)
                dve.wait_ge(floated, 2)
                with nc.vector.Fori(0, NCH) as it:
                    for k in range(2):
                        dve.wait_ge(counted[k], it)
                        nc.vector.tensor_tensor(
                            hot_hi[k][:], i25.unsqueeze(1).to_broadcast([P, CH, NT]),
                            hi[k][:, ds(it * CH, CH)].unsqueeze(2).to_broadcast([P, CH, NT]), ALU.is_equal)
                        nc.vector.tensor_tensor(
                            hot_lo[k][:], i128.unsqueeze(1).to_broadcast([P, CH, P]),
                            lo[k][:, ds(it * CH, CH)].unsqueeze(2).to_broadcast([P, CH, P]),
                            ALU.is_equal).then_inc(hot[k], 1)
                dve.wait_ge(total, 1)
                for k in range(2):
                    nc.vector.tensor_copy(count[k][:, 1, :], hist[:, k, 0:P]).then_inc(t1, 1)
                dve.wait_ge(t1, 2)
                for k in range(2):
                    nc.vector.tensor_reduce(small[:, k, 0:1], count[k][:, 1, :], AXX, ALU.add)
                    nc.vector.tensor_tensor_scan(incl[:, k, :], c["ones"][0:NT, :], count[k][:, 1, :], 0.0,
                                                 ALU.mult, ALU.add).then_inc(t1, 1)
                dve.wait_ge(t1, 4)
                nc.vector.tensor_scalar(small[:, :, 1:2], small[:, :, 0:1], float(RUN * P - 1), None,
                                        ALU.add).then_inc(t1, 1)
                dve.wait_ge(t1, 5)
                nc.vector.tensor_copy(small_i[:, :, 0:1], small[:, :, 1:2]).then_inc(t1, 1)
                dve.wait_ge(t1, 6)
                nc.vector.tensor_scalar(small_i[:, :, 1:2], small_i[:, :, 0:1],
                                        (RUN * P).bit_length() - 1, None, ALU.logical_shift_right).then_inc(t1, 1)
                dve.wait_ge(t1, 7)
                nc.vector.tensor_copy(small[:, :, 2:3], small_i[:, :, 1:2]).then_inc(t2, 1)
                dve.wait_ge(total, 2)
                nc.vector.tensor_copy(small[:, :, 3], misc[0:NT, 0, 0:2]).then_inc(t1, 1)
                dve.wait_ge(t1, 8)
                nc.vector.tensor_tensor(small[:, :, 6:7], small[:, :, 3:4], small[:, :, 2:3], ALU.add)
                nc.vector.tensor_scalar(small[:, :, 5:6], small[:, :, 3:4], float(RUN * P), None,
                                        ALU.mult).then_inc(t1, 1)
                dve.wait_ge(t1, 9)
                nc.vector.tensor_scalar(small[:, :, 4:5], small[:, :, 6:7], float(RUN), None, ALU.mult)
                for k in range(2):
                    nc.vector.tensor_tensor(incl[:, k, :], incl[:, k, :], count[k][:, 1, :],
                                            ALU.subtract).then_inc(t1, 1)
                dve.wait_ge(t1, 11)
                for k in range(2):
                    nc.vector.tensor_scalar(starts[k][:], incl[:, k, :], small[:, k, 5:6], None,
                                            ALU.add)
                for k in range(2):
                    if k:
                        dve.wait_ge(total, 3)
                    nc.vector.tensor_scalar(past[:], c["iota"][0:NT, :], small[:, k, 4:5], None,
                                            ALU.is_ge).then_inc(ended, 1)
                    dve.wait_ge(total, 3 + k)
                    nc.vector.tensor_scalar(c["block_f"][k][:], misc[:, k, 0:ST], float(NT - 1), None,
                                            ALU.min).then_inc(t1, 1)
                    dve.wait_ge(t1, 12 + k)
                    nc.vector.tensor_copy(c["block_i"][k][:], c["block_f"][k][:])
                nc.vector.tensor_copy(degree[:], misc[:, 0, 500 - NT:500])

            @block.tensor
            def _(pe):
                pe.wait_ge(blank_made, 4)
                for k in range(2):
                    nc.tensor.matmul(hist[:, k, 0:P], zero[:, 0:NT], zero[:], start=True, stop=False)
                with nc.tensor.Fori(0, NCH) as it:
                    for k in range(2):
                        pe.wait_ge(hot[k], it + 1)
                        for j in range(CH):
                            last = nc.tensor.matmul(hist[:, k, 0:P], hot_hi[k][:, j, :], hot_lo[k][:, j, :],
                                                    start=False, stop=False)
                        last.then_inc(counted[k], 1)
                for k in range(2):
                    last = nc.tensor.matmul(hist[:, k, 0:P], zero[:, 0:NT], zero[:], start=False, stop=True)
                last.then_inc(total, 1)
                pe.wait_ge(t2, 1)
                nc.tensor.matmul(misc[0:NT, 0, 0:2], c["before_row"][0:NT, 0:NT], small[:, :, 2],
                                 start=True, stop=True).then_inc(total, 1)
                pe.wait_ge(t1, 8)
                nc.tensor.transpose(misc[:, 0, 500 - NT:500], count[0][:, 1, :], c["ident"][0:NT, 0:NT])
                for k in range(2):
                    pe.wait_ge(ended, k + 1)
                    nc.tensor.matmul(misc[:, k, 0:ST], c["ones"][0:NT, :], past[:],
                                     start=True, stop=True).then_inc(total, 1)

        row = [ph.sb(f"row{k}", [P, CH * P], I32) for k in range(2)]
        row_in = ph.sems("row_in", 2)
        hot2 = ph.sems("hot2_", 2)
        turned = ph.sems("turned", 2)
        spread = ph.sems("spread", 2)
        hist_done = ph.sems("hist_done", 2)
        running = ph.sems("running", 2)
        looked = ph.sems("looked", 2)
        ranked = ph.sems("ranked", 2)
        s1, s2 = ph.sems("s1_", 2), ph.sems("s2_", 2)
        placed = ph.sems("placed", 2)
        ringed = ph.sems("ringed", 2)
        scattered = ph.gather_sems(2)
        started, released = ph.sem("started"), ph.sem("released")
        turn_hi = [ph.sb(f"turn_hi{k}", [NT, CH * P]) for k in range(2)]
        junk = ph.sb("junk", [P, CH * P], BF16)
        junk2 = ph.sb("junk2", [P, CH * P], BF16)
        rank = [ph.sb(f"rank{k}", [P, CH]) for k in range(2)]
        seen = [ph.sb(f"seen{k}", [P, CH]) for k in range(2)]
        pos = [ph.sb(f"pos{k}", [P, CH]) for k in range(2)]
        pos_i = [ph.sb(f"pos_i{k}", [P, CH, 3], I32) for k in range(2)]
        rows = [ph.sb(f"rows{k}", [P, CH], I32) for k in range(2)]
        ring = [ph.sb(f"ring{k}", [P, CH, PW]) for k in range(2)]
        hist8 = ph.ps("hist8", [NT, CH * P])
        look = ph.ps("look", [P, CH * P])
        turn = ph.ps("turn", [NT, CH * P], BF16)
        block = ph.block()

        @block.sync
        def _(sp):
            with nc.sync.Fori(0, NCH) as it:
                for k in range(2):
                    sp.wait_ge(ranked[k], it)
                    sp.dma_start(row[k][:], io[keys[k] + "_r"][ds(it * (CH * P), CH * P)]
                                 .partition_broadcast(P)).then_inc(row_in[k], 16)

        @block.vector
        def _(dve):
            def make_hot(n, k):
                dve.wait_ge(hist_done[k], n)
                dve.wait_ge(s1[k], n)
                nc.vector.tensor_tensor(
                    hot_hi[k][:], i25.unsqueeze(1).to_broadcast([P, CH, NT]),
                    hi[k][:, ds(n * CH, CH)].unsqueeze(2).to_broadcast([P, CH, NT]), ALU.is_equal)
                nc.vector.tensor_tensor(
                    hot_lo[k][:], i128.unsqueeze(1).to_broadcast([P, CH, P]),
                    lo[k][:, ds(n * CH, CH)].unsqueeze(2).to_broadcast([P, CH, P]),
                    ALU.is_equal).then_inc(hot2[k], 1)

            def rank_in_tile(n, k):
                dve.wait_ge(row_in[k], n * 16 + 16)
                for j in range(CH):
                    last = nc.vector.scalar_tensor_tensor(
                        junk[:, j * P:(j + 1) * P], row[k][:, j * P:(j + 1) * P], key[k][:, ds(n * CH + j, 1)],
                        c["before_col"][:], ALU.is_equal, ALU.mult, accum_out=rank[k][:, j:j + 1])
                last.then_inc(ranked[k], 1)

            def count_on(n, k, j):
                if j == 0:
                    dve.wait_ge(hist_done[k], n + 1)
                else:
                    dve.wait_ge(running[k], n * CH + j)
                nc.vector.tensor_tensor(count[k][:, j + 1, :], count[k][:, j, :],
                                        hist8[:, j * P:(j + 1) * P], ALU.add).then_inc(running[k], 1)

            def look_up(n, k):
                dve.wait_ge(looked[k], n + 1)
                nc.vector.tensor_copy(count[k][:, 0, :], count[k][:, CH, :])
                for j in range(CH):
                    last = nc.vector.scalar_tensor_tensor(
                        junk2[:, j * P:(j + 1) * P], look[:, j * P:(j + 1) * P], 1.0, hot_lo[k][:, j, :],
                        ALU.mult, ALU.mult, accum_out=seen[k][:, j:j + 1])
                last.then_inc(s1[k], 1)

            def place(n, k, step):
                if step == 0:
                    dve.wait_ge(s1[k], n + 1)
                    dve.wait_ge(ranked[k], n + 1)
                    nc.vector.tensor_tensor(pos[k][:], seen[k][:], rank[k][:], ALU.add).then_inc(s2[k], 1)
                elif step == 1:
                    dve.wait_ge(s2[k], n * 4 + 1)
                    nc.vector.tensor_copy(pos_i[k][:, :, 0], pos[k][:]).then_inc(s2[k], 1)
                elif step == 2:
                    dve.wait_ge(s2[k], n * 4 + 2)
                    nc.vector.tensor_scalar(pos_i[k][:, :, 1], pos_i[k][:, :, 0], P - 1, None,
                                            ALU.bitwise_and).then_inc(s2[k], 1)
                elif step == 3:
                    nc.vector.tensor_scalar(pos_i[k][:, :, 2], pos_i[k][:, :, 0], 7, None,
                                            ALU.logical_shift_right).then_inc(s2[k], 1)
                elif step == 4:
                    dve.wait_ge(s2[k], n * 4 + 4)
                    dve.wait_ge(scattered[k], n * (16 * CH))
                    nc.vector.scalar_tensor_tensor(rows[k][:], pos_i[k][:, :, 1], float(ST),
                                                   pos_i[k][:, :, 2], ALU.mult, ALU.add).then_inc(placed[k], 1)

            def finish(n, k, m=None, other=None):
                if other is not None:
                    make_hot(m, other)
                    rank_in_tile(m, other)
                look_up(n, k)
                for j in range(CH):
                    if j < 5:
                        place(n, k, j)
                    if other is not None:
                        count_on(m, other, j)

            for k in range(2):
                nc.vector.tensor_copy(count[k][:, 0, :], starts[k][:]).then_inc(started, 1)
            dve.wait_ge(started, 2)
            make_hot(0, 0)
            rank_in_tile(0, 0)
            for j in range(CH):
                count_on(0, 0, j)
            with nc.vector.Fori(0, NCH - 1) as it:
                finish(it, 0, it, 1)
                finish(it, 1, it + 1, 0)
            finish(NCH - 1, 0, NCH - 1, 1)
            finish(NCH - 1, 1)

        @block.scalar
        def _(act):
            with nc.scalar.Fori(0, NCH) as it:
                for k in range(2):
                    act.wait_ge(turned[k], it + 1)
                    act.wait_ge(looked[k], it)
                    nc.scalar.copy(turn_hi[k][:], turn[:]).then_inc(spread[k], 1)
                    act.wait_ge(scattered[k], it * (16 * CH))
                    nc.scalar.copy(ring[k][:].bitcast(U32).rearrange("p t w -> p (t w)"),
                                   pay[k][:, ds(it * CH, CH), :].bitcast(U32).rearrange("p t w -> p (t w)")
                                   ).then_inc(ringed[k], 1)

        @block.tensor
        def _(pe):
            with nc.tensor.Fori(0, NCH) as it:
                for k in range(2):
                    pe.wait_ge(hot2[k], it + 1)
                    if k:
                        pe.wait_ge(spread[0], it + 1)
                    else:
                        pe.wait_ge(spread[1], it)
                    for j in range(CH):
                        last = nc.tensor.transpose(turn[:, j * P:(j + 1) * P], hot_hi[k][:, j, :],
                                                   c["ident_h"][:])
                    last.then_inc(turned[k], 1)
                    if k:
                        pe.wait_ge(running[0], it * CH + CH)
                    else:
                        pe.wait_ge(running[1], it * CH)
                    for j in range(CH):
                        last = nc.tensor.matmul(hist8[:, j * P:(j + 1) * P], hot_hi[k][:, j, :],
                                                hot_lo[k][:, j, :], start=True, stop=True)
                    last.then_inc(hist_done[k], 1)
                    pe.wait_ge(spread[k], it + 1)
                    pe.wait_ge(running[k], it * CH + CH)
                    if k:
                        pe.wait_ge(s1[0], it + 1)
                    else:
                        pe.wait_ge(s1[1], it)
                    for j in range(CH):
                        last = nc.tensor.matmul(look[:, j * P:(j + 1) * P], turn_hi[k][:, j * P:(j + 1) * P],
                                                count[k][:, j, :], start=True, stop=True)
                    last.then_inc(looked[k], 1)

        @block.gpsimd
        def _(pool):
            with nc.gpsimd.Fori(0, NCH) as it:
                for k in range(2):
                    pool.wait_ge(placed[k], it + 1)
                    pool.wait_ge(ringed[k], it + 1)
                    pool.sem_inc(released, 1)
                    for j in range(CH):
                        pool.indirect_dma_start(
                            out=slots[k], out_offset=bass.IndirectOffsetOnAxis(
                                ap=rows[k][:, j:j + 1].bitcast(U32), axis=0),
                            in_=ring[k][:, j, :], in_offset=None).then_inc(scattered[k], 16)
            for k in range(2):
                pool.wait_ge(scattered[k], NCH * CH * 16)


def turn_slot_rows(nc, c, slots, lo_rows, key_rows):
    TQ = ST // 4
    with Phase(nc, "turn") as ph:
        loaded, turned, copied, stored = ph.sem("loaded"), ph.sem("turned"), ph.sem("copied"), ph.sem("stored")
        slot = [ph.sb(f"slot{k}", [P, ST, PW]) for k in range(2)]
        word = ph.sb("word", [P, 4, ST])
        out = ph.sb("out", [TQ, 4, 4, P])
        picked = ph.sem("picked")
        pt = ph.ps("pt", [TQ, 4, 4, P])
        block = ph.block()

        @block.sync
        def _(sp):
            for k in range(2):
                sp.dma_start(slot[k][:], slots[k].rearrange("(p t) w -> p t w", t=ST)).then_inc(loaded, 16)
            for n in range(4):
                sp.wait_ge(copied, n + 1)
                dst = (lo_rows, key_rows)[n % 2][n // 2]
                sp.dma_start(dst.rearrange("(q t e) -> t q e", q=4, e=P), out[:, n, :, :]).then_inc(stored, 16)
            sp.wait_ge(stored, 64)

        @block.vector
        def _(dve):
            dve.wait_ge(loaded, 32)
            for n in range(4):
                nc.vector.tensor_copy(word[:, n, :], slot[n // 2][:, :, (LO, KEY)[n % 2]]).then_inc(picked, 1)

        @block.tensor
        def _(pe):
            for n in range(4):
                pe.wait_ge(picked, n + 1)
                for q in range(4):
                    last = nc.tensor.transpose(pt[:, n, q, :], word[:, n, q * TQ:(q + 1) * TQ], c["ident"][:])
                last.then_inc(turned, 1)

        @block.scalar
        def _(act):
            for n in range(4):
                act.wait_ge(turned, n + 1)
                nc.scalar.copy(out[:, n, :, :], pt[:, n, :, :]).then_inc(copied, 1)


def layernorm_stats(nc, c, name, src, update=None):
    with Phase(nc, name) as ph:
        st = ph.sb("st", [P, NT, 6])
        d = ph.sb("d", [P, NT])
        v = ph.sb("v", [P, NT])
        w = ph.sb("w", [P, NT])
        sd = ph.sb("sd", [P, NT])
        counted, step, rooted, updated = (ph.sem(k) for k in ("counted", "step", "rooted", "updated"))
        block = ph.block()

        @block.vector
        def _(dve):
            if update:
                for i in range(NT):
                    update(i).then_inc(updated, 1)
            for i in range(NT):
                if update:
                    dve.wait_ge(updated, i + 1)
                last = nc.vector.bn_stats(st[:, i, :], src[:, i, :])
            last.then_inc(counted, 1)
            dve.wait_ge(counted, 1)
            nc.vector.tensor_tensor(d[:], st[:, :, 1], st[:, :, 4], ALU.subtract)
            nc.vector.tensor_tensor(v[:], st[:, :, 2], st[:, :, 5], ALU.add)
            nc.vector.tensor_tensor(w[:], st[:, :, 1], st[:, :, 4], ALU.add).then_inc(step, 1)
            dve.wait_ge(step, 1)
            nc.vector.tensor_scalar(c["mean"][:], w[:], 0.5, None, ALU.mult)
            nc.vector.scalar_tensor_tensor(d[:], d[:], 0.25, d[:], ALU.mult, ALU.mult).then_inc(step, 1)
            dve.wait_ge(step, 2)
            nc.vector.scalar_tensor_tensor(v[:], v[:], 1.0 / D, d[:], ALU.mult, ALU.add).then_inc(step, 1)
            dve.wait_ge(rooted, 1)
            nc.vector.reciprocal(c["rstd"][:], sd[:])

        @block.scalar
        def _(act):
            act.wait_ge(step, 3)
            nc.scalar.activation(sd[:], v[:], ACT.Sqrt, bias=c["eps"][:]).then_inc(rooted, 1)


class Group:

    BANKS = 3

    def __init__(self, ph, c, src, name="g", pT=None, scale=None, ahead=None):
        self.nc, self.c, self.src, self.scale, self.ahead = ph.nc, c, src, scale, ahead
        self.xn = ph.sb(name + "_xn", [P, GT, D])
        self.xT = ph.sb(name + "_xT", [P, D // P, GR])
        self.pT = ph.ps(name + "_pT", [P, 3, 512]) if pT is None else pT
        self.normed, self.turned = ph.sem(name + "_normed"), ph.sem(name + "_turned")
        self.ready, self.used = ph.sem(name + "_ready"), ph.sem(name + "_used")

    def normalise(self, dve, it):
        dve.wait_ge(self.turned, it * self.BANKS)
        for j in range(GT):
            i = it * GT + j
            row = self.src[:, ds(i, 1), 0:D].rearrange("p a b -> p (a b)")
            if self.scale is None:
                last = self.nc.vector.tensor_scalar(self.xn[:, j, :], row, self.c["mean"][:, ds(i, 1)],
                                                    self.c["rstd"][:, ds(i, 1)], ALU.subtract, ALU.mult)
            else:
                last = self.nc.vector.tensor_scalar(self.xn[:, j, :], row, self.scale[:, ds(i, 1)], None,
                                                    ALU.mult)
        last.then_inc(self.normed, 1)

    def turn(self, pe, it):
        pe.wait_ge(self.normed, it + 1)
        pe.wait_ge(self.ready, it * self.BANKS)
        if self.ahead:
            pe.wait_ge(self.ahead.ready, (it + 1) * self.BANKS)
        for b in range(self.BANKS):
            for j in range(2 * b, min(2 * b + 2, GT)):
                for h in range(2):
                    col = (j % 2) * D + h * P
                    last = self.nc.tensor.transpose(self.pT[:, b, col:col + P], self.xn[:, j, h * P:(h + 1) * P],
                                                    self.c["ident"][:])
            last.then_inc(self.turned, 1)

    def copy(self, act, it):
        for b in range(self.BANKS):
            act.wait_ge(self.turned, it * self.BANKS + b + 1)
            if b == 0:
                act.wait_ge(self.used, it)
            n = 2 if b < 2 else 1
            self.nc.scalar.copy(
                self.xT[:, :, 2 * b * P:(2 * b + n) * P].rearrange("p h (j r) -> p j h r", r=P),
                self.pT[:, b, 0:n * D].rearrange("p (j h r) -> p j h r", h=2, r=P)).then_inc(self.ready, 1)


def rowof(t, i):
    return t[:, ds(i, 1), :].rearrange("p a b -> p (a b)")


def attention_inputs(nc, c, io, X, q_rows, kv_table):
    with Phase(nc, "qkv") as ph:
        g = Group(ph, c, X)
        w = ph.sb("w", [P, 2, 4 * D])
        bias = ph.sb("bias", [P, 4 * D])
        kv = ph.sb("kv", [P, GT, 2 * D])
        prod = ph.ps("prod", [P, 2, 4 * D])
        loaded, done, moved = ph.sem("loaded"), ph.sem("done"), ph.sem("moved")
        evac = ph.sem("evac")
        stored = ph.sems("stored", GT)
        block = ph.block()

        @block.sync
        def _(sp):
            sp.dma_start(w[:], io["W0"].rearrange("(h p) n -> p h n", p=P)).then_inc(loaded, 16)
            sp.dma_start(bias[:], io["b0"].partition_broadcast(P)).then_inc(loaded, 16)
            with nc.sync.Fori(0, NG) as it:
                for j in range(GT):
                    sp.wait_ge(evac, it * GT + j + 1)
                    sp.dma_start(kv_table[ds((it * GT + j) * P, P), :], kv[:, j, :]).then_inc(stored[j], 16)
            for j in range(GT):
                sp.wait_ge(stored[j], 16 * NG)

        @block.vector
        def _(dve):
            dve.wait_ge(loaded, 32)
            g.normalise(dve, 0)

            def group(it, more):
                if more:
                    g.normalise(dve, it + 1)
                for j in range(GT):
                    i = it * GT + j
                    dve.wait_ge(done, i + 1)
                    nc.vector.tensor_tensor(rowof(q_rows, i), prod[:, j % 2, D:2 * D], bias[:, D:2 * D], ALU.add)
                    dve.wait_ge(stored[j], it * 16)
                    nc.vector.tensor_tensor(kv[:, j, :], prod[:, j % 2, 2 * D:], bias[:, 2 * D:],
                                            ALU.add)
                    nc.vector.tensor_tensor(rowof(X, i), rowof(X, i), bias[:, 0:D], ALU.add).then_inc(moved, 1)
                    dve.wait_ge(moved, i + 1)
                    nc.vector.tensor_tensor(rowof(X, i), rowof(X, i), prod[:, j % 2, 0:D],
                                            ALU.add).then_inc(evac, 1)

            with nc.vector.Fori(0, NG - 1) as it:
                group(it, True)
            group(NG - 1, False)

        @block.scalar
        def _(act):
            with nc.scalar.Fori(0, NG) as it:
                g.copy(act, it)

        @block.tensor
        def _(pe):
            pe.wait_ge(loaded, 32)
            with nc.tensor.Fori(0, NG) as it:
                g.turn(pe, it)
                for j in range(GT):
                    pe.wait_ge(g.ready, it * g.BANKS + j // 2 + 1)
                    pe.wait_ge(evac, it * GT + max(j - 1, 0))
                    for half in range(2):
                        for h in range(2):
                            last = nc.tensor.matmul(prod[:, j % 2, half * 512:(half + 1) * 512],
                                                    g.xT[:, h, j * P:(j + 1) * P],
                                                    w[:, h, half * 512:(half + 1) * 512],
                                                    start=(h == 0), stop=(h == 1))
                    last.then_inc(done, 1)
                pe.wait_ge(done, it * GT + GT)
                pe.sem_inc(g.used, 1)


def attention_scores(nc, c, slots, lo_rows, q_rows, kv_table, v_stream, scores, blocks):
    H, DH, R = 8, D // 8, 4
    last_round = NU // R - 1
    with Phase(nc, "score") as ph:
        slot = ph.sb("slot", [P, ST + R * U, PW])
        lo_row = ph.sb("lo_row", [1, R, U * P])
        hotT = ph.sb("hotT", [P, R, U, P])
        idx = ph.sb("idx", [P, R, U], I32)
        kv = ph.sb("kv", [P, R, U, 2 * D])
        prod = ph.sb("prod", [P, 2, U, D])
        q = [ph.ps(f"q{u}", [P, U, D]) for u in range(2)]
        every = [ph.ps(f"every{u}", [P, U * P]) for u in range(2)]
        spread = ph.sems("spread", R)
        loaded, blanked, released = ph.sem("loaded"), ph.sem("blanked"), ph.sem("released")
        row_in, picked, hot = ph.sems("row_in", R), ph.sems("picked", R), ph.sems("hot", R)
        gathered, asked, mult = ph.gather_sems(R), ph.sems("asked", R), ph.sems("mult", R)
        streamed, summed = ph.sems("streamed", R), ph.sems("summed", 2)
        block = ph.block()

        @block.sync
        def _(sp):
            def fetch_row(start, u):
                sp.dma_start(lo_row[:, u, :], lo_rows[ds(start, U * P)].unsqueeze(0)).then_inc(row_in[u], 16)

            def stream(n, u):
                sp.wait_ge(gathered[u], (n + 1) * (16 * U))
                sp.dma_start(v_stream[:, ds((n * R + u) * U, U), :], kv[:, u, :, D:]).then_inc(streamed[u], 16)

            sp.dma_start(slot[:, 0:ST, :], slots.rearrange("(p t) w -> p t w", t=ST)).then_inc(loaded, 16)
            for u in range(R):
                fetch_row(u * (U * P), u)
            with nc.sync.Fori(0, last_round) as it:
                for u in range(R):
                    sp.wait_ge(spread[u], it + 1)
                    fetch_row(it * (R * U * P) + (R + u) * (U * P), u)
                    stream(it, u)
            for u in range(R):
                stream(last_round, u)
            for u in range(R):
                sp.wait_ge(streamed[u], 16 * (NU // R))

        @block.scalar
        def _(act):
            def pick(n, u):
                nc.scalar.copy(idx[:, u, :].bitcast(U32), slot[:, ds((n * R + u) * U, U), OTHER].bitcast(U32)
                               ).then_inc(picked[u], 1)

            act.wait_ge(loaded, 16)
            act.wait_ge(blanked, 1)
            for u in range(R):
                pick(0, u)
            with nc.scalar.Fori(0, NU // R) as it:
                for u in range(R):
                    act.wait_ge(gathered[u], (it + 1) * (16 * U))
                    pick(it + 1, u)

        @block.gpsimd
        def _(pool):
            with nc.gpsimd.Fori(0, NU // R) as it:
                for u in range(R):
                    pool.wait_ge(picked[u], it + 1)
                    pool.wait_ge(mult[u], it)
                    pool.wait_ge(streamed[u], it * 16)
                    pool.sem_inc(released, 1)
                    for j in range(U):
                        pool.indirect_dma_start(
                            out=kv[:, u, j, :], out_offset=None, in_=kv_table,
                            in_offset=bass.IndirectOffsetOnAxis(ap=idx[:, u, j:j + 1].bitcast(U32), axis=0)
                        ).then_inc(gathered[u], 16)

        @block.vector
        def _(dve):
            def make_hot(n, u):
                dve.wait_ge(spread[u], n + 1)
                dve.wait_ge(asked[u], n)
                nc.vector.tensor_scalar(hotT[:, u, :, :].rearrange("p a b -> p (a b)"), every[u % 2][:],
                                        c["iota_p"][:], None, ALU.is_equal).then_inc(hot[u], 1)

            def score(n, u, hot_next=None):
                dve.wait_ge(gathered[u], (n + 1) * (16 * U))
                dve.wait_ge(asked[u], n + 1)
                dve.wait_ge(summed[u % 2], n * (R // 2) + u // 2)
                nc.vector.tensor_tensor(prod[:, u % 2, :, :], kv[:, u, :, 0:D], q[u % 2][:], ALU.mult
                                        ).then_inc(mult[u], 1)
                if hot_next:
                    make_hot(*hot_next)
                dve.wait_ge(mult[u], n + 1)
                nc.vector.tensor_reduce(
                    scores[:, ds((n * R + u) * (U * H), U * H)],
                    prod[:, u % 2, :, :].rearrange("p j (h d) -> p (j h) d", d=DH), AXX, ALU.add
                ).then_inc(summed[u % 2], 1)

            dve.wait_ge(loaded, 16)
            nc.vector.memset(slot[:, ST:, :], 0.0).then_inc(blanked, 1)
            make_hot(0, 0)
            make_hot(0, 1)
            with nc.vector.Fori(0, last_round) as it:
                for u in range(R):
                    score(it, u, (it + (u + 2) // R, (u + 2) % R))
            for u in range(R):
                score(last_round, u, (last_round, u + 2) if u + 2 < R else None)

        @block.tensor
        def _(pe):
            def spread_row(n, u, free=True):
                pe.wait_ge(row_in[u], n * 16 + 16)
                if free:
                    pe.wait_ge(hot[(u + 2) % R], n + u // 2)
                nc.tensor.matmul(every[u % 2][:], c["ones"][0:1, :], lo_row[:, u, :], start=True, stop=True
                                 ).then_inc(spread[u], 1)

            def ask(n, u, following=None):
                if following:
                    spread_row(*following)
                nb = load_blocks(nc.tensor, blocks, n * R + u)
                pe.wait_ge(hot[u], n + 1)
                pe.wait_ge(mult[(u + 2) % R], n + u // 2)
                for j in range(U):
                    last = nc.tensor.matmul(q[u % 2][:, j, :], hotT[:, u, j, :], rowof(q_rows, nb[j // RUN]),
                                            start=True, stop=True)
                last.then_inc(asked[u], 1)

            for u in range(2):
                spread_row(0, u, free=False)
            with nc.tensor.Fori(0, last_round) as it:
                for u in range(R):
                    ask(it, u, (it + (u + 2) // R, (u + 2) % R))
            for u in range(R):
                ask(last_round, u, (last_round, u + 2) if u + 2 < R else None)


def load_blocks(eng, blocks, unit):
    return [eng.value_load(blocks[0:1, ds(unit * U + j, 1)], min_val=0, max_val=NT - 1)
            for j in range(0, U, RUN)]


def segment_softmax(nc, c, name, H, scale, key_rows, scores):
    J = P // H
    G = ST // J
    L = G * P
    R = ST // (P // 4)
    S = G // R
    with Phase(nc, name) as ph:
        sc = ph.sb("sc", [P, L])
        key = ph.sb("key", [P, L])
        neg = ph.sb("neg", [P, L + 1])
        top = ph.sb("top", [P, L])
        tin = ph.sb("tin", [P, S, P])
        j_sel, h_sel = ph.sb("j_sel", [P, J]), ph.sb("h_sel", [P, P])
        ints = ph.sb("ints", [P, 2, P + 2], I32)
        flt = ph.sb("flt", [P, P + 2])
        ends = ph.sb("ends", [P, 4])
        each = ph.sb("each", [P, 4, J])
        every = ph.sb("every", [P, 4, J])
        cand = ph.sb("cand", [P, 2, 2 * J])
        best = ph.sb("best", [P, 2])
        pt = [ph.ps(f"pt{s}", [P, P]) for s in range(S)]
        pall = ph.ps("pall", [P, 4 * J])
        loaded = ph.sem("loaded")
        picked, turned, copied = ph.sem("picked"), ph.sem("turned"), ph.sem("copied")
        step, spread = ph.sem("step"), ph.sem("spread")
        raised, back, written = ph.sem("raised"), ph.sem("back"), ph.sem("written")
        by_stretch = scores[:].rearrange("p (j g h) -> p g j h", g=G, h=H)
        block = ph.block()

        @block.sync
        def _(sp):
            sp.dma_start(key[:],
                         key_rows.rearrange("(j l) -> j l", l=L).unsqueeze(1).to_broadcast([J, H, L])
                         ).then_inc(loaded, 16)

        @block.vector
        def _(dve):
            with nc.vector.Fori(0, R) as it:
                for s in range(S):
                    dve.wait_ge(turned, it * S + max(s + 1 - S, 0))
                    nc.vector.tensor_copy(
                        tin[:, s, :].rearrange("p (j h) -> p j h", h=H),
                        by_stretch[:, ds(it * S + s, 1), :, :].rearrange("p g j h -> p (g j) h")
                    ).then_inc(picked, 1)
            nc.vector.tensor_copy(ints[:, 0, 0:P], c["iota"][:, 0:P])
            nc.vector.tensor_copy(ints[:, 0, P:P + 1], c["iota_p"][:]).then_inc(step, 1)
            dve.wait_ge(step, 1)
            nc.vector.tensor_scalar(ints[:, 1, 0:P + 1], ints[:, 0, 0:P + 1], H - 1, None, ALU.bitwise_and).then_inc(step, 1)
            nc.vector.tensor_scalar(ints[:, 1, P + 1:P + 2], ints[:, 0, P:P + 1], H.bit_length() - 1, None,
                                    ALU.logical_shift_right).then_inc(step, 1)
            dve.wait_ge(step, 3)
            nc.vector.tensor_copy(flt[:], ints[:, 1, :]).then_inc(step, 1)
            dve.wait_ge(step, 4)
            nc.vector.tensor_scalar(h_sel[:], flt[:, 0:P], flt[:, P:P + 1], None, ALU.is_equal)
            nc.vector.tensor_scalar(j_sel[:], c["iota"][:, 0:J], flt[:, P + 1:P + 2], None, ALU.is_equal)
            dve.wait_ge(loaded, 16)
            nc.vector.memset(neg[:, 0:1], -BIG)
            nc.vector.memset(neg[:, L:L + 1], -BIG)
            nc.vector.tensor_tensor(neg[:, 1:L], key[:, 1:L], key[:, 0:L - 1], ALU.not_equal).then_inc(step, 1)
            dve.wait_ge(step, 5)
            nc.vector.tensor_scalar(neg[:, 1:L], neg[:, 1:L], -BIG, None, ALU.mult).then_inc(step, 1)
            dve.wait_ge(step, 6)
            dve.wait_ge(copied, G)
            nc.vector.tensor_tensor_scan(top[:], neg[:, 0:L], sc[:], -BIG, ALU.add, ALU.max).then_inc(step, 1)
            dve.wait_ge(step, 7)
            nc.vector.tensor_tensor_scan(top[:, ::-1], neg[:, L:0:-1], top[:, ::-1], -BIG, ALU.add, ALU.max
                                         ).then_inc(step, 1)
            dve.wait_ge(step, 8)
            nc.vector.tensor_copy(ends[:, 0:1], key[:, 0:1])
            nc.vector.tensor_copy(ends[:, 1:2], key[:, L - 1:L])
            nc.vector.tensor_copy(ends[:, 2:3], top[:, 0:1])
            nc.vector.tensor_copy(ends[:, 3:4], top[:, L - 1:L]).then_inc(step, 1)
            dve.wait_ge(step, 9)
            for n in range(4):
                nc.vector.tensor_scalar(each[:, n, :], j_sel[:], ends[:, n:n + 1], None, ALU.mult
                                        ).then_inc(step, 1)
            dve.wait_ge(spread, 1)
            nc.vector.tensor_copy(every[:].rearrange("p a j -> p (a j)"), pall[:]).then_inc(step, 1)
            dve.wait_ge(step, 14)
            for n in range(2):
                nc.vector.tensor_scalar(cand[:, n, :], every[:, 0:2, :].rearrange("p a j -> p (a j)"),
                                        ends[:, n:n + 1], -BIG, ALU.not_equal, ALU.mult).then_inc(step, 1)
            for n in range(2):
                dve.wait_ge(step, 15 + n)
                nc.vector.tensor_tensor(cand[:, n, :], cand[:, n, :],
                                        every[:, 2:4, :].rearrange("p a j -> p (a j)"), ALU.add
                                        ).then_inc(step, 1)
            dve.wait_ge(step, 18)
            nc.vector.tensor_reduce(best[:], cand[:], AXX, ALU.max).then_inc(step, 1)
            dve.wait_ge(step, 19)
            for n in range(2):
                nc.vector.tensor_scalar(neg[:, 0:L], key[:], ends[:, n:n + 1], -BIG, ALU.not_equal, ALU.mult
                                        ).then_inc(step, 1)
                dve.wait_ge(step, 20 + 2 * n)
                nc.vector.scalar_tensor_tensor(top[:], neg[:, 0:L], best[:, n:n + 1], top[:], ALU.add, ALU.max
                                               ).then_inc(step, 1)
                dve.wait_ge(step, 21 + 2 * n)
            nc.vector.tensor_tensor(sc[:], sc[:], top[:], ALU.subtract).then_inc(step, 1)
            with nc.vector.Fori(0, R) as it:
                for s in range(S):
                    dve.wait_ge(back, it * S + s + 1)
                    nc.vector.tensor_copy(
                        by_stretch[:, ds(it * S + s, 1), :, :].rearrange("p g j h -> p (g j) h"),
                        pt[s][:].rearrange("p (j h) -> p j h", h=H)).then_inc(written, 1)

        @block.tensor
        def _(pe):
            with nc.tensor.Fori(0, R) as it:
                for s in range(S):
                    pe.wait_ge(picked, it * S + s + 1)
                    pe.wait_ge(copied, it * S + max(s + 1 - S, 0))
                    nc.tensor.transpose(pt[s][:], tin[:, s, :], c["ident"][:]).then_inc(turned, 1)
            pe.wait_ge(step, 13)
            nc.tensor.matmul(pall[:], h_sel[:], each[:].rearrange("p a j -> p (a j)"), start=True, stop=True
                             ).then_inc(spread, 1)
            with nc.tensor.Fori(0, R) as it:
                for s in range(S):
                    pe.wait_ge(raised, it * S + s + 1)
                    pe.wait_ge(written, it * S + max(s + 1 - S, 0))
                    nc.tensor.transpose(pt[s][:], tin[:, s, :], c["ident"][:]).then_inc(back, 1)

        @block.scalar
        def _(act):
            with nc.scalar.Fori(0, R) as it:
                for s in range(S):
                    act.wait_ge(turned, it * S + s + 1)
                    nc.scalar.copy(sc[:, ds((it * S + s) * P, P)], pt[s][:]).then_inc(copied, 1)
            act.wait_ge(step, 24)
            with nc.scalar.Fori(0, R) as it:
                for s in range(S):
                    act.wait_ge(back, it * S + max(s + 1 - S, 0))
                    nc.scalar.activation(tin[:, s, :], sc[:, ds((it * S + s) * P, P)], ACT.Exp, scale=scale
                                         ).then_inc(raised, 1)


def attention_values(nc, c, name, slots, v_stream, ex, blocks, agg, H, VW):
    W = D + H
    R = 4
    with Phase(nc, name) as ph:
        slot = ph.sb("slot", [P, ST, PW])
        hot = ph.sb("hot", [P, R, U, P])
        v = ph.sb("v", [P, R, U, D])
        msg = ph.sb("msg", [P, R, U, W])
        out = [ph.ps(f"out{u}", [P, U // RUN, 512]) for u in range(R)]
        loaded = ph.sem("loaded")
        v_in, made, scaled, tailed = ph.sems("v_in", R), ph.sems("made", R), ph.sems("scaled", R), ph.sems("tailed", R)
        summed, added, cleared = ph.sems("summed", R), ph.sems("added", R), ph.sem("cleared")
        block = ph.block()

        @block.sync
        def _(sp):
            sp.dma_start(slot[:], slots.rearrange("(p t) w -> p t w", t=ST)).then_inc(loaded, 16)
            with nc.sync.Fori(0, NU // R) as it:
                for u in range(R):
                    sp.wait_ge(scaled[u], it)
                    sp.wait_ge(tailed[u], it)
                    sp.dma_start(v[:, u, :, :], v_stream[:, ds((it * R + u) * U, U), :]).then_inc(v_in[u], 16)

        @block.scalar
        def _(act):
            with nc.scalar.Fori(0, NU // R) as it:
                for u in range(R):
                    act.wait_ge(summed[u], it)
                    last = nc.scalar.copy(
                        msg[:, u, :, VW:VW + H],
                        ex[:, ds((it * R + u) * (U * H), U * H)].rearrange("p (j h) -> p j h", h=H))
                    if VW < D:
                        act.wait_ge(v_in[u], it * 16 + 16)
                        last = nc.scalar.copy(msg[:, u, :, VW + H:W], v[:, u, :, VW:D])
                    last.then_inc(tailed[u], 1)

        @block.gpsimd
        def _(pool):
            with nc.gpsimd.Fori(0, NU // R) as it:
                for u in range(R):
                    pool.wait_ge(summed[u], it)
                    pool.wait_ge(v_in[u], it * 16 + 16)
                    nc.gpsimd.tensor_tensor(
                        msg[:, u, :, 0:VW].rearrange("p j (h d) -> p j h d", h=H),
                        v[:, u, :, 0:VW].rearrange("p j (h d) -> p j h d", h=H),
                        ex[:, ds((it * R + u) * (U * H), U * H)].rearrange("p (j h) -> p j h", h=H)
                        .unsqueeze(3).to_broadcast([P, U, H, VW // H]), ALU.mult).then_inc(scaled[u], 1)

        @block.vector
        def _(dve):
            def make(it, u):
                dve.wait_ge(summed[u], it)
                nc.vector.tensor_tensor(
                    hot[:, u, :, :], c["iota"][:, 0:P].unsqueeze(1).to_broadcast([P, U, P]),
                    slot[:, ds((it * R + u) * U, U), LO].unsqueeze(2).to_broadcast([P, U, P]),
                    ALU.is_equal).then_inc(made[u], 1)

            def add(it, u, following=None):
                nb = load_blocks(nc.vector, blocks, it * R + u)
                dve.wait_ge(summed[u], it + 1)
                for r in range(U // RUN):
                    if r:
                        dve.wait_ge(added[u], it * (U // RUN) + r)
                    else:
                        dve.wait_ge(added[u - 1], (it + min(u, 1)) * (U // RUN))
                    nc.vector.tensor_tensor(agg[:, ds(nb[r], 1), 0:W].rearrange("p a b -> p (a b)"),
                                            agg[:, ds(nb[r], 1), 0:W].rearrange("p a b -> p (a b)"),
                                            out[u][:, r, 0:W], ALU.add).then_inc(added[u], 1)
                    if r == 0 and following:
                        make(*following)

            nc.vector.memset(agg[:], 0.0).then_inc(cleared, 1)
            dve.wait_ge(loaded, 16)
            dve.wait_ge(cleared, 1)
            for u in range(2):
                make(0, u)
            with nc.vector.Fori(0, NU // R - 1) as it:
                for u in range(R):
                    add(it, u, (it + (u + 2) // R, (u + 2) % R))
            for u in range(R):
                add(NU // R - 1, u, (NU // R - 1, u + 2) if u + 2 < R else None)

        @block.tensor
        def _(pe):
            with nc.tensor.Fori(0, NU // R) as it:
                for u in range(R):
                    pe.wait_ge(made[u], it + 1)
                    pe.wait_ge(scaled[u], it + 1)
                    pe.wait_ge(tailed[u], it + 1)
                    pe.wait_ge(added[u], it * (U // RUN))
                    for j in range(U):
                        last = nc.tensor.matmul(out[u][:, j // RUN, 0:W], hot[:, u, j, :], msg[:, u, j, :],
                                                start=(j % RUN == 0), stop=(j % RUN == RUN - 1))
                    last.then_inc(summed[u], 1)


def attention_output(nc, c, io, X, agg):
    H = 8
    with Phase(nc, "attn_out") as ph:
        w = ph.sb("w", [P, 2, D])
        msg = ph.sb("msg", [P, GT, D])
        den = ph.sb("den", [P, NT, H])
        rec = ph.sb("rec", [P, NT, H])
        mT = ph.sb("mT", [P, GT, 2, P])
        pT = ph.ps("pT", [P, GT, 512])
        prod = ph.ps("prod", [P, 3, 512])
        loaded, clipped, recd, made = ph.sem("loaded"), ph.sem("clipped"), ph.sem("recd"), ph.sem("made")
        turned, copied, done, added = ph.sem("turned"), ph.sem("copied"), ph.sem("done"), ph.sem("added")
        block = ph.block()

        @block.sync
        def _(sp):
            sp.dma_start(w[:], io["W0m"].rearrange("(h p) n -> p h n", p=P)).then_inc(loaded, 16)

        @block.vector
        def _(dve):
            nc.vector.tensor_scalar(den[:], agg[:, :, D:D + H], 1e-20, None, ALU.max).then_inc(clipped, 1)
            dve.wait_ge(clipped, 1)
            nc.vector.reciprocal(rec[:], den[:]).then_inc(recd, 1)
            dve.wait_ge(recd, 1)
            with nc.vector.Fori(0, NG) as it:
                dve.wait_ge(turned, it * GT)
                for j in range(GT):
                    i = it * GT + j
                    nc.vector.tensor_tensor(
                        msg[:, j, :].rearrange("p (h d) -> p h d", h=H),
                        agg[:, ds(i, 1), 0:D].rearrange("p a (h d) -> p (a h) d", h=H),
                        rec[:, ds(i, 1), :].rearrange("p a h -> p (a h)").unsqueeze(2)
                        .to_broadcast([P, H, D // H]), ALU.mult).then_inc(made, 1)
                for j in range(GT):
                    i = it * GT + j
                    dve.wait_ge(done, i + 1)
                    nc.vector.tensor_tensor(rowof(X, i), rowof(X, i), prod[:, j % 3, 0:D],
                                            ALU.add).then_inc(added, 1)

        @block.tensor
        def _(pe):
            pe.wait_ge(loaded, 16)
            with nc.tensor.Fori(0, NG) as it:
                for j in range(GT):
                    pe.wait_ge(made, it * GT + j + 1)
                    pe.wait_ge(copied, it * GT + j)
                    for h in range(2):
                        last = nc.tensor.transpose(pT[:, j, h * P:(h + 1) * P], msg[:, j, h * P:(h + 1) * P],
                                                   c["ident"][:])
                    last.then_inc(turned, 1)
                for j in range(GT):
                    pe.wait_ge(copied, it * GT + j + 1)
                    pe.wait_ge(added, it * GT + max(j - 2, 0))
                    for h in range(2):
                        last = nc.tensor.matmul(prod[:, j % 3, 0:D], mT[:, j, h, :], w[:, h, :],
                                                start=(h == 0), stop=(h == 1))
                    last.then_inc(done, 1)

        @block.scalar
        def _(act):
            with nc.scalar.Fori(0, NG) as it:
                for j in range(GT):
                    act.wait_ge(turned, it * GT + j + 1)
                    act.wait_ge(done, it * GT)
                    nc.scalar.copy(mT[:, j, :, :].rearrange("p h r -> p (h r)"), pT[:, j, 0:D]).then_inc(copied, 1)


class Products:

    def __init__(self, ph, jobs, g):
        self.nc, self.jobs = ph.nc, jobs
        self.hp = ph.ps("hp", [P, 4, 512])
        self.yp = [ph.ps("yp", [P, 512])[:, 0:D], g.pT[:, 2, 0:D]]
        self.filled, self.kept = ph.sem("filled"), ph.sem("kept")
        self.done, self.taken = ph.sem("done"), ph.sem("taken")
        self.nt = sum(j["kind"] == "T" for j in jobs)
        self.nr = len(jobs) - self.nt

    def multiply(self, pe, it, before=None):
        t = r = 0
        for job in self.jobs:
            if before:
                before(pe, it, job)
            if job["kind"] == "T":
                pe.wait_ge(self.kept, it * self.nt + max(t - 1, job.get("needs", 0), 0))
                m = job["rows"]
                for half in range(2):
                    out = self.hp[0:m, 2 * (t % 2) + half, 0:HR]
                    terms = job["terms"]
                    for k, (w, x) in enumerate(terms):
                        last = self.nc.tensor.matmul(out, w, x[:, half * HR:(half + 1) * HR],
                                                     start=(k == 0), stop=(k == len(terms) - 1))
                last.then_inc(self.filled, 1)
                t += 1
            else:
                pe.wait_ge(self.taken, it * self.nr + max(r - 1, 0))
                if job.get("needs", 0):
                    pe.wait_ge(self.kept, it * self.nt + job["needs"])
                terms = job["terms"]
                for k, (x, w) in enumerate(terms):
                    last = self.nc.tensor.matmul(self.yp[r % 2], x, w,
                                                 start=(k == 0), stop=(k == len(terms) - 1))
                last.then_inc(self.done, 1)
                r += 1

    def keep(self, act, it, before=None):
        t = 0
        for job in self.jobs:
            if before:
                before(act, it, job)
            if job["kind"] == "T":
                act.wait_ge(self.filled, it * self.nt + t + 1)
                m = job["rows"]
                self.nc.scalar.activation(
                    job["out"].rearrange("p (a b) -> p a b", a=2),
                    self.hp[0:m, 2 * (t % 2):2 * (t % 2) + 2, 0:HR], job["func"],
                    bias=job["bias"], scale=job.get("scale", 1.0)).then_inc(self.kept, 1)
                t += 1

    def take(self, dve, it):
        r = 0
        for job in self.jobs:
            if job["kind"] == "R":
                dve.wait_ge(self.done, it * self.nr + r + 1)
                job["take"](it, self.yp[r % 2]).then_inc(self.taken, 1)
                r += 1


class Gate:

    def __init__(self, ph, c, g, experts, w, bias_row, extra=0):
        self.nc, self.c, self.g, self.n, self.w, self.bias_row = ph.nc, c, g, experts, w, bias_row
        self.lg = ph.sb("gate_lg", [P, GT, experts])
        self.mx = ph.sb("gate_mx", [P, GT])
        self.ex = ph.sb("gate_ex", [P, GT, experts])
        self.sm = ph.sb("gate_sm", [P, GT])
        self.rs = ph.sb("gate_rs", [P, GT])
        self.wt = ph.sb("gate_wt", [P, GT, experts + extra])
        self.wT = ph.sb("gate_wT", [experts + extra, GT, P])
        self.m = experts + extra
        self.logits, self.step = ph.sem("gate_logits"), ph.sem("gate_step")
        self.exped, self.gated = ph.sem("gate_exped"), ph.sem("gate_gated")
        self.turned, self.copied = ph.sem("gate_turned"), ph.sem("gate_copied")

    def bcast(self, t, n=None):
        return t[:].unsqueeze(2).to_broadcast([P, GT, n or self.n])

    def ask(self, pe, it, pr):
        pe.wait_ge(pr.taken, it * pr.nr)
        for j in range(GT):
            for h in range(2):
                last = self.nc.tensor.matmul(pr.yp[0][:, j * self.n:(j + 1) * self.n],
                                             self.g.xT[:, h, j * P:(j + 1) * P], self.w[:, h, :],
                                             start=(h == 0), stop=(h == 1))
        last.then_inc(self.logits, 1)

    def turn(self, pe, it):
        pe.wait_ge(self.gated, it + 1)
        for j in range(GT):
            last = self.nc.tensor.transpose(self.g.pT[0:self.m, j // 4, (j % 4) * P:(j % 4 + 1) * P],
                                            self.wt[:, j, :], self.c["ident"][:])
        last.then_inc(self.turned, 1)

    def before_product(self, pe, it, job):
        if job.get("turns_gate"):
            self.turn(pe, it)
        if job.get("reads_gate"):
            pe.wait_ge(self.copied, it + 1)

    def before_keep(self, act, it, job):
        if job.get("turns_gate"):
            self.copy(act, it)

    def copy(self, act, it):
        act.wait_ge(self.turned, it + 1)
        self.nc.scalar.copy(self.wT[:, 0:4, :].rearrange("e j r -> e (j r)"), self.g.pT[0:self.m, 0, :])
        self.nc.scalar.copy(self.wT[:, 4, :], self.g.pT[0:self.m, 1, 0:P]).then_inc(self.copied, 1)

    STEPS = 5

    def start(self, dve, it, pr, steps):
        nc, s = self.nc, self.step
        base = it * steps
        dve.wait_ge(self.logits, it + 1)
        nc.vector.tensor_tensor(self.lg[:], pr.yp[0][:, 0:GT * self.n].rearrange("p (j e) -> p j e", e=self.n),
                                self.bias_row[:].unsqueeze(1).to_broadcast([P, GT, self.n]), ALU.add).then_inc(s, 1)
        dve.wait_ge(s, base + 1)
        nc.vector.tensor_reduce(self.mx[:], self.lg[:], AXX, ALU.max).then_inc(s, 1)
        dve.wait_ge(s, base + 2)
        nc.vector.tensor_tensor(self.lg[:], self.lg[:], self.bcast(self.mx), ALU.subtract).then_inc(s, 1)
        dve.wait_ge(self.exped, it * (steps > 5) + it + 1)
        nc.vector.tensor_reduce(self.sm[:], self.ex[:], AXX, ALU.add).then_inc(s, 1)
        dve.wait_ge(s, base + 4)
        nc.vector.reciprocal(self.rs[:], self.sm[:]).then_inc(s, 1)
        dve.wait_ge(s, base + 5)

    def exp(self, act, it, steps):
        act.wait_ge(self.step, it * steps + 3)
        self.nc.scalar.activation(self.ex[:], self.lg[:], ACT.Exp).then_inc(self.exped, 1)


def batch_norm_terms(nc, c, name, io, keys, scale, shift, start_loads=None):
    with Phase(nc, name) as ph:
        b, g, be, m, v = (ph.sb(k, list(scale.shape)) for k in ("b", "g", "be", "m", "v"))
        eps = ph.sb("eps", [P, 1])
        loaded, rooted, step, set_ = ph.sem("loaded"), ph.sem("rooted"), ph.sem("step"), ph.sem("set")
        block = ph.block()

        @block.sync
        def _(sp):
            for t, k in zip((b, g, be, m, v), keys):
                sp.dma_start(t[:], io[k]).then_inc(loaded, 16)
            if start_loads:
                start_loads(sp)

        @block.scalar
        def _(act):
            act.wait_ge(set_, 1)
            act.wait_ge(loaded, 80)
            nc.scalar.activation(v[:], v[:], ACT.Sqrt, bias=eps[:]).then_inc(rooted, 1)

        @block.vector
        def _(dve):
            nc.vector.memset(eps[:], BN_EPS).then_inc(set_, 1)
            dve.wait_ge(rooted, 1)
            nc.vector.reciprocal(scale[:], v[:])
            nc.vector.tensor_tensor(b[:], b[:], m[:], ALU.subtract).then_inc(step, 1)
            dve.wait_ge(step, 1)
            nc.vector.tensor_tensor(scale[:], scale[:], g[:], ALU.mult).then_inc(step, 1)
            dve.wait_ge(step, 2)
            nc.vector.tensor_tensor(b[:], b[:], scale[:], ALU.mult).then_inc(step, 1)
            dve.wait_ge(step, 3)
            nc.vector.tensor_tensor(shift[:], b[:], be[:], ALU.add)


def expert_layers(nc, c, io, X):
    NE, M = 8, 2
    with Phase(nc, "moe0") as outer:
        s1, t1, s2, t2 = (outer.sb(k, [P, NE * M]) for k in ("s1", "t1", "s2", "t2"))
        w1, w2, w3 = (outer.sb(k, [P, NE, 2, D]) for k in ("w1", "w2", "w3"))
        weights_in = outer.sem("weights_in")

        def load_weights(sp):
            for t, k in ((w1, "F0W1"), (w2, "F0W2"), (w3, "F0W3")):
                sp.dma_start(t[:].rearrange("p e k n -> p (e k) n"),
                             io[k].rearrange("e (k p) n -> p (e k) n", p=P)).then_inc(weights_in, 16)

        batch_norm_terms(nc, c, "bn1", io, ["F0b1", "F0g1", "F0be1", "F0m1", "F0v1"], s1, t1)
        batch_norm_terms(nc, c, "bn2", io, ["F0b2", "F0g2", "F0be2", "F0m2", "F0v2"], s2, t2, load_weights)
        layernorm_stats(nc, c, "norm1", X)
        with Phase(nc, "moe0_") as ph:
            g = Group(ph, c, X)
            wr, br, bo = ph.sb("wr", [P, 2, NE]), ph.sb("br", [P, NE]), ph.sb("bo", [NE, D])
            h1, h2 = ph.sb("h1", [P, 2, M, GR]), ph.sb("h2", [P, 2, M, GR])
            gate = Gate(ph, c, g, NE, wr, br)
            loaded = ph.sem("loaded")
            jobs = []
            order = [("first", 0)]
            for e in range(NE):
                order += [("first", e + 1)] * (e + 1 < NE) + [("second", e)] + [("out", e - 1)] * (e > 0)
            order += [("out", NE - 1)]

            def take_bias(j):
                return lambda it, y: nc.vector.tensor_tensor(rowof(X, it * GT + j), rowof(X, it * GT + j), y, ALU.add)

            def take_expert(j, e):
                def take(it, y):
                    nc.vector.wait_ge(pr.taken, it * (GT * (NE + 1)) + GT * e + j + 1)
                    return nc.vector.scalar_tensor_tensor(
                        rowof(X, it * GT + j), y, gate.wt[:, j, e:e + 1], rowof(X, it * GT + j), ALU.mult, ALU.add)
                return take

            kept, t = {}, 0
            for what, e in order:
                if (what, e) == ("first", 2):
                    for j in range(GT):
                        jobs.append(dict(kind="R", terms=[(gate.wT[:, j, :], bo[:])], take=take_bias(j),
                                         reads_gate=(j == 0)))
                if what == "out":
                    for j in range(GT):
                        jobs.append(dict(kind="R", needs=kept["second", e], take=take_expert(j, e), terms=[
                            (h2[:, e % 2, k, j * P:(j + 1) * P], w3[:, e, k, :]) for k in range(M)]))
                    continue
                w, x, h, s, b = (w1, g.xT, h1, s1, t1) if what == "first" else (w2, h1, h2, s2, t2)
                for m in range(M):
                    jobs.append(dict(
                        kind="T", rows=P, func=ACT.Relu, out=h[:, e % 2, m, :],
                        needs=kept["first", e] if what == "second" else 0,
                        turns_gate=(what == "second" and e == 0 and m == 1),
                        scale=s[:, e * M + m:e * M + m + 1], bias=b[:, e * M + m:e * M + m + 1],
                        terms=[(w[:, e, k, m * P:(m + 1) * P],
                                g.xT[:, k, :] if what == "first" else h1[:, e % 2, k, :]) for k in range(2)]))
                    t += 1
                kept[what, e] = t
            pr = Products(ph, jobs, g)
            block = ph.block()

            @block.sync
            def _(sp):
                sp.dma_start(wr[:], io["F0Wr"].rearrange("(k p) n -> p k n", p=P)).then_inc(loaded, 16)
                sp.dma_start(br[:], io["F0br"].partition_broadcast(P)).then_inc(loaded, 16)
                sp.dma_start(bo[:], io["F0bo"]).then_inc(loaded, 16)

            @block.vector
            def _(dve):
                dve.wait_ge(loaded, 48)
                g.normalise(dve, 0)

                def group(it, more):
                    gate.start(dve, it, pr, Gate.STEPS)
                    nc.vector.tensor_tensor(gate.wt[:], gate.ex[:], gate.bcast(gate.rs), ALU.mult
                                            ).then_inc(gate.gated, 1)
                    if more:
                        g.normalise(dve, it + 1)
                    dve.wait_ge(gate.gated, it + 1)
                    pr.take(dve, it)

                with nc.vector.Fori(0, NG - 1) as it:
                    group(it, True)
                group(NG - 1, False)

            @block.scalar
            def _(act):
                with nc.scalar.Fori(0, NG) as it:
                    g.copy(act, it)
                    gate.exp(act, it, Gate.STEPS)
                    pr.keep(act, it, gate.before_keep)

            @block.tensor
            def _(pe):
                pe.wait_ge(loaded, 48)
                with nc.tensor.Fori(0, NG) as it:
                    pe.wait_ge(pr.taken, it * pr.nr)
                    g.turn(pe, it)
                    pe.wait_ge(g.ready, (it + 1) * g.BANKS)
                    gate.ask(pe, it, pr)
                    pe.wait_ge(weights_in, 48)
                    pr.multiply(pe, it, gate.before_product)
                    pe.wait_ge(pr.done, (it + 1) * pr.nr)
                    pe.sem_inc(g.used, 1)


def aggregate(nc, c, name, slots, table, blocks, agg, weighted):
    R = 4
    with Phase(nc, name) as ph:
        slot = ph.sb("slot", [P, ST + R * U, PW])
        hot = ph.sb("hot", [P, R, U, P])
        idx = ph.sb("idx", [P, R, U], I32)
        row = ph.sb("row", [P, R, U, D])
        out = [ph.ps(f"out{u}", [P, U // RUN, 512]) for u in range(2)]
        loaded, cleared, released = ph.sem("loaded"), ph.sem("cleared"), ph.sem("released")
        picked, gathered = ph.sems("picked", R), ph.gather_sems(R)
        made, summed, added = ph.sems("made", R), ph.sems("summed", R), ph.sem("added")
        block = ph.block()

        @block.sync
        def _(sp):
            sp.dma_start(slot[:, 0:ST, :], slots.rearrange("(p t) w -> p t w", t=ST)).then_inc(loaded, 16)

        @block.scalar
        def _(act):
            def pick(n, u):
                nc.scalar.copy(idx[:, u, :].bitcast(U32), slot[:, ds((n * R + u) * U, U), OTHER].bitcast(U32)
                               ).then_inc(picked[u], 1)

            act.wait_ge(loaded, 16)
            act.wait_ge(cleared, 2)
            for u in range(R):
                pick(0, u)
            with nc.scalar.Fori(0, NU // R) as it:
                for u in range(R):
                    act.wait_ge(gathered[u], (it + 1) * (16 * U))
                    pick(it + 1, u)

        @block.gpsimd
        def _(pool):
            with nc.gpsimd.Fori(0, NU // R) as it:
                for u in range(R):
                    pool.wait_ge(picked[u], it + 1)
                    pool.wait_ge(summed[u], it)
                    pool.sem_inc(released, 1)
                    for j in range(U):
                        pool.indirect_dma_start(
                            out=row[:, u, j, :], out_offset=None, in_=table,
                            in_offset=bass.IndirectOffsetOnAxis(ap=idx[:, u, j:j + 1].bitcast(U32), axis=0)
                        ).then_inc(gathered[u], 16)

        @block.vector
        def _(dve):
            def make(n, u):
                dve.wait_ge(summed[u], n)
                for j in range(U):
                    t = (n * R + u) * U + j
                    last = nc.vector.tensor_scalar(
                        hot[:, u, j, :], c["iota"][:, 0:P], slot[:, ds(t, 1), LO],
                        slot[:, ds(t, 1), WGT] if weighted else None, ALU.is_equal,
                        ALU.mult if weighted else ALU.bypass)
                last.then_inc(made[u], 1)

            def add(n, u):
                nb = load_blocks(nc.vector, blocks, n * R + u)
                dve.wait_ge(summed[u], n + 1)
                for r in range(U // RUN):
                    dve.wait_ge(added, (n * R + u) * (U // RUN) + r)
                    nc.vector.tensor_tensor(agg[:, ds(nb[r], 1), 0:D].rearrange("p a b -> p (a b)"),
                                            agg[:, ds(nb[r], 1), 0:D].rearrange("p a b -> p (a b)"),
                                            out[u % 2][:, r, 0:D], ALU.add).then_inc(added, 1)

            nc.vector.memset(agg[:], 0.0).then_inc(cleared, 1)
            nc.vector.memset(slot[:, ST:, :], 0.0).then_inc(cleared, 1)
            dve.wait_ge(loaded, 16)
            dve.wait_ge(cleared, 2)
            make(0, 0)
            with nc.vector.Fori(0, NU // R - 1) as it:
                for u in range(R):
                    make(it + (u + 1) // R, (u + 1) % R)
                    add(it, u)
            for u in range(R):
                if u + 1 < R:
                    make(NU // R - 1, u + 1)
                add(NU // R - 1, u)

        @block.tensor
        def _(pe):
            with nc.tensor.Fori(0, NU // R) as it:
                for u in range(R):
                    pe.wait_ge(made[u], it + 1)
                    pe.wait_ge(gathered[u], (it + 1) * (16 * U))
                    pe.wait_ge(added, (it * R + max(u - 1, 0)) * (U // RUN))
                    for j in range(U):
                        last = nc.tensor.matmul(out[u % 2][:, j // RUN, 0:D], hot[:, u, j, :], row[:, u, j, :],
                                                start=(j % RUN == 0), stop=(j % RUN == RUN - 1))
                    last.then_inc(summed[u], 1)


def store_normalised(nc, c, name, X, table):
    with Phase(nc, name) as ph:
        xn = ph.sb("xn", [P, GT, D])
        normed, stored = ph.sem("normed"), ph.sems("stored", GT)
        block = ph.block()

        @block.vector
        def _(dve):
            with nc.vector.Fori(0, NG) as it:
                for j in range(GT):
                    i = it * GT + j
                    dve.wait_ge(stored[j], it * 16)
                    nc.vector.tensor_scalar(xn[:, j, :], rowof(X, i), c["mean"][:, ds(i, 1)],
                                            c["rstd"][:, ds(i, 1)], ALU.subtract, ALU.mult).then_inc(normed, 1)

        @block.sync
        def _(sp):
            with nc.sync.Fori(0, NG) as it:
                for j in range(GT):
                    i = it * GT + j
                    sp.wait_ge(normed, i + 1)
                    sp.dma_start(table[ds(i * P, P), :], xn[:, j, :]).then_inc(stored[j], 16)
            for j in range(GT):
                sp.wait_ge(stored[j], 16 * NG)


def sage_layers(nc, c, io, X, agg, degree, inv_deg, z_table):
    M = 4
    with Phase(nc, "sage") as ph:
        g = Group(ph, c, X)
        m = Group(ph, c, agg, "m", pT=g.pT, scale=inv_deg, ahead=g)
        w1, w2 = ph.sb("w1", [P, 4, M * P]), ph.sb("w2", [P, M, 2 * D])
        b1, b2 = ph.sb("b1", [P, M]), ph.sb("b2", [P, D])
        h = ph.sb("h", [P, M, GR])
        z = ph.sb("z", [P, GT, D])
        loaded, stored, clipped = ph.sem("loaded"), ph.sems("stored", GT), ph.sem("clipped")
        biased = ph.sem("biased")
        jobs = []
        for n in range(M):
            jobs.append(dict(kind="T", rows=P, func=ACT.Relu, out=h[:, n, :], bias=b1[:, n:n + 1], terms=[
                (w1[:, k, n * P:(n + 1) * P], (m, g)[k // 2].xT[:, k % 2, :]) for k in range(4)]))

        def take_z(j):
            def take(it, y):
                nc.vector.wait_ge(stored[j], it * 16)
                return nc.vector.tensor_copy(z[:, j, :], y)
            return take

        def take_x(j):
            def take(it, y):
                nc.vector.wait_ge(biased, it * GT + j + 1)
                return nc.vector.tensor_tensor(rowof(X, it * GT + j), rowof(X, it * GT + j), y, ALU.add)
            return take

        for j in range(GT):
            for n, take in enumerate((take_z(j), take_x(j))):
                jobs.append(dict(kind="R", needs=M, take=take, terms=[
                    (h[:, k, j * P:(j + 1) * P], w2[:, k, n * D:(n + 1) * D]) for k in range(M)]))
        pr = Products(ph, jobs, g)
        block = ph.block()

        @block.sync
        def _(sp):
            sp.dma_start(w1[:], io["S1W1"].rearrange("(k p) n -> p k n", p=P)).then_inc(loaded, 16)
            sp.dma_start(w2[:], io["S1W2"].rearrange("(k p) n -> p k n", p=P)).then_inc(loaded, 16)
            sp.dma_start(b1[:], io["S1b1"]).then_inc(loaded, 16)
            sp.dma_start(b2[:], io["S1b2"].partition_broadcast(P)).then_inc(loaded, 16)
            with nc.sync.Fori(0, NG) as it:
                for j in range(GT):
                    sp.wait_ge(pr.taken, it * pr.nr + 2 * j + 1)
                    sp.dma_start(z_table[ds((it * GT + j) * P, P), :], z[:, j, :]).then_inc(stored[j], 16)
            for j in range(GT):
                sp.wait_ge(stored[j], 16 * NG)

        @block.vector
        def _(dve):
            dve.wait_ge(loaded, 64)
            nc.vector.tensor_scalar(inv_deg[:], degree[:], 1.0, None, ALU.max).then_inc(clipped, 1)
            dve.wait_ge(clipped, 1)
            nc.vector.reciprocal(inv_deg[:], inv_deg[:]).then_inc(clipped, 1)
            dve.wait_ge(clipped, 2)
            g.normalise(dve, 0)
            m.normalise(dve, 0)

            def group(it, more):
                dve.wait_ge(g.normed, it + 1)
                for j in range(GT):
                    nc.vector.tensor_tensor(rowof(X, it * GT + j), rowof(X, it * GT + j), b2[:], ALU.add
                                            ).then_inc(biased, 1)
                if more:
                    g.normalise(dve, it + 1)
                    m.normalise(dve, it + 1)
                pr.take(dve, it)

            with nc.vector.Fori(0, NG - 1) as it:
                group(it, True)
            group(NG - 1, False)

        @block.scalar
        def _(act):
            with nc.scalar.Fori(0, NG) as it:
                g.copy(act, it)
                m.copy(act, it)
                pr.keep(act, it)

        @block.tensor
        def _(pe):
            pe.wait_ge(loaded, 64)
            with nc.tensor.Fori(0, NG) as it:
                pe.wait_ge(pr.taken, it * pr.nr)
                g.turn(pe, it)
                m.turn(pe, it)
                pe.wait_ge(m.ready, (it + 1) * m.BANKS)
                pr.multiply(pe, it)
                pe.wait_ge(pr.done, (it + 1) * pr.nr)
                pe.sem_inc(g.used, 1)
                pe.sem_inc(m.used, 1)


def add_scaled(nc, X, agg, scale):
    return lambda i: nc.vector.scalar_tensor_tensor(X[:, i, :], agg[:, i, 0:D], scale[:, i:i + 1], X[:, i, :],
                                                    ALU.mult, ALU.add)


def choose_tokens(nc, c, io, X, row_dram, chosen):
    TOP = int(0.5 * N) - 1
    LAST = N - (NT - 1) * P
    with Phase(nc, "choose") as ph:
        wr, br = ph.sb("wr", [P, D]), ph.sb("br", [P, 1])
        xn, prod = ph.sb("xn", [P, NT, D]), ph.sb("prod", [P, NT, D])
        rw = ph.sb("rw", [P, NT])
        pad = ph.sb("pad", [P, 1])
        rows = ph.sb("rows", [NT, P])
        every = ph.sb("every", [P, NP])
        junk = ph.sb("junk", [P, 4, NP], BF16)
        part = ph.sb("part", [P, NT, 4])
        rank = ph.sb("rank", [P, NT])
        pt = ph.ps("pt", [NT, P])
        loaded, normed, dotted, step = ph.sem("loaded"), ph.sem("normed"), ph.sem("dotted"), ph.sem("step")
        turned, copied, stored, back = ph.sem("turned"), ph.sem("copied"), ph.sem("stored"), ph.sem("back")
        counted = ph.sem("counted")
        block = ph.block()

        @block.sync
        def _(sp):
            sp.dma_start(wr[:], io["C1wr"].partition_broadcast(P)).then_inc(loaded, 16)
            sp.dma_start(br[:], io["C1br"].partition_broadcast(P)).then_inc(loaded, 16)
            sp.wait_ge(copied, 1)
            sp.dma_start(row_dram.rearrange("(t r) -> t r", r=P), rows[:]).then_inc(stored, 16)
            sp.wait_ge(stored, 16)
            sp.dma_start(every[:], row_dram.partition_broadcast(P)).then_inc(back, 16)

        @block.vector
        def _(dve):
            nc.vector.memset(part[:], 0.0)
            dve.wait_ge(loaded, 32)
            with nc.vector.Fori(0, NT) as i:
                nc.vector.tensor_scalar(rowof(xn, i), rowof(X, i), c["mean"][:, ds(i, 1)],
                                        c["rstd"][:, ds(i, 1)], ALU.subtract, ALU.mult).then_inc(normed, 1)
            dve.wait_ge(normed, NT)
            with nc.vector.Fori(0, NG) as it:
                nc.vector.tensor_tensor(prod[:, ds(it * GT, GT), :], xn[:, ds(it * GT, GT), :],
                                        wr[:].unsqueeze(1).to_broadcast([P, GT, D]), ALU.mult).then_inc(dotted, 1)
            dve.wait_ge(dotted, NG)
            nc.vector.tensor_reduce(rw[:], prod[:], AXX, ALU.add).then_inc(step, 1)
            nc.vector.tensor_scalar(pad[:], c["iota_p"][:], float(LAST), -BIG, ALU.is_ge, ALU.mult
                                    ).then_inc(step, 1)
            dve.wait_ge(step, 2)
            nc.vector.tensor_scalar(rw[:], rw[:], br[:], None, ALU.add).then_inc(step, 1)
            dve.wait_ge(step, 3)
            nc.vector.tensor_tensor(rw[:, NT - 1:NT], rw[:, NT - 1:NT], pad[:], ALU.add).then_inc(step, 1)
            dve.wait_ge(back, 16)
            for t in range(NT):
                w = rw[:, t:t + 1]
                own = slice(t * P, (t + 1) * P)
                if t:
                    dve.wait_ge(counted, t)
                if t:
                    nc.vector.tensor_scalar(junk[:, 0, 0:t * P], every[:, 0:t * P], w, 0.0, ALU.is_ge, ALU.add,
                                            accum_out=part[:, t, 0:1])
                nc.vector.tensor_scalar(junk[:, 1, 0:NP - t * P], every[:, t * P:], w, 0.0, ALU.is_gt, ALU.add,
                                        accum_out=part[:, t, 1:2])
                nc.vector.scalar_tensor_tensor(junk[:, 2, 0:P], every[:, own], w, c["before_col"][:],
                                               ALU.is_equal, ALU.mult, accum_out=part[:, t, 2:3]
                                               ).then_inc(counted, 1)
            dve.wait_ge(counted, NT)
            nc.vector.tensor_reduce(rank[:], part[:], AXX, ALU.add).then_inc(step, 1)
            dve.wait_ge(step, 5)
            nc.vector.scalar_tensor_tensor(chosen[:], rank[:], TOP - 0.5, rw[:], ALU.is_lt, ALU.mult)

        @block.tensor
        def _(pe):
            pe.wait_ge(step, 4)
            nc.tensor.transpose(pt[:], rw[:], c["ident"][:]).then_inc(turned, 1)

        @block.scalar
        def _(act):
            act.wait_ge(turned, 1)
            nc.scalar.copy(rows[:], pt[:]).then_inc(copied, 1)


def chosen_ffn(nc, c, io, X, chosen):
    M = 8
    with Phase(nc, "ffn1") as ph:
        g = Group(ph, c, X)
        w1, w2 = ph.sb("w1", [P, 2, M * P]), ph.sb("w2", [P, M, D])
        b1, b2 = ph.sb("b1", [P, M]), ph.sb("b2", [P, D])
        h = ph.sb("h", [P, M, GR])
        y = ph.sb("y", [P, GT, D])
        loaded, raised, based = ph.sem("loaded"), ph.sem("raised"), ph.sem("based")
        jobs = []
        for n in range(M):
            jobs.append(dict(kind="T", rows=P, func=ACT.Gelu_apprx_tanh, out=h[:, n, :], bias=b1[:, n:n + 1],
                             terms=[(w1[:, k, n * P:(n + 1) * P], g.xT[:, k, :]) for k in range(2)]))

        def take_x(j):
            return lambda it, product: nc.vector.tensor_tensor(y[:, j, :], product, b2[:], ALU.add)

        for j in range(GT):
            jobs.append(dict(kind="R", needs=M, take=take_x(j), terms=[
                (h[:, k, j * P:(j + 1) * P], w2[:, k, :]) for k in range(M)]))
        pr = Products(ph, jobs, g)
        block = ph.block()

        @block.sync
        def _(sp):
            sp.dma_start(w1[:], io["C1W1"].rearrange("(k p) n -> p k n", p=P)).then_inc(loaded, 16)
            sp.dma_start(w2[:], io["C1W2"].rearrange("(k p) n -> p k n", p=P)).then_inc(loaded, 16)
            sp.dma_start(b1[:], io["C1b1"]).then_inc(loaded, 16)
            sp.dma_start(b2[:], io["C1b2"].partition_broadcast(P)).then_inc(loaded, 16)

        @block.vector
        def _(dve):
            dve.wait_ge(loaded, 64)
            def prepare(n):
                g.normalise(dve, n)
                dve.wait_ge(g.normed, n + 1)
                nc.vector.tensor_tensor(X[:, ds(n * GT, GT), :], X[:, ds(n * GT, GT), :], g.xn[:], ALU.add
                                        ).then_inc(based, 1)

            def group(it, more):
                if more:
                    dve.wait_ge(based, it + 1)
                    prepare(it + 1)
                pr.take(dve, it)
                dve.wait_ge(based, it + 1)
                dve.wait_ge(pr.taken, (it + 1) * pr.nr)
                for j in range(GT):
                    row = rowof(X, it * GT + j)
                    nc.vector.scalar_tensor_tensor(row, y[:, j, :], chosen[:, ds(it * GT + j, 1)], row,
                                                   ALU.mult, ALU.add).then_inc(raised, 1)
                dve.wait_ge(raised, (it + 1) * GT)

            prepare(0)
            with nc.vector.Fori(0, NG - 1) as it:
                group(it, True)
            group(NG - 1, False)

        @block.scalar
        def _(act):
            with nc.scalar.Fori(0, NG) as it:
                g.copy(act, it)
                pr.keep(act, it)

        @block.tensor
        def _(pe):
            pe.wait_ge(loaded, 64)
            with nc.tensor.Fori(0, NG) as it:
                pe.wait_ge(pr.taken, it * pr.nr)
                g.turn(pe, it)
                pe.wait_ge(g.ready, (it + 1) * g.BANKS)
                pr.multiply(pe, it)
                pe.wait_ge(pr.done, (it + 1) * pr.nr)
                pe.sem_inc(g.used, 1)


def mixture_ffn(nc, c, io, X):
    NE, K = 4, 2
    EH = 64
    STEPS = 14
    with Phase(nc, "moe2") as ph:
        g = Group(ph, c, X)
        sw1, sw2, sw3 = ph.sb("sw1", [P, 2, 2 * P]), ph.sb("sw2", [P, 2, P]), ph.sb("sw3", [P, D])
        ew1, ew2, ew3 = ph.sb("ew1", [P, NE, 2, P]), ph.sb("ew2", [P, NE, EH]), ph.sb("ew3", [EH, NE, D])
        bias = ph.sb("bias", [P, 3 + NE])
        eb2 = ph.sb("eb2", [EH, NE])
        b3 = ph.sb("b3", [NE + 1, D])
        gw, gb = ph.sb("gw", [P, 2, NE]), ph.sb("gb", [P, NE])
        sh1, sh2 = ph.sb("sh1", [P, 2, GR]), ph.sb("sh2", [P, GR])
        eh1, eh2 = ph.sb("eh1", [P, NE, GR]), ph.sb("eh2", [EH, NE, GR])
        gate = Gate(ph, c, g, NE, gw, gb, extra=1)
        lower, upper = ph.sb("lower", [P, NE, NE]), ph.sb("upper", [P, NE, NE])
        ge, gt = ph.sb("ge", [P, GT, NE, NE]), ph.sb("gt", [P, GT, NE, NE])
        prob = ph.sb("prob", [P, GT, NE])
        sel = ph.sb("sel", [P, GT, NE])
        loaded, masked = ph.sem("loaded"), ph.sem("masked")
        jobs = []

        def T(w, x, out, func, b, needs, rows=P):
            jobs.append(dict(kind="T", rows=rows, func=func, out=out, bias=b, needs=needs,
                             turns_gate=(len(jobs) == 6), terms=list(zip(w, x))))

        for n in range(2):
            T([sw1[:, k, n * P:(n + 1) * P] for k in range(2)], [g.xT[:, k, :] for k in range(2)],
              sh1[:, n, :], ACT.Relu, bias[:, n:n + 1], 0)
        for e in range(NE):
            T([ew1[:, e, k, :] for k in range(2)], [g.xT[:, k, :] for k in range(2)],
              eh1[:, e, :], ACT.Relu, bias[:, 3 + e:4 + e], 0)
        T([sw2[:, k, :] for k in range(2)], [sh1[:, k, :] for k in range(2)], sh2[:], ACT.Relu, bias[:, 2:3], 2)
        for e in range(NE):
            T([ew2[:, e, :]], [eh1[:, e, :]], eh2[:, e, :], ACT.Relu, eb2[:, e:e + 1], 3 + e, rows=EH)

        def take(j, e):
            def f(it, y):
                i = it * GT + j
                if e < 0:
                    return nc.vector.tensor_tensor(rowof(X, i), rowof(X, i), y, ALU.add)
                nc.vector.wait_ge(pr.taken, it * pr.nr + GT * (e + 1) + j + 1 - GT)
                return nc.vector.scalar_tensor_tensor(rowof(X, i), y, gate.wt[:, j, e:e + 1], rowof(X, i),
                                                      ALU.mult, ALU.add)
            return f

        for j in range(GT):
            jobs.append(dict(kind="R", needs=7, take=take(j, -1), reads_gate=(j == 0), terms=[
                (gate.wT[:, j, :], b3[:]), (sh2[:, j * P:(j + 1) * P], sw3[:])]))
        for e in range(NE):
            for j in range(GT):
                jobs.append(dict(kind="R", needs=8 + e, take=take(j, e), terms=[
                    (eh2[:, e, j * P:(j + 1) * P], ew3[:, e, :])]))
        pr = Products(ph, jobs, g)
        block = ph.block()

        @block.sync
        def _(sp):
            sp.dma_start(sw1[:], io["M2sW1"].rearrange("(k p) n -> p k n", p=P)).then_inc(loaded, 16)
            sp.dma_start(sw2[:], io["M2sW2"].rearrange("(k p) n -> p k n", p=P)).then_inc(loaded, 16)
            sp.dma_start(sw3[:], io["M2sW3"]).then_inc(loaded, 16)
            sp.dma_start(ew1[:].rearrange("p e k n -> p (e k) n"),
                         io["M2eW1"].rearrange("e (k p) n -> p (e k) n", p=P)).then_inc(loaded, 16)
            sp.dma_start(ew2[:], io["M2eW2"].rearrange("e p n -> p e n")).then_inc(loaded, 16)
            sp.dma_start(ew3[:], io["M2eW3"].rearrange("e p n -> p e n")).then_inc(loaded, 16)
            sp.dma_start(bias[:], io["M2b"]).then_inc(loaded, 16)
            sp.dma_start(eb2[:], io["M2eb2"]).then_inc(loaded, 16)
            sp.dma_start(b3[:], io["M2b3"]).then_inc(loaded, 16)
            sp.dma_start(gw[:], io["M2gW"].rearrange("(k p) n -> p k n", p=P)).then_inc(loaded, 16)
            sp.dma_start(gb[:], io["M2gb"].partition_broadcast(P)).then_inc(loaded, 16)

        @block.gpsimd
        def _(pool):
            pat = c["ones"][:, 0:NE * NE].rearrange("p (a b) -> p a b", b=NE)
            nc.gpsimd.affine_select(out=lower[:], in_=pat, compare_op=ALU.is_gt, fill=0.0, base=0,
                                    pattern=[[1, NE], [-1, NE]], channel_multiplier=0).then_inc(masked, 1)
            nc.gpsimd.affine_select(out=upper[:], in_=pat, compare_op=ALU.is_gt, fill=0.0, base=0,
                                    pattern=[[-1, NE], [1, NE]], channel_multiplier=0).then_inc(masked, 1)

        @block.vector
        def _(dve):
            dve.wait_ge(loaded, 16 * 11)
            dve.wait_ge(masked, 2)
            nc.vector.memset(gate.wt[:], 1.0)
            s, V = gate.step, nc.vector
            shape = [P, GT, NE, NE]
            g.normalise(dve, 0)

            def group(it, more):
                gate.start(dve, it, pr, STEPS)
                base = it * STEPS
                V.tensor_tensor(prob[:], gate.ex[:], gate.bcast(gate.rs), ALU.mult).then_inc(s, 1)
                dve.wait_ge(s, base + 6)
                mine = prob[:].unsqueeze(3).to_broadcast(shape)
                theirs = prob[:].unsqueeze(2).to_broadcast(shape)
                V.tensor_tensor(ge[:], theirs, mine, ALU.is_ge)
                V.tensor_tensor(gt[:], theirs, mine, ALU.is_gt)
                V.tensor_reduce(gate.mx[:], prob[:], AXX, ALU.max).then_inc(s, 1)
                dve.wait_ge(s, base + 7)
                V.tensor_tensor(ge[:], ge[:], lower[:].unsqueeze(1).to_broadcast(shape), ALU.mult)
                V.tensor_tensor(gt[:], gt[:], upper[:].unsqueeze(1).to_broadcast(shape), ALU.mult)
                V.tensor_tensor(gate.lg[:], prob[:], gate.bcast(gate.mx), ALU.subtract).then_inc(s, 1)
                dve.wait_ge(s, base + 8)
                V.tensor_tensor(ge[:], ge[:], gt[:], ALU.add).then_inc(s, 1)
                dve.wait_ge(s, base + 9)
                V.tensor_reduce(sel[:], ge[:], AXX, ALU.add).then_inc(s, 1)
                dve.wait_ge(s, base + 10)
                dve.wait_ge(gate.exped, it * 2 + 2)
                V.scalar_tensor_tensor(sel[:], sel[:], K - 0.5, gate.ex[:], ALU.is_lt, ALU.mult).then_inc(s, 1)
                dve.wait_ge(s, base + 11)
                V.tensor_reduce(gate.sm[:], sel[:], AXX, ALU.add).then_inc(s, 1)
                dve.wait_ge(s, base + 12)
                V.reciprocal(gate.rs[:], gate.sm[:]).then_inc(s, 1)
                dve.wait_ge(s, base + 13)
                V.tensor_tensor(gate.wt[:, :, 0:NE], sel[:], gate.bcast(gate.rs), ALU.mult
                                ).then_inc(gate.gated, 1)
                V.sem_inc(s, 1)
                if more:
                    g.normalise(dve, it + 1)
                dve.wait_ge(gate.gated, it + 1)
                pr.take(dve, it)

            with nc.vector.Fori(0, NG - 1) as it:
                group(it, True)
            group(NG - 1, False)

        @block.scalar
        def _(act):
            with nc.scalar.Fori(0, NG) as it:
                g.copy(act, it)
                gate.exp(act, it, STEPS)
                act.wait_ge(gate.step, it * STEPS + 8)
                nc.scalar.activation(gate.ex[:], gate.lg[:], ACT.Exp).then_inc(gate.exped, 1)
                pr.keep(act, it, gate.before_keep)

        @block.tensor
        def _(pe):
            pe.wait_ge(loaded, 16 * 11)
            with nc.tensor.Fori(0, NG) as it:
                pe.wait_ge(pr.taken, it * pr.nr)
                g.turn(pe, it)
                pe.wait_ge(g.ready, (it + 1) * g.BANKS)
                gate.ask(pe, it, pr)
                pr.multiply(pe, it, gate.before_product)
                pe.wait_ge(pr.done, (it + 1) * pr.nr)
                pe.sem_inc(g.used, 1)


def row_product(nc, c, io, name, X, weight, take_to_dram=None, bias=None):
    with Phase(nc, name) as ph:
        g = Group(ph, c, X)
        w, b = ph.sb("w", [P, 2, D]), ph.sb("b", [P, D])
        z = ph.sb("z", [P, GT, D])
        loaded, stored, biased = ph.sem("loaded"), ph.sems("stored", GT), ph.sem("biased")

        def take(j):
            def f(it, y):
                if take_to_dram is None:
                    nc.vector.wait_ge(biased, it * GT + j + 1)
                    return nc.vector.tensor_tensor(rowof(X, it * GT + j), rowof(X, it * GT + j), y, ALU.add)
                nc.vector.wait_ge(stored[j], it * 16)
                return nc.vector.tensor_copy(z[:, j, :], y)
            return f

        pr = Products(ph, [dict(kind="R", take=take(j), terms=[
            (g.xT[:, k, j * P:(j + 1) * P], w[:, k, :]) for k in range(2)]) for j in range(GT)], g)
        block = ph.block()

        @block.sync
        def _(sp):
            sp.dma_start(w[:], io[weight].rearrange("(k p) n -> p k n", p=P)).then_inc(loaded, 16)
            sp.dma_start(b[:], io[bias or weight].rearrange("n -> n").partition_broadcast(P) if bias else
                         io[weight][0:P, :]).then_inc(loaded, 16)
            if take_to_dram is not None:
                with nc.sync.Fori(0, NG) as it:
                    for j in range(GT):
                        sp.wait_ge(pr.taken, it * GT + j + 1)
                        sp.dma_start(take_to_dram[ds((it * GT + j) * P, P), :], z[:, j, :]).then_inc(stored[j], 16)
                for j in range(GT):
                    sp.wait_ge(stored[j], 16 * NG)

        @block.vector
        def _(dve):
            dve.wait_ge(loaded, 32)
            g.normalise(dve, 0)

            def group(it, more):
                if take_to_dram is None:
                    dve.wait_ge(g.normed, it + 1)
                    for j in range(GT):
                        nc.vector.tensor_tensor(rowof(X, it * GT + j), rowof(X, it * GT + j), b[:], ALU.add
                                                ).then_inc(biased, 1)
                if more:
                    g.normalise(dve, it + 1)
                pr.take(dve, it)

            with nc.vector.Fori(0, NG - 1) as it:
                group(it, True)
            group(NG - 1, False)

        @block.scalar
        def _(act):
            with nc.scalar.Fori(0, NG) as it:
                g.copy(act, it)

        @block.tensor
        def _(pe):
            pe.wait_ge(loaded, 32)
            with nc.tensor.Fori(0, NG) as it:
                pe.wait_ge(pr.taken, it * pr.nr)
                g.turn(pe, it)
                pe.wait_ge(g.ready, (it + 1) * g.BANKS)
                pr.multiply(pe, it)
                pe.wait_ge(pr.done, (it + 1) * pr.nr)
                pe.sem_inc(g.used, 1)


def add_relu(nc, X, agg):
    return lambda i: nc.vector.scalar_tensor_tensor(X[:, i, :], agg[:, i, 0:D], 0.0, X[:, i, :],
                                                    ALU.max, ALU.add)


TY = 19
TT = 45
TG = TT // GT
PROJ, TD, H2 = 192, 32, 4
DK = (PROJ + TD) // H2
KVQ = 2 * PROJ + DK
assert NP + TY * (P - 1) < (TT + 1) * P
TWO_PI = 6.283185307179586
ROUND = 12582912.0


def sort_nodes(nc, c, io, X, pos_i, type_i, xs):
    with Phase(nc, "nodes") as ph:
        ty_i, ty = ph.sb("ty_i", [P, NT], I32), ph.sb("ty", [P, NT])
        hot, incl, tmp = ph.sb("hot", [P, TY, NT]), ph.sb("incl", [P, TY, NT]), ph.sb("tmp", [P, TY, NT])
        tot, run = ph.sb("tot", [P, TY, NT]), ph.sb("run", [P, TY, NT])
        keep = ph.sb("keep", [P, TY, NT])
        num, num_i = ph.sb("num", [P, 6, TY]), ph.sb("num_i", [P, 2, TY], I32)
        pos, tt = ph.sb("pos", [P, NT]), ph.sb("tt", [P, TT])
        past = ph.sb("past", [P, TT, TY])
        zero = ph.sb("zero", [P, D])
        xn = ph.sb("xn", [P, GT, D])
        zrow = ph.sem("zrow")
        loaded, step, pe_done, filled = ph.sem("loaded"), ph.sem("step"), ph.sem("pe_done"), ph.sem("filled")
        placed, normed = ph.sem("placed"), ph.sem("normed")
        sent = ph.gather_sems(GT)
        ranks, totals = ph.ps("ranks", [P, TY * NT]), ph.ps("totals", [P, TY * NT])
        block = ph.block()

        @block.sync
        def _(sp):
            sp.dma_start(ty_i[:], io["T2type"]).then_inc(loaded, 16)
            sp.wait_ge(zrow, 1)
            sp.dma_start(xs.rearrange("(t p) d -> p t d", p=P), zero[:].unsqueeze(1).to_broadcast([P, TT, D])
                         ).then_inc(filled, 16)

        @block.vector
        def _(dve):
            V = nc.vector
            V.memset(zero[:], 0.0).then_inc(zrow, 1)
            V.memset(keep[:], 1.0).then_inc(zrow, 1)
            dve.wait_ge(zrow, 2)
            V.memset(keep[:, :, 0:1], 0.0)
            dve.wait_ge(loaded, 16)
            V.tensor_copy(ty[:], ty_i[:]).then_inc(step, 1)
            dve.wait_ge(step, 1)
            V.tensor_tensor(hot[:], c["iota"][:, 0:TY].unsqueeze(2).to_broadcast([P, TY, NT]),
                            ty[:].unsqueeze(1).to_broadcast([P, TY, NT]), ALU.is_equal).then_inc(step, 1)
            dve.wait_ge(pe_done, 2)
            V.tensor_copy(tot[:].rearrange("p a b -> p (a b)"), totals[:]).then_inc(step, 1)
            dve.wait_ge(step, 3)
            V.tensor_tensor_scan(run[:].rearrange("p a b -> p (a b)"), keep[:].rearrange("p a b -> p (a b)"),
                                 tot[:].rearrange("p a b -> p (a b)"), 0.0, ALU.mult, ALU.add).then_inc(step, 1)
            dve.wait_ge(step, 4)
            V.tensor_scalar(num[:, 0, :], run[:, :, NT - 1], float(P - 1), None, ALU.add)
            V.tensor_tensor(tmp[:], run[:], tot[:], ALU.subtract).then_inc(step, 1)
            dve.wait_ge(step, 5)
            V.tensor_copy(num_i[:, 0, :], num[:, 0, :])
            V.tensor_tensor(incl[:].rearrange("p a b -> p (a b)"), tmp[:].rearrange("p a b -> p (a b)"),
                            ranks[:], ALU.add).then_inc(step, 1)
            dve.wait_ge(step, 6)
            V.tensor_scalar(num_i[:, 1, :], num_i[:, 0, :], 7, None, ALU.logical_shift_right).then_inc(step, 1)
            dve.wait_ge(step, 7)
            V.tensor_copy(num[:, 1, :], num_i[:, 1, :]).then_inc(step, 1)
            dve.wait_ge(step, 8)
            V.tensor_tensor_scan(num[:, 2, :], c["ones"][:, 0:TY], num[:, 1, :], 0.0, ALU.mult, ALU.add
                                 ).then_inc(step, 1)
            dve.wait_ge(step, 9)
            V.tensor_tensor(num[:, 3, :], num[:, 2, :], num[:, 1, :], ALU.subtract)
            V.tensor_tensor(past[:], c["iota"][:, 0:TT].unsqueeze(2).to_broadcast([P, TT, TY]),
                            num[:, 2, :].unsqueeze(1).to_broadcast([P, TT, TY]), ALU.is_ge).then_inc(step, 1)
            dve.wait_ge(step, 10)
            V.tensor_scalar(num[:, 4, :], num[:, 3, :], float(P), None, ALU.mult)
            V.tensor_reduce(tt[:], past[:], AXX, ALU.add).then_inc(step, 1)
            dve.wait_ge(step, 11)
            V.tensor_tensor(tmp[:], incl[:], num[:, 4, :].unsqueeze(2).to_broadcast([P, TY, NT]), ALU.add)
            V.tensor_scalar(tt[:], tt[:], float(TY - 1), None, ALU.min).then_inc(step, 1)
            dve.wait_ge(step, 12)
            V.tensor_copy(type_i[:], tt[:])
            V.tensor_tensor(tmp[:], tmp[:], hot[:], ALU.mult).then_inc(step, 1)
            dve.wait_ge(step, 13)
            V.tensor_reduce(pos[:], tmp[:].rearrange("p t i -> p i t"), AXX, ALU.add).then_inc(step, 1)
            dve.wait_ge(step, 14)
            V.tensor_copy(pos_i[:], pos[:]).then_inc(placed, 1)
            for i in range(NT):
                if i >= GT:
                    dve.wait_ge(sent[i % GT], 16 * (i // GT))
                V.tensor_scalar(xn[:, i % GT, :], X[:, i, :], c["mean"][:, i:i + 1], c["rstd"][:, i:i + 1],
                                ALU.subtract, ALU.mult).then_inc(normed, 1)

        @block.tensor
        def _(pe):
            pe.wait_ge(step, 2)
            for out, m in ((ranks, "before_row"), (totals, "ones")):
                nc.tensor.matmul(out[:], c[m][:], hot[:].rearrange("p a b -> p (a b)"), start=True, stop=True
                                 ).then_inc(pe_done, 1)

        @block.gpsimd
        def _(pool):
            pool.wait_ge(filled, 16)
            pool.wait_ge(placed, 1)
            for i in range(NT):
                pool.wait_ge(normed, i + 1)
                pool.indirect_dma_start(
                    out=xs, out_offset=bass.IndirectOffsetOnAxis(ap=pos_i[:, i:i + 1].bitcast(U32), axis=0),
                    in_=xn[:, i % GT, :], in_offset=None).then_inc(sent[i % GT], 16)
            for j in range(GT):
                pool.wait_ge(sent[j], 16 * NG)


def type_projections(nc, c, io, type_i, xs, kvq_s):
    with Phase(nc, "typed") as ph:
        w = ph.sb("w", [P, TY * 2, KVQ])
        wb = ph.sb("wb", [1, TY, KVQ])
        pT = ph.ps("pT", [P, 3, 512])
        prod = ph.ps("prod", [P, GT, 512])
        qloaded, summed = ph.sem("qloaded"), ph.sem("summed")
        x_in, turned, ready = ph.sem("x_in"), ph.sem("turned"), ph.sem("ready")
        done, taken, stored = ph.sem("done"), ph.sem("taken"), ph.sems("stored", GT)

        with Phase(nc, "typed_q") as pq:
            wq, bq = pq.sb("wq", [P, TY * 2, PROJ]), pq.sb("bq", [1, TY, PROJ])
            block = pq.block()

            @block.sync
            def _(sp):
                for n, k in enumerate(("Wv", "Wk")):
                    sp.dma_start(w[:, :, n * PROJ:(n + 1) * PROJ],
                                 io["T2" + k].rearrange("t (k p) n -> p (t k) n", p=P)).then_inc(qloaded, 16)
                sp.dma_start(wq[:], io["T2Wq"].rearrange("t (k p) n -> p (t k) n", p=P)).then_inc(qloaded, 16)
                for n, k in enumerate(("bv", "bk")):
                    sp.dma_start(wb[:, :, n * PROJ:(n + 1) * PROJ], io["T2" + k].unsqueeze(0)).then_inc(qloaded, 16)
                sp.dma_start(bq[:], io["T2bq"].unsqueeze(0)).then_inc(qloaded, 16)

            @block.vector
            def _(dve):
                dve.wait_ge(qloaded, 96)
                for n, (dst, q) in enumerate(((w[:, :, 2 * PROJ:], wq[:]), (wb[:, :, 2 * PROJ:], bq[:]))):
                    nc.vector.tensor_tensor(dst, q[:, :, 0:DK], q[:, :, DK:2 * DK], ALU.add).then_inc(summed, 1)
                    dve.wait_ge(summed, 3 * n + 1)
                    nc.vector.tensor_tensor(dst, dst, q[:, :, 2 * DK:3 * DK], ALU.add).then_inc(summed, 1)
                    dve.wait_ge(summed, 3 * n + 2)
                    nc.vector.tensor_tensor(dst[:, :, 0:PROJ - 3 * DK], dst[:, :, 0:PROJ - 3 * DK],
                                            q[:, :, 3 * DK:], ALU.add).then_inc(summed, 1)

        x = ph.sb("x", [P, GT, D])
        xT = ph.sb("xT", [P, GT, D])
        y = ph.sb("y", [P, GT, KVQ])
        block = ph.block()

        @block.sync
        def _(sp):
            def fetch(n):
                sp.dma_start(x[:], xs.rearrange("(t p) d -> p t d", p=P)[:, ds(n * GT, GT), :]).then_inc(x_in, 16)

            def store(n):
                for j in range(GT):
                    sp.wait_ge(taken, n * GT + j + 1)
                    sp.dma_start(kvq_s[ds((n * GT + j) * P, P), :], y[:, j, :]).then_inc(stored[j], 16)

            fetch(0)
            with nc.sync.Fori(0, TG - 1) as it:
                sp.wait_ge(turned, (it + 1) * 3)
                fetch(it + 1)
                store(it)
            store(TG - 1)
            for j in range(GT):
                sp.wait_ge(stored[j], 16 * TG)

        @block.tensor
        def _(pe):
            with nc.tensor.Fori(0, TG) as it:
                pe.wait_ge(x_in, it * 16 + 16)
                pe.wait_ge(ready, it * 3)
                for b in range(3):
                    for j in range(2 * b, min(2 * b + 2, GT)):
                        for h in range(2):
                            col = (j % 2) * D + h * P
                            last = nc.tensor.transpose(pT[:, b, col:col + P], x[:, j, h * P:(h + 1) * P],
                                                       c["ident"][:])
                    last.then_inc(turned, 1)
                pe.wait_ge(taken, it * GT)
                for j in range(GT):
                    pe.wait_ge(ready, it * 3 + j // 2 + 1)
                    t = nc.tensor.value_load(type_i[0:1, ds(it * GT + j, 1)], min_val=0, max_val=TY - 1)
                    for h in range(2):
                        nc.tensor.matmul(prod[:, j, 0:KVQ], xT[:, j, h * P:(h + 1) * P],
                                         w[:, ds(t * 2 + h, 1), :].rearrange("p a n -> p (a n)"),
                                         start=(h == 0), stop=False)
                    nc.tensor.matmul(prod[:, j, 0:KVQ], c["ones"][0:1, :],
                                     wb[:, ds(t, 1), :].rearrange("p a n -> p (a n)"),
                                     start=False, stop=True).then_inc(done, 1)

        @block.scalar
        def _(act):
            with nc.scalar.Fori(0, TG) as it:
                for b in range(3):
                    act.wait_ge(turned, it * 3 + b + 1)
                    if b == 0:
                        act.wait_ge(done, it * GT)
                    n = 2 if b < 2 else 1
                    nc.scalar.copy(xT[:, 2 * b:2 * b + n, :].rearrange("p j d -> p (j d)"),
                                   pT[:, b, 0:n * D]).then_inc(ready, 1)

        @block.vector
        def _(dve):
            with nc.vector.Fori(0, TG) as it:
                for j in range(GT):
                    dve.wait_ge(done, it * GT + j + 1)
                    dve.wait_ge(stored[j], it * 16)
                    nc.vector.tensor_copy(y[:, j, :], prod[:, j, 0:KVQ]).then_inc(taken, 1)


def nodes_back(nc, c, pos_i, kvq_s, vk_table, q_rows):
    with Phase(nc, "back") as ph:
        y = ph.sb("y", [P, GT, KVQ])
        got, kept = ph.gather_sems(GT), ph.sem("kept")
        stored = ph.sems("stored", GT)
        block = ph.block()

        @block.gpsimd
        def _(pool):
            for i in range(NT):
                j = i % GT
                if i >= GT:
                    pool.wait_ge(kept, i - GT + 1)
                    pool.wait_ge(stored[j], 16 * (i // GT))
                pool.indirect_dma_start(
                    out=y[:, j, :], out_offset=None, in_=kvq_s,
                    in_offset=bass.IndirectOffsetOnAxis(ap=pos_i[:, i:i + 1].bitcast(U32), axis=0)
                ).then_inc(got[j], 16)

        @block.vector
        def _(dve):
            for i in range(NT):
                dve.wait_ge(got[i % GT], 16 * (i // GT) + 16)
                nc.vector.tensor_copy(q_rows[:, i, :], y[:, i % GT, 2 * PROJ:]).then_inc(kept, 1)

        @block.sync
        def _(sp):
            for i in range(NT):
                sp.wait_ge(got[i % GT], 16 * (i // GT) + 16)
                sp.dma_start(vk_table[i * P:(i + 1) * P, :], y[:, i % GT, 0:2 * PROJ]).then_inc(stored[i % GT], 16)
            for j in range(GT):
                sp.wait_ge(stored[j], 16 * NG)


def timed_scores(nc, c, io, name, slots, lo_rows, q_rows, vk_table, v_stream, scores, blocks):
    W = PROJ + TD
    R = 4
    last_round = NU // R - 1
    with Phase(nc, name) as ph:
        slot = ph.sb("slot", [P, ST + R * U, PW])
        logt = ph.sb("logt", [P, ST, 3])
        wt, bt = ph.sb("wt", [P, TD]), ph.sb("bt", [P, TD])
        lo_row = ph.sb("lo_row", [1, R, U * P])
        hotT = ph.sb("hotT", [P, R, U, P])
        idx = ph.sb("idx", [P, R, U], I32)
        vk = ph.sb("vk", [P, R, U, 2 * PROJ + TD])
        turns, whole = ph.sb("turns", [P, 2, 3 * U, TD]), ph.sb("whole", [P, 2, 3 * U, TD])
        emb = ph.sb("emb", [P, R, U, 2, TD])
        q_time = ph.sb("q_time", [P, R, U, DK])
        prod = ph.sb("prod", [P, 2, U, W])
        q = [ph.ps(f"q{u}", [P, U, P]) for u in range(R)]
        every = [ph.ps(f"every{u}", [P, U * P]) for u in range(2)]
        spread = ph.sems("spread", R)
        loaded, prepared, logged, released = ph.sem("loaded"), ph.sem("prepared"), ph.sem("logged"), ph.sem("rel")
        row_in, picked, hot = ph.sems("row_in", R), ph.sems("picked", R), ph.sems("hot", R)
        gathered, asked, mult = ph.gather_sems(R), ph.sems("asked", R), ph.sems("mult", R)
        phase, rounded, left = ph.sems("phase", 2), ph.sems("rounded", 2), ph.sems("left", 2)
        waved, joined = ph.sems("waved", R), ph.sems("joined", R)
        streamed, summed = ph.sems("streamed", R), ph.sems("summed", 2)
        block = ph.block()

        @block.sync
        def _(sp):
            def fetch_row(start, u):
                sp.dma_start(lo_row[:, u, :], lo_rows[ds(start, U * P)].unsqueeze(0)).then_inc(row_in[u], 16)

            def stream(n, u):
                sp.wait_ge(gathered[u], (n + 1) * (16 * U))
                sp.wait_ge(waved[u], n + 1)
                sp.dma_start(v_stream[:, ds((n * R + u) * U, U), PROJ:D],
                             emb[:, u, :, :, :].rearrange("p j e d -> p j (e d)")).then_inc(streamed[u], 16)
                sp.dma_start(v_stream[:, ds((n * R + u) * U, U), 0:PROJ], vk[:, u, :, 0:PROJ]
                             ).then_inc(streamed[u], 16)

            sp.dma_start(slot[:, 0:ST, :], slots.rearrange("(p t) w -> p t w", t=ST)).then_inc(loaded, 16)
            sp.dma_start(wt[:], io["T2w"].partition_broadcast(P)).then_inc(loaded, 16)
            sp.dma_start(bt[:], io["T2b"].partition_broadcast(P)).then_inc(loaded, 16)
            for u in range(R):
                fetch_row(u * (U * P), u)
            with nc.sync.Fori(0, last_round) as it:
                for u in range(R):
                    sp.wait_ge(spread[u], it + 1)
                    fetch_row(it * (R * U * P) + (R + u) * (U * P), u)
                    stream(it, u)
            for u in range(R):
                stream(last_round, u)
            for u in range(R):
                sp.wait_ge(streamed[u], 32 * (NU // R))

        @block.gpsimd
        def _(pool):
            with nc.gpsimd.Fori(0, NU // R) as it:
                for u in range(R):
                    pool.wait_ge(picked[u], it + 1)
                    pool.wait_ge(mult[u], it)
                    pool.wait_ge(streamed[u], it * 32)
                    pool.sem_inc(released, 1)
                    for j in range(U):
                        pool.indirect_dma_start(
                            out=vk[:, u, j, 0:2 * PROJ], out_offset=None, in_=vk_table,
                            in_offset=bass.IndirectOffsetOnAxis(ap=idx[:, u, j:j + 1].bitcast(U32), axis=0)
                        ).then_inc(gathered[u], 16)

        @block.scalar
        def _(act):
            def pick(n, u):
                nc.scalar.copy(idx[:, u, :].bitcast(U32), slot[:, ds((n * R + u) * U, U), OTHER].bitcast(U32)
                               ).then_inc(picked[u], 1)

            act.wait_ge(loaded, 48)
            act.wait_ge(prepared, 4)
            for u in range(2):
                pick(0, u)
            nc.scalar.activation(logt[:], slot[:, 0:ST, TB:TB + 3], ACT.Ln, bias=c["ones"][:, 0:1]
                                 ).then_inc(logged, 1)
            with nc.scalar.Fori(0, NU // R) as it:
                for u in range(R):
                    done_before = it * (R // 2) + u // 2
                    act.wait_ge(phase[u % 2], (done_before + 1) * 2)
                    act.wait_ge(left[u % 2], done_before)
                    nc.scalar.activation(whole[:, u % 2, :, :].rearrange("p a d -> p (a d)"),
                                         turns[:, u % 2, :, :].rearrange("p a d -> p (a d)"), ACT.Copy,
                                         bias=ROUND).then_inc(rounded[u % 2], 1)
                    act.wait_ge(left[u % 2], done_before + 1)
                    act.wait_ge(streamed[u], it * 32)
                    act.wait_ge(asked[u], it)
                    parts = turns[:, u % 2, :, :].rearrange("p (j e) d -> p j e d", e=3)
                    nc.scalar.activation(q_time[:, u, :, DK - TD:], parts[:, :, 2, :], ACT.Sin,
                                         scale=-6.283185)
                    nc.scalar.activation(emb[:, u, :, :, :], parts[:, :, 0:2, :], ACT.Sin,
                                         scale=-6.283185).then_inc(waved[u], 1)
                    act.wait_ge(waved[u], it + 1)
                    act.wait_ge(mult[u], it)
                    nc.scalar.copy(vk[:, u, :, 2 * PROJ:], emb[:, u, :, 0, :]).then_inc(joined[u], 1)
                    if u < 2:
                        act.wait_ge(gathered[u + 2], it * (16 * U))
                        pick(it, u + 2)
                    else:
                        act.wait_ge(gathered[u - 2], (it + 1) * (16 * U))
                        pick(it + 1, u - 2)

        @block.vector
        def _(dve):
            V = nc.vector

            def make_hot(n, u):
                dve.wait_ge(spread[u], n + 1)
                dve.wait_ge(asked[u], n)
                V.tensor_scalar(hotT[:, u, :, :].rearrange("p a b -> p (a b)"), every[u % 2][:],
                                c["iota_p"][:], None, ALU.is_equal).then_inc(hot[u], 1)

            def turns_scaled(n, u):
                if u < 2:
                    dve.wait_ge(waved[u + 2], n)
                else:
                    dve.wait_ge(waved[u - 2], n + 1)
                V.tensor_tensor(turns[:, u % 2, :, :],
                                logt[:, ds((n * R + u) * U, U), :].rearrange("p t e -> p (t e)")
                                .unsqueeze(2).to_broadcast([P, 3 * U, TD]),
                                wt[:].unsqueeze(1).to_broadcast([P, 3 * U, TD]), ALU.mult
                                ).then_inc(phase[u % 2], 1)

            def turns_shifted(n, u):
                dve.wait_ge(phase[u % 2], (n * (R // 2) + u // 2) * 2 + 1)
                V.tensor_tensor(turns[:, u % 2, :, :], turns[:, u % 2, :, :],
                                bt[:].unsqueeze(1).to_broadcast([P, 3 * U, TD]), ALU.add
                                ).then_inc(phase[u % 2], 1)

            def turns_left(n, u):
                dve.wait_ge(rounded[u % 2], n * (R // 2) + u // 2 + 1)
                V.scalar_tensor_tensor(turns[:, u % 2, :, :], whole[:, u % 2, :, :], ROUND, turns[:, u % 2, :, :],
                                       ALU.subtract, ALU.subtract).then_inc(left[u % 2], 1)

            def multiply(n, u):
                dve.wait_ge(asked[u], n + 1)
                dve.wait_ge(gathered[u], (n + 1) * (16 * U))
                dve.wait_ge(joined[u], n + 1)
                dve.wait_ge(summed[u % 2], n * (R // 2) + u // 2)
                V.tensor_tensor(
                    prod[:, u % 2, :, :].rearrange("p j (h d) -> p j h d", d=DK),
                    vk[:, u, :, PROJ:].rearrange("p j (h d) -> p j h d", d=DK),
                    q[u][:, :, 0:DK].unsqueeze(2).to_broadcast([P, U, H2, DK]), ALU.mult).then_inc(mult[u], 1)

            def total(n, u):
                dve.wait_ge(mult[u], n + 1)
                V.tensor_reduce(scores[:, ds((n * R + u) * (U * H2), U * H2)],
                                prod[:, u % 2, :, :].rearrange("p j (h d) -> p (j h) d", d=DK), AXX, ALU.add
                                ).then_inc(summed[u % 2], 1)

            V.memset(slot[:, ST:, :], 0.0).then_inc(prepared, 1)
            V.memset(q_time[:], 0.0).then_inc(prepared, 1)
            dve.wait_ge(loaded, 48)
            V.tensor_scalar(wt[:], wt[:], 1.0 / TWO_PI, None, ALU.mult).then_inc(prepared, 1)
            V.tensor_scalar(bt[:], bt[:], 1.0 / TWO_PI, 0.25, ALU.mult, ALU.add).then_inc(prepared, 1)
            dve.wait_ge(prepared, 4)
            dve.wait_ge(logged, 1)
            for u in range(2):
                make_hot(0, u)
                turns_scaled(0, u)
                turns_shifted(0, u)
                turns_left(0, u)

            def unit(n, u, following):
                if following:
                    make_hot(*following)
                    turns_scaled(*following)
                multiply(n, u)
                if following:
                    turns_shifted(*following)
                total(n, u)
                if following:
                    turns_left(*following)

            with nc.vector.Fori(0, last_round) as it:
                for u in range(R):
                    unit(it, u, (it + (u + 2) // R, (u + 2) % R))
            for u in range(R):
                unit(last_round, u, (last_round, u + 2) if u + 2 < R else None)

        @block.tensor
        def _(pe):
            def spread_row(n, u, free=True):
                pe.wait_ge(row_in[u], n * 16 + 16)
                if free:
                    pe.wait_ge(hot[(u + 2) % R], n + u // 2)
                nc.tensor.matmul(every[u % 2][:], c["ones"][0:1, :], lo_row[:, u, :], start=True, stop=True
                                 ).then_inc(spread[u], 1)

            def ask(n, u, following=None):
                if following:
                    spread_row(*following)
                nb = load_blocks(nc.tensor, blocks, n * R + u)
                pe.wait_ge(hot[u], n + 1)
                pe.wait_ge(mult[u], n)
                pe.wait_ge(waved[u], n + 1)
                nc.tensor.matmul(q[u][:, :, 0:DK], c["ident"][:], q_time[:, u, :, :], start=True, stop=False)
                for j in range(U):
                    last = nc.tensor.matmul(q[u][:, j, 0:DK], hotT[:, u, j, :], rowof(q_rows, nb[j // RUN]),
                                            start=False, stop=(j == U - 1))
                last.then_inc(asked[u], 1)

            for u in range(2):
                spread_row(0, u, free=False)
            with nc.tensor.Fori(0, last_round) as it:
                for u in range(R):
                    ask(it, u, (it + (u + 2) // R, (u + 2) % R))
            for u in range(R):
                ask(last_round, u, (last_round, u + 2) if u + 2 < R else None)


def fold_direction(nc, name, agg, both, first):
    VW = PROJ + TD
    with Phase(nc, name) as ph:
        den, rec = ph.sb("den", [P, NT, H2]), ph.sb("rec", [P, NT, H2])
        t = ph.sb("t", [P, NT, VW])
        s = ph.sem("s")
        block = ph.block()

        @block.vector
        def _(dve):
            V = nc.vector
            V.tensor_scalar(den[:], agg[:, :, VW:VW + H2], 1e-16, None, ALU.add).then_inc(s, 1)
            dve.wait_ge(s, 1)
            V.reciprocal(rec[:], den[:]).then_inc(s, 1)
            dve.wait_ge(s, 2)
            dst = both[:, :, 0:VW] if first else t[:]
            for h in range(H2):
                cols = slice(h * DK, (h + 1) * DK)
                last = V.tensor_tensor(dst[:, :, cols], agg[:, :, cols],
                                       rec[:, :, h:h + 1].to_broadcast([P, NT, DK]), ALU.mult)
            if first:
                V.tensor_copy(both[:, :, VW:D], agg[:, :, VW + H2:D + H2])
            else:
                last.then_inc(s, 1)
                dve.wait_ge(s, 3)
                V.tensor_tensor(both[:, :, 0:VW], both[:, :, 0:VW], t[:], ALU.add)
                V.tensor_tensor(both[:, :, VW:D], both[:, :, VW:D], agg[:, :, VW + H2:D + H2], ALU.add)


def type_output(nc, c, io, pos_i, type_i, both, xs, as_, X):
    with Phase(nc, "tout") as ph:
        w = ph.sb("w", [P, TY * 2, D])
        rows = ph.sb("rows", [P, 2, TY, D])
        ba = ph.sb("ba", [1, TY, D])
        pT, prod = ph.ps("pT", [P, 3, 512]), ph.ps("prod", [P, GT, 512])
        loaded, summed = ph.sem("loaded"), ph.sem("summed")
        filled, zeroed = ph.sem("filled"), ph.sem("zeroed")
        a_in, x_in, turned, ready, done = (ph.sem(k) for k in ("a_in", "x_in", "turned", "ready", "done"))
        added, counted, aggred, rooted, recd = (ph.sem(k) for k in ("added", "counted", "aggred", "rooted", "recd"))
        spread = ph.sem("spread")
        normed, scaled, final, stored = ph.sem("normed"), ph.sem("scaled"), ph.sem("final"), ph.sem("stored")
        order = "(t p) d -> p t d"

        with Phase(nc, "tout_w") as pw:
            low = pw.sb("low", [P, TY, D])
            low_in, wrote = pw.sem("low_in"), pw.gather_sems(1)[0]
            w_k = w[:].rearrange("p (t k) n -> p t k n", k=2)
            zero = pw.sb("zero", [P, D])
            block = pw.block()

            @block.sync
            def _(sp):
                wa = io["T2Wa"].rearrange("t (s k p) n -> s p t k n", s=2, p=P)
                for k in range(2):
                    sp.dma_start(w_k[:, :, k, :], wa[0, :, :, k, :]).then_inc(loaded, 16)
                for n, k in enumerate(("gamma", "beta")):
                    sp.dma_start(rows[:, n, :, :].rearrange("p t n -> p (t n)"),
                                 io["T2" + k].rearrange("t n -> (t n)").partition_broadcast(P)).then_inc(loaded, 16)
                sp.dma_start(ba[:], io["T2ba"].unsqueeze(0)).then_inc(loaded, 16)
                sp.wait_ge(zeroed, 1)
                sp.dma_start(as_.rearrange(order, p=P), zero[:].unsqueeze(1).to_broadcast([P, TT, D])
                             ).then_inc(filled, 16)
                for k in range(2):
                    if k:
                        sp.wait_ge(summed, 1)
                    sp.dma_start(low[:], wa[1, :, :, k, :]).then_inc(low_in, 16)
                sp.wait_ge(loaded, 16 * 5)

            @block.vector
            def _(dve):
                nc.vector.memset(zero[:], 0.0).then_inc(zeroed, 1)
                dve.wait_ge(loaded, 16 * 5)
                for k in range(2):
                    dve.wait_ge(low_in, 16 * (k + 1))
                    nc.vector.tensor_tensor(w_k[:, :, k, :], w_k[:, :, k, :], low[:], ALU.add).then_inc(summed, 1)

            @block.gpsimd
            def _(pool):
                pool.wait_ge(filled, 16)
                for i in range(NT):
                    pool.indirect_dma_start(
                        out=as_, out_offset=bass.IndirectOffsetOnAxis(ap=pos_i[:, i:i + 1].bitcast(U32), axis=0),
                        in_=both[:, i, :], in_offset=None).then_inc(wrote, 16)
                pool.wait_ge(wrote, 16 * NT)

        a, x = ph.sb("a", [P, GT, D]), ph.sb("x", [P, GT, D])
        aT = ph.sb("aT", [P, GT, D])
        y = ph.sb("y", [P, GT, D])
        st, mv = ph.sb("st", [P, GT, 6]), ph.sb("mv", [P, GT, 2])
        sd, rs = ph.sb("sd", [P, GT]), ph.sb("rs", [P, GT])

        with ph.nc.Block() as block:
            @block.sync
            def _(sp):
                def fetch(t, table, n, arrived):
                    sp.dma_start(t[:], table.rearrange(order, p=P)[:, ds(n * GT, GT), :]).then_inc(arrived, 16)

                def store(n):
                    sp.wait_ge(final, (n + 1) * GT)
                    sp.dma_start(as_.rearrange(order, p=P)[:, ds(n * GT, GT), :], y[:]).then_inc(stored, 16)

                fetch(a, as_, 0, a_in)
                fetch(x, xs, 0, x_in)
                with nc.sync.Fori(0, TG - 1) as it:
                    sp.wait_ge(turned, (it + 1) * 3)
                    fetch(a, as_, it + 1, a_in)
                    sp.wait_ge(added, it * GT + GT)
                    fetch(x, xs, it + 1, x_in)
                    store(it)
                store(TG - 1)
                sp.wait_ge(stored, 16 * TG)

            @block.tensor
            def _(pe):
                with nc.tensor.Fori(0, TG) as it:
                    pe.wait_ge(a_in, it * 16 + 16)
                    pe.wait_ge(ready, it * 3)
                    for b in range(3):
                        for j in range(2 * b, min(2 * b + 2, GT)):
                            for h in range(2):
                                col = (j % 2) * D + h * P
                                last = nc.tensor.transpose(pT[:, b, col:col + P], a[:, j, h * P:(h + 1) * P],
                                                           c["ident"][:])
                        last.then_inc(turned, 1)
                    pe.wait_ge(added, it * GT)
                    for j in range(GT):
                        pe.wait_ge(ready, it * 3 + j // 2 + 1)
                        t = nc.tensor.value_load(type_i[0:1, ds(it * GT + j, 1)], min_val=0, max_val=TY - 1)
                        for h in range(2):
                            nc.tensor.matmul(prod[:, j, 0:D], aT[:, j, h * P:(h + 1) * P],
                                             w[:, ds(t * 2 + h, 1), :].rearrange("p a n -> p (a n)"),
                                             start=(h == 0), stop=False)
                        nc.tensor.matmul(prod[:, j, 0:D], c["ones"][0:1, :],
                                         ba[:, ds(t, 1), :].rearrange("p a n -> p (a n)"),
                                         start=False, stop=True).then_inc(done, 1)

            @block.scalar
            def _(act):
                with nc.scalar.Fori(0, TG) as it:
                    for b in range(3):
                        act.wait_ge(turned, it * 3 + b + 1)
                        if b == 0:
                            act.wait_ge(done, it * GT)
                        n = 2 if b < 2 else 1
                        nc.scalar.copy(aT[:, 2 * b:2 * b + n, :].rearrange("p j d -> p (j d)"),
                                       pT[:, b, 0:n * D]).then_inc(ready, 1)
                    act.wait_ge(aggred, (it + 1) * GT)
                    nc.scalar.activation(sd[:], mv[:, :, 1], ACT.Sqrt, bias=c["eps"][:]).then_inc(rooted, 1)

            @block.vector
            def _(dve):
                V = nc.vector
                with nc.vector.Fori(0, TG) as it:
                    dve.wait_ge(x_in, it * 16 + 16)
                    dve.wait_ge(stored, it * 16)
                    for j in range(GT):
                        dve.wait_ge(done, it * GT + j + 1)
                        V.tensor_tensor(y[:, j, :], prod[:, j, 0:D], x[:, j, :], ALU.add).then_inc(added, 1)
                    for j in range(GT):
                        dve.wait_ge(added, it * GT + j + 1)
                        V.bn_stats(st[:, j, :], y[:, j, :]).then_inc(counted, 1)
                    for j in range(GT):
                        if j == 0:
                            dve.wait_ge(counted, it * GT + GT)
                            dve.sem_inc(spread, 1)
                        V.bn_aggr(mv[:, j, :], st[:, j, :]).then_inc(aggred, 1)
                    dve.wait_ge(rooted, it + 1)
                    V.reciprocal(rs[:], sd[:]).then_inc(recd, 1)
                    dve.wait_ge(recd, it + 1)
                    for j in range(GT):
                        V.tensor_scalar(y[:, j, :], y[:, j, :], mv[:, j, 0:1], rs[:, j:j + 1],
                                        ALU.subtract, ALU.mult).then_inc(normed, 1)
                    for j in range(GT):
                        t = nc.vector.value_load(type_i[0:1, ds(it * GT + j, 1)], min_val=0, max_val=TY - 1)
                        for n, (before, after) in enumerate(((normed, scaled), (scaled, final))):
                            dve.wait_ge(before, it * GT + j + 1)
                            V.tensor_tensor(y[:, j, :], y[:, j, :],
                                            rows[:, n, ds(t, 1), :].rearrange("p a n -> p (a n)"),
                                            (ALU.mult, ALU.add)[n]).then_inc(after, 1)

        with Phase(nc, "tout_x") as px:
            got = px.gather_sems(GT)
            moved = px.sem("moved")
            back = px.sb("back", [P, GT, D])
            block = px.block()

            @block.gpsimd
            def _(pool):
                for i in range(NT):
                    if i >= GT:
                        pool.wait_ge(moved, i - GT + 1)
                    pool.indirect_dma_start(
                        out=back[:, i % GT, :], out_offset=None, in_=as_,
                        in_offset=bass.IndirectOffsetOnAxis(ap=pos_i[:, i:i + 1].bitcast(U32), axis=0)
                    ).then_inc(got[i % GT], 16)

            @block.vector
            def _(dve):
                for i in range(NT):
                    dve.wait_ge(got[i % GT], 16 * (i // GT) + 16)
                    nc.vector.tensor_tensor(X[:, i, :], X[:, i, :], back[:, i % GT, :], ALU.add).then_inc(moved, 1)


def store_nodes(nc, X, out):
    with Phase(nc, "store") as ph:
        stored = ph.sem("stored")
        block = ph.block()
        whole = N // P
        rest = N - whole * P

        @block.sync
        def _(sp):
            sp.dma_start(out[0:whole * P].rearrange("(t p) d -> p t d", p=P), X[:, 0:whole, :]).then_inc(stored, 16)
            sp.dma_start(out[whole * P:N], X[0:rest, whole, :]).then_inc(stored, 16)
            sp.wait_ge(stored, 32)


def gnn_ffn_kernel(nc, io, out):
    def table(name, *shape):
        return nc.dram_tensor(name, shape, F32, kind="Internal").ap()

    with ExitStack() as whole:
        def sb(name, shape, dt=F32, stack=whole):
            return stack.enter_context(nc.sbuf_tensor(name, shape, dt))

        c = dict(ident=sb("ident", [P, P]), ones=sb("ones", [P, P]), before_col=sb("before_col", [P, P]),
                 before_row=sb("before_row", [P, P]), iota=sb("iota", [P, ST]), iota_p=sb("iota_p", [P, 1]),
                 eps=sb("eps", [P, 1]), ident_h=sb("ident_h", [P, P], BF16),
                 mean=sb("mean", [P, NT]), rstd=sb("rstd", [P, NT]),
                 block_f=[sb(f"block_f{k}", [P, ST]) for k in range(2)],
                 block_i=[sb(f"block_i{k}", [P, ST], I32) for k in range(2)])
        X = sb("X", [P, NT, D])
        degree, inv_degree, chosen = sb("degree", [P, NT]), sb("inv_degree", [P, NT]), sb("chosen", [P, NT])
        slots = [table(f"slots{k}", P * ST, PW) for k in range(2)]
        lo_rows = [table(f"lo_rows{k}", P * ST) for k in range(2)]
        key_rows = [table(f"key_rows{k}", P * ST) for k in range(2)]
        v_stream = table("v_stream", P, ST, D)
        node_table = table("node_table", NP, D)

        make_constants(nc, c)
        with ExitStack() as part:
            starts = [sb(f"starts{k}", [NT, P], stack=part) for k in range(2)]
            sort_edges(nc, c, io, X, slots, degree, starts)
        turn_slot_rows(nc, c, slots, lo_rows, key_rows)

        layernorm_stats(nc, c, "norm0", X)
        with ExitStack() as part:
            agg = sb("agg0", [P, NT, D + 8], stack=part)
            Q, scores = sb("Q", [P, NT, D], stack=part), sb("scores0", [P, ST * 8], stack=part)
            kv_table = table("kv_table", NP, 2 * D)
            attention_inputs(nc, c, io, X, Q, kv_table)
            attention_scores(nc, c, slots[0], lo_rows[0], Q, kv_table, v_stream, scores, c["block_i"][0])
            segment_softmax(nc, c, "soft0", 8, 32 ** -0.5, key_rows[0], scores)
            attention_values(nc, c, "values0", slots[0], v_stream, scores, c["block_i"][0], agg, 8, D)
            attention_output(nc, c, io, X, agg)
        expert_layers(nc, c, io, X)

        layernorm_stats(nc, c, "norm2", X)
        store_normalised(nc, c, "xn", X, node_table)
        sage_table = table("sage_table", NP, D)
        with ExitStack() as part:
            agg = sb("agg1", [P, NT, D], stack=part)
            aggregate(nc, c, "mean1", slots[0], node_table, c["block_i"][0], agg, False)
            sage_layers(nc, c, io, X, agg, degree, inv_degree, sage_table)
            aggregate(nc, c, "mean2", slots[0], sage_table, c["block_i"][0], agg, False)
            layernorm_stats(nc, c, "norm3", X, add_scaled(nc, X, agg, inv_degree))
        choose_tokens(nc, c, io, X, table("router_row", NP), chosen)
        chosen_ffn(nc, c, io, X, chosen)

        layernorm_stats(nc, c, "norm4", X)
        with ExitStack() as part:
            pos_i, type_i = sb("pos_i", [P, NT], I32, part), sb("type_i", [P, TT], I32, part)
            sorted_x, sorted_agg = table("sorted_x", TT * P, D), table("sorted_agg", TT * P, D)
            sorted_kvq, vk_table = table("sorted_kvq", TT * P, KVQ), table("vk_table", NP, 2 * PROJ)
            sort_nodes(nc, c, io, X, pos_i, type_i, sorted_x)
            type_projections(nc, c, io, type_i, sorted_x, sorted_kvq)
            both = sb("both", [P, NT, D], stack=part)
            with ExitStack() as inner:
                agg, q_rows = sb("agg2", [P, NT, D + H2], stack=inner), sb("q_rows", [P, NT, DK], stack=inner)
                scores = sb("scores2", [P, ST * H2], stack=inner)
                nodes_back(nc, c, pos_i, sorted_kvq, vk_table, q_rows)
                for k in range(2):
                    timed_scores(nc, c, io, f"timed{k}", slots[k], lo_rows[k], q_rows, vk_table, v_stream,
                                 scores, c["block_i"][k])
                    segment_softmax(nc, c, f"soft2{k}", H2, DK ** -0.5, key_rows[k], scores)
                    attention_values(nc, c, f"values2{k}", slots[k], v_stream, scores, c["block_i"][k], agg,
                                     H2, PROJ + TD)
                    fold_direction(nc, f"fold{k}", agg, both, k == 0)
            type_output(nc, c, io, pos_i, type_i, both, sorted_x, sorted_agg, X)
        layernorm_stats(nc, c, "norm5", X)
        mixture_ffn(nc, c, io, X)

        layernorm_stats(nc, c, "norm6", X)
        row_product(nc, c, io, "support", X, "G3w", take_to_dram=node_table)
        with ExitStack() as part:
            agg = sb("agg3", [P, NT, D], stack=part)
            aggregate(nc, c, "weighted", slots[1], node_table, c["block_i"][1], agg, True)
            layernorm_stats(nc, c, "norm7", X, add_relu(nc, X, agg))
        row_product(nc, c, io, "last", X, "F3w", bias="F3b")
        store_nodes(nc, X, out)


def laid_out(i):
    def cols(a):
        return a.reshape(-1, P).T

    def pad(a, rows, value):
        return np.concatenate([a, np.full((rows - len(a),) + a.shape[1:], value, a.dtype)])

    def edge_cols(a):
        return np.swapaxes(a.reshape((ET, P) + a.shape[1:]), 0, 1)

    heads = 8
    qkv_w = i["L0_gnn_W_qkv"].reshape(D, heads, 3, D // heads)
    qkv_b = i["L0_gnn_b_qkv"].reshape(heads, 3, D // heads)
    src, dst = pad(i["src"], EP, NP - 1), pad(i["dst"], EP, NP - 1)
    r = dict(x=pad(i["x"], NP, 0), src_c=edge_cols(src), dst_c=edge_cols(dst), src_r=src, dst_r=dst,
             attr_c=edge_cols(pad(i["edge_attr_5"], EP, 0)), w_c=edge_cols(pad(i["edge_weight"], EP, 0)),
             W0=np.concatenate([i["L0_gnn_W_out"][:D]] + [qkv_w[:, :, k].reshape(D, D) for k in range(3)], 1),
             b0=np.concatenate([i["L0_gnn_b_out"]] + [qkv_b[:, k].reshape(D) for k in range(3)]),
             W0m=i["L0_gnn_W_out"][D:])
    r.update(F0W1=i["L0_ffn_W1"], F0W2=i["L0_ffn_W2"], F0W3=i["L0_ffn_Wo"], F0Wr=i["L0_ffn_Wr"],
             F0br=i["L0_ffn_br"], F0bo=i["L0_ffn_bo"])
    for layer in (1, 2):
        for k in ("b", "g", "be", "m", "v"):
            r[f"F0{k}{layer}"] = cols(i[f"L0_ffn_{k}{layer}"])
    r.update(S1W1=np.concatenate([i["L1_gnn_W1l"].T, i["L1_gnn_W1r"].T]),
             S1W2=np.concatenate([i["L1_gnn_W2l"].T, i["L1_gnn_W2r"].T], 1),
             S1b1=cols(i["L1_gnn_b1"]), S1b2=i["L1_gnn_b2"],
             C1wr=i["L1_ffn_wr"].reshape(-1), C1br=i["L1_ffn_br"], C1W1=i["L1_ffn_w1"], C1W2=i["L1_ffn_w2"],
             C1b1=cols(i["L1_ffn_b1"]), C1b2=i["L1_ffn_b2"])
    m = {k[7:]: v for k, v in i.items() if k.startswith("L2_ffn_")}
    r.update(M2sW1=m["sW1"], M2sW2=m["sW2"], M2sW3=m["sW3"], M2eW1=m["eW1"], M2eW2=m["eW2"], M2eW3=m["eW3"],
             M2b=cols(np.concatenate([m["sb1"], m["sb2"], m["eb1"].reshape(-1)])), M2eb2=m["eb2"].T,
             M2b3=np.concatenate([m["eb3"], m["sb3"][None]]), M2gW=m["gW"], M2gb=m["gb"])
    r.update(T2type=cols(pad(i["node_type_19"], NP, 0)), T2w=i["L2_gnn_w_time"], T2b=i["L2_gnn_b_time"])
    for k in ("Wk", "Wq", "Wv", "bk", "bq", "bv", "Wa", "ba", "gamma", "beta"):
        r["T2" + k] = i["L2_gnn_" + k]
    r.update(G3w=i["L3_gnn_weight"], F3w=i["L3_ffn_weight"].T, F3b=i["L3_ffn_bias"])
    return r


def kernel(**inputs):
    import numpy as _np
    import concourse.bacc as _bacc
    from concourse import mybir as _mybir
    from concourse.bass_utils import run_bass_kernel_spmd as _run

    nc = _bacc.Bacc("TRN2", target_bir_lowering=False, num_devices=1)
    arrays, io = {}, {}
    for name, a in laid_out({k: _np.asarray(v) for k, v in inputs.items()}).items():
        a = _np.ascontiguousarray(a)
        arrays[f"in_{name}_dram"] = a
        io[name] = nc.dram_tensor(f"in_{name}_dram", a.shape, _mybir.dt.from_np(a.dtype), kind="ExternalInput").ap()
    out = nc.dram_tensor("out_0_dram", (N, D), F32, kind="ExternalOutput").ap()
    gnn_ffn_kernel(nc, io, out)
    r = _run(nc, [arrays], core_ids=[0])
    return r.results[0]["out_0_dram"]
```
